# Optimizing a Trainium2 kernel written in Bass

```python
import numpy as np
import jax
import jax.numpy as jnp

def _softmax(x, axis=-1):
    return jax.nn.softmax(x, axis=axis)

def _gelu(x):
    return jax.nn.gelu(x, approximate=True)

def _silu(x):
    return jax.nn.silu(x)

def _sigmoid(x):
    return jax.nn.sigmoid(x)

def _layernorm(x, axis=-1, eps=1e-05):
    m = jnp.mean(x, axis=axis, keepdims=True)
    v = jnp.var(x, axis=axis, keepdims=True)
    return (x - m) / jnp.sqrt(v + eps)

def _scatter_add(tgt, idx, src, axis=0):
    return tgt.at[idx].add(src)

def _segment_sum(src, seg, n):
    return jax.ops.segment_sum(src, seg, n)
kernel_name = 'mk_gps_d1_gnn_r32_24977b'

def setup_inputs(seed: int=0):
    np.random.seed(seed)
    _w = jnp.asarray

    def _rec_inputs():
        import jax
        import jax.numpy as jnp
        _gk = jax.random.key(seed)
        x = -0.0003713 + 1 * jax.random.normal(jax.random.fold_in(_gk, 1), (3125, 256), jnp.float32)
        src = jax.random.randint(jax.random.fold_in(_gk, 2), (50000,), 0, 3125, jnp.int32)
        dst = jax.random.randint(jax.random.fold_in(_gk, 3), (50000,), 0, 3125, jnp.int32)
        _o = jnp.argsort(dst, stable=True)
        src = src[_o]
        dst = dst[_o]
        edge_weight1 = jax.random.uniform(jax.random.fold_in(_gk, 12), (50000, 1), jnp.float32, 0.0, 0.999998)
        return (x, src, dst, edge_weight1)
    x, src, dst, edge_weight1 = _rec_inputs()

    def _L0_gnn_setup():
        import jax, jax.numpy as jnp
        import numpy as np
        N_NODES = 50000
        DIM_H = 256
        N_EDGES = 25000
        LN_EPS = 1e-05

        def _layer_norm(x, g, b):
            mu = jnp.mean(x, axis=-1, keepdims=True)
            var = jnp.mean(jnp.square(x - mu), axis=-1, keepdims=True)
            return (x - mu) * jax.lax.rsqrt(var + LN_EPS) * g + b
        key = jax.random.key(seed)
        ks = jax.random.split(key, 12)
        d = DIM_H

        def lin(k, fan_in, fan_out):
            lim = 1.0 / np.sqrt(fan_in)
            kw, kb = jax.random.split(k)
            W = jax.random.uniform(kw, (fan_in, fan_out), jnp.float32, -lim, lim)
            b = jax.random.uniform(kb, (fan_out,), jnp.float32, -lim, lim)
            return (W, b)
        h = jax.random.normal(ks[0], (N_NODES, d), jnp.float32)
        e = jax.random.randint(ks[1], (2, N_EDGES), 0, N_NODES, jnp.int64)
        d2 = jax.random.uniform(ks[2], (N_EDGES, 1), jnp.float32)
        mW1, mb1 = lin(ks[3], 2 * d + 1, d)
        mW2, mb2 = lin(ks[4], d, d)
        ln_g = jnp.ones((d,), jnp.float32)
        ln_b = jnp.zeros((d,), jnp.float32)
        uW1, ub1 = lin(ks[5], 2 * d, d)
        uW2, ub2 = lin(ks[6], d, d)
        return {'h': h, 'e': e, 'd2': d2, 'mW1': mW1, 'mb1': mb1, 'ln_g': ln_g, 'ln_b': ln_b, 'mW2': mW2, 'mb2': mb2, 'uW1': uW1, 'ub1': ub1, 'uW2': uW2, 'ub2': ub2}
    _L0_gnn_all = _L0_gnn_setup()
    _L0_gnn_in = {k: v for k, v in _L0_gnn_all.items() if k in ('mW1', 'mb1', 'ln_g', 'ln_b', 'mW2', 'mb2', 'uW1', 'ub1', 'uW2', 'ub2')}
    del _L0_gnn_all

    def _L0_mix_setup():
        import jax, jax.numpy as jnp
        import numpy as np
        HEADS = 8
        DIM_HEAD = 64
        EPS = 1e-05

        def _inst_norm_lastdim(t):
            mu = jnp.mean(t, axis=-1, keepdims=True)
            var = jnp.mean(jnp.square(t - mu), axis=-1, keepdims=True)
            return (t - mu) * jax.lax.rsqrt(var + EPS)
        key = jax.random.key(seed)
        k1, k2, k3, k4 = jax.random.split(key, 4)
        b, n, dim = (4, 256, 256)
        inner = HEADS * DIM_HEAD
        x = jax.random.normal(k1, (b, n, dim), dtype=jnp.float32)
        Wqkv = jax.random.normal(k2, (3 * inner, dim), dtype=jnp.float32) * (1.0 / np.sqrt(dim))
        Wout = jax.random.normal(k3, (dim, inner), dtype=jnp.float32) * (1.0 / np.sqrt(inner))
        bout = jax.random.normal(k4, (dim,), dtype=jnp.float32) * 0.01
        return {'x': x, 'Wqkv': Wqkv, 'Wout': Wout, 'bout': bout}
    _L0_mix_all = _L0_mix_setup()
    _L0_mix_in = {k: v for k, v in _L0_mix_all.items() if k in ('Wqkv', 'Wout', 'bout')}
    del _L0_mix_all

    def _L0_ffn_setup():
        import jax, jax.numpy as jnp
        import numpy as np
        E = 8
        K = 2
        D = 256
        H = 512
        DOUT = 256
        EPS = 1e-05
        key = jax.random.key(seed)
        ks = jax.random.split(key, 9)
        s = 0.02
        return {'x': jax.random.normal(ks[0], (4, 256, D), jnp.float32), 'gamma': 1.0 + 0.05 * jax.random.normal(ks[1], (D,), jnp.float32), 'beta': 0.05 * jax.random.normal(ks[2], (D,), jnp.float32), 'Wr': 0.01 * jax.random.normal(ks[3], (D, E), jnp.float32), 'br': jnp.zeros((E,), jnp.float32), 'W1': s * jax.random.normal(ks[4], (E, D, H), jnp.float32), 'b1': s * jax.random.normal(ks[5], (E, H), jnp.float32), 'W2': s * jax.random.normal(ks[6], (E, H, DOUT), jnp.float32), 'b2': s * jax.random.normal(ks[7], (E, DOUT), jnp.float32)}
    _L0_ffn_all = _L0_ffn_setup()
    _L0_ffn_in = {k: v for k, v in _L0_ffn_all.items() if k in ('gamma', 'beta', 'Wr', 'br', 'W1', 'b1', 'W2', 'b2')}
    del _L0_ffn_all
    return {'x': x, 'src': src, 'dst': dst, 'edge_weight1': edge_weight1, 'L0_gnn_mW1': _L0_gnn_in['mW1'], 'L0_gnn_mb1': _L0_gnn_in['mb1'], 'L0_gnn_ln_g': _L0_gnn_in['ln_g'], 'L0_gnn_ln_b': _L0_gnn_in['ln_b'], 'L0_gnn_mW2': _L0_gnn_in['mW2'], 'L0_gnn_mb2': _L0_gnn_in['mb2'], 'L0_gnn_uW1': _L0_gnn_in['uW1'], 'L0_gnn_ub1': _L0_gnn_in['ub1'], 'L0_gnn_uW2': _L0_gnn_in['uW2'], 'L0_gnn_ub2': _L0_gnn_in['ub2'], 'L0_mix_Wqkv': _L0_mix_in['Wqkv'], 'L0_mix_Wout': _L0_mix_in['Wout'], 'L0_mix_bout': _L0_mix_in['bout'], 'L0_ffn_gamma': _L0_ffn_in['gamma'], 'L0_ffn_beta': _L0_ffn_in['beta'], 'L0_ffn_Wr': _L0_ffn_in['Wr'], 'L0_ffn_br': _L0_ffn_in['br'], 'L0_ffn_W1': _L0_ffn_in['W1'], 'L0_ffn_b1': _L0_ffn_in['b1'], 'L0_ffn_W2': _L0_ffn_in['W2'], 'L0_ffn_b2': _L0_ffn_in['b2']}

def reference(x, src, dst, edge_weight1, L0_gnn_mW1, L0_gnn_mb1, L0_gnn_ln_g, L0_gnn_ln_b, L0_gnn_mW2, L0_gnn_mb2, L0_gnn_uW1, L0_gnn_ub1, L0_gnn_uW2, L0_gnn_ub2, L0_mix_Wqkv, L0_mix_Wout, L0_mix_bout, L0_ffn_gamma, L0_ffn_beta, L0_ffn_Wr, L0_ffn_br, L0_ffn_W1, L0_ffn_b1, L0_ffn_W2, L0_ffn_b2):
    import jax
    import jax.numpy as jnp

    def _L0_gnn_ref(h, e, d2, mW1, mb1, ln_g, ln_b, mW2, mb2, uW1, ub1, uW2, ub2):
        import jax, jax.numpy as jnp
        import numpy as np
        N_NODES = 50000
        DIM_H = 256
        N_EDGES = 25000
        LN_EPS = 1e-05

        def _layer_norm(x, g, b):
            mu = jnp.mean(x, axis=-1, keepdims=True)
            var = jnp.mean(jnp.square(x - mu), axis=-1, keepdims=True)
            return (x - mu) * jax.lax.rsqrt(var + LN_EPS) * g + b
        ei, ej = (e[0], e[1])
        hi = h[ei]
        hj = h[ej]
        x = jnp.concatenate((hi, hj, d2), axis=-1)
        msg = jax.nn.silu(x @ mW1 + mb1)
        msg = _layer_norm(msg, ln_g, ln_b)
        msg = jax.nn.silu(msg @ mW2 + mb2)
        agg = jax.ops.segment_sum(msg, ei, num_segments=h.shape[0])
        y = jnp.concatenate((h, agg), axis=-1)
        y = jax.nn.silu(y @ uW1 + ub1) @ uW2 + ub2
        return h + y

    def _L0_mix_ref(x, Wqkv, Wout, bout):
        import jax, jax.numpy as jnp
        import numpy as np
        HEADS = 8
        DIM_HEAD = 64
        EPS = 1e-05

        def _inst_norm_lastdim(t):
            mu = jnp.mean(t, axis=-1, keepdims=True)
            var = jnp.mean(jnp.square(t - mu), axis=-1, keepdims=True)
            return (t - mu) * jax.lax.rsqrt(var + EPS)
        b, n, dim = x.shape
        qkv = jnp.einsum('bnc,fc->bnf', x, Wqkv)
        q, k, v = jnp.split(qkv, 3, axis=-1)

        def to_heads(t):
            return t.reshape(b, n, HEADS, DIM_HEAD).transpose(0, 2, 1, 3)
        q, k, v = (to_heads(q), to_heads(k), to_heads(v))
        k = _inst_norm_lastdim(k)
        v = _inst_norm_lastdim(v)
        dots = jnp.einsum('bhnd,bhne->bhde', k, v)
        out = jnp.einsum('bhnd,bhde->bhne', q, dots) / n
        out = out.transpose(0, 2, 1, 3).reshape(b, n, HEADS * DIM_HEAD)
        return jnp.einsum('bnf,cf->bnc', out, Wout) + bout

    def _L0_ffn_ref(x, gamma, beta, Wr, br, W1, b1, W2, b2):
        import jax, jax.numpy as jnp
        import numpy as np
        E = 8
        K = 2
        D = 256
        H = 512
        DOUT = 256
        EPS = 1e-05
        mu = jnp.mean(x, axis=-1, keepdims=True)
        var = jnp.mean(jnp.square(x - mu), axis=-1, keepdims=True)
        xn = (x - mu) * jax.lax.rsqrt(var + EPS) * gamma + beta
        logits = jnp.einsum('bsd,de->bse', xn, Wr) + br
        top_vals, top_idx = jax.lax.top_k(logits, K)
        w = jax.nn.softmax(top_vals, axis=-1)
        w_full = jnp.einsum('bsk,bske->bse', w, jax.nn.one_hot(top_idx, E, dtype=w.dtype))
        y = jnp.zeros(x.shape[:-1] + (DOUT,), x.dtype)
        for e in range(E):
            h = jax.nn.gelu(jnp.einsum('bsd,dh->bsh', xn, W1[e]) + b1[e], approximate=False)
            y_e = jnp.einsum('bsh,hd->bsd', h, W2[e]) + b2[e]
            y = y + y_e * w_full[..., e, None]
        return y
    edge_index = jnp.stack([src, dst])
    xn = _layernorm(x, axis=-1)
    x = x + _L0_gnn_ref(xn, edge_index, edge_weight1, L0_gnn_mW1, L0_gnn_mb1, L0_gnn_ln_g, L0_gnn_ln_b, L0_gnn_mW2, L0_gnn_mb2, L0_gnn_uW1, L0_gnn_ub1, L0_gnn_uW2, L0_gnn_ub2) + _L0_mix_ref(xn[None], L0_mix_Wqkv, L0_mix_Wout, L0_mix_bout)[0]
    x = x + _L0_ffn_ref(_layernorm(x, axis=-1)[None], L0_ffn_gamma, L0_ffn_beta, L0_ffn_Wr, L0_ffn_br, L0_ffn_W1, L0_ffn_b1, L0_ffn_W2, L0_ffn_b2)[0]
    return x

_drawn_inputs = setup_inputs


def setup_inputs(seed=0):
    import zlib

    import numpy as np

    out = dict(_drawn_inputs(seed))
    spreads = {'L0_gnn_ln_g': (1.0, 0.2), 'L0_gnn_ln_b': (0.0, 0.1), 'L0_ffn_br': (0.0, 0.323)}
    factors = {'edge_weight1': 30.748,
     'L0_gnn_mb1': 3.373,
     'L0_gnn_ub1': 8.0,
     'L0_gnn_ub2': 3.391,
     'L0_mix_bout': 8.0,
     'L0_ffn_gamma': 8.0,
     'L0_ffn_beta': 8.0,
     'L0_ffn_Wr': 3.2,
     'L0_ffn_b1': 22.894,
     'L0_ffn_b2': 8.0}
    for name, (base, spread) in spreads.items():
        noise = np.random.default_rng([zlib.crc32(name.encode()), seed]).standard_normal(out[name].shape)
        drawn = base * np.exp(spread * noise) if base else spread * noise
        out[name] = jnp.asarray(drawn.astype(out[name].dtype))
    for name, factor in factors.items():
        out[name] = (out[name] * factor).astype(out[name].dtype)
    return out
```

```python
import concourse.bass as bass
from concourse import mybir
from contextlib import ExitStack

F32 = mybir.dt.float32
F32R = mybir.dt.float32r
F16 = mybir.dt.float16
I32 = mybir.dt.int32
U32 = mybir.dt.uint32
U16 = mybir.dt.uint16
ALU = mybir.AluOpType
ACT = mybir.ActivationFunctionType
AX = mybir.AxisListType

EPS = 1e-5
ROUND = 12582912.0
RSQRT_MAGIC = 1597463007


class Steps:

    def __init__(self, engine, semaphore):
        self.engine, self.semaphore, self.count, self.turns = engine, semaphore, 0, None

    def did(self, instruction):
        instruction.then_inc(self.semaphore, 1)
        self.count += 1

    def join(self):
        self.engine.wait_ge(self.semaphore, self.count if self.turns is None else self.turns + self.count)

    def enter(self, index, first, per_turn):
        self.turns, self.start, self.per_turn = (index - first) * per_turn, self.count, per_turn

    def leave(self, trips):
        assert self.count - self.start == self.per_turn, (self.count, self.start)
        self.turns, self.count = None, self.start + self.per_turn * trips


def gps_layer(nc, x, src, dst, edge_weight1, mW1, mb1, ln_g, ln_b, mW2, mb2, uW1, ub1, uW2, ub2,
              Wqkv, Wout, bout, gamma, beta, Wr, br, W1, b1, W2, b2, out):
    N, D = x.shape
    E = src.shape[0]
    NP = 125
    NB = N // NP
    EC = E // NP
    KD = D // 128
    G = 2
    UE = 128 * G
    TURN = 6
    UNITS = -(-((E + NB * (UE - 1)) // UE) // TURN) * TURN
    TILES = UNITS * G
    HD = 64
    NQ = Wqkv.shape[0] // 3
    HEADS = NQ // HD
    QC = NQ // 128
    NE, _, HID = W1.shape
    HC = HID // 128
    TOPK = 2
    SLOT_TILES = (TOPK * N + NE * 127) // 128
    KT = TOPK * NB
    assert NP * NB == N and NP * EC == E and SLOT_TILES % 2 == 0 and D == 256

    dst_table = nc.dram_tensor("dst_table", [N, D], F32).ap()
    sorted_edges = nc.dram_tensor("sorted_edges", [128 * TILES, 4], F32).ap()
    expert_in = nc.dram_tensor("expert_in", [SLOT_TILES * 128, D], F32).ap()
    expert_out = nc.dram_tensor("expert_out", [SLOT_TILES * 128, D], F32).ap()

    ctx = ExitStack()
    with ctx:
        def sem(name):
            return ctx.enter_context(nc.semaphore(name))

        base = (nc.sbuf_base + 31) // 32 * 32
        place, size_of, filled, cursor = {}, {}, {}, [base]

        def region(name, size):
            place[name], size_of[name], filled[name] = cursor[0], size, 0
            cursor[0] += (size + 31) // 32 * 32

        def at(name, shape, dt, owner, byte=0):
            return nc.alloc_sbuf_tensor_at(name, shape, dt, offset=place[owner] + byte)

        def nbytes(shape, dt):
            n = {F16: 2, U16: 2}.get(dt, 4)
            for k in shape[1:]:
                n *= k
            return (n + 31) // 32 * 32

        def inside(name, shape, dt, owner):
            t = at(name, shape, dt, owner, filled[owner])
            filled[owner] += nbytes(shape, dt)
            assert filled[owner] <= size_of[owner], (owner, name, filled[owner])
            return t

        NODE = NB * D * 4
        region("res", NODE)
        region("blocks", NODE)
        assert KD * 128 == D
        region("turned", NODE)
        region("src_hi", NODE)
        region("src_lo", NODE)
        region("edges", TILES * 16 + 512)
        region("work", 34 * 1024)
        region("weights", 32 * 1024)
        region("small", 9600)
        ctx.enter_context(nc.sbuf_tensor("arena", [128, (cursor[0] - base) // 4], F32))

        res = at("res_t", [128, NB, D], F32, "res")
        xn = at("xn_t", [128, NB, D], F32, "blocks")
        agg = at("agg_t", [128, NB, D], F32, "blocks")
        xnT = at("xnT_t", [128, NB, KD, 128], F32, "turned")
        src_hi = at("src_hi_t", [128, NB, D], F32R, "src_hi")
        src_lo = at("src_lo_t", [128, NB, D], F32R, "src_lo")
        recs = at("recs_t", [128, TILES, 4], F32, "edges")
        rec_sb = at("rec_sb_t", [128, EC, 4], F32, "edges")

        onehot = at("onehot_t", [128, NB, EC], F16, "turned")
        masked = at("masked_t", [128, NB, EC], U16, "turned")
        scanned = at("scanned_t", [128, NB * EC], F16, "work")
        src_i = at("src_i_t", [128, EC], I32, "blocks")
        dst_i = at("dst_i_t", [128, EC], I32, "blocks", 2048)
        blk_f = at("blk_f_t", [128, EC], F32, "blocks", 4096)
        row_f = at("row_f_t", [128, EC], F32, "blocks", 6144)
        rank_f = at("rank_f_t", [128, EC], F32, "blocks", 8192)
        low_i = at("low_i_t", [128, EC], I32, "blocks", 12288)
        top_i = at("top_i_t", [128, EC], I32, "blocks", 14336)
        d2_r = at("d2_r_t", [128, EC], F32R, "blocks", 16384)
        d2_f = at("d2_f_t", [128, EC], F32, "blocks", 18432)
        unit_le = at("unit_le_t", [1, UNITS, NB], F16, "work")
        defaults = at("defaults_t", [128, TILES // 12, 4], F32, "blocks", 20480)
        bias_bc = at("bias_bc_t", [128, D], F32, "work", 32768)
        bout_bc = at("bout_bc_t", [128, D], F32, "work", 33792)
        unit_f = at("unit_f_t", [1, UNITS], F32, "work", 16384)

        wkv_nat = at("wkv_nat_t", [128, 2 * QC, D], F32, "work", 20480)
        wout_nat = at("wout_nat_t", [128, KD, NQ], F32, "work", 28672)
        dst_stage = [at(f"dst_stage{i}", [128, D], F32, "work", 1024 * i) for i in range(2)]
        kv_sq = at("kv_sq_t", [128, 2 * NQ], F32, "work", 2048)
        k_n = [at(f"k_n{i}", [128, NQ], F32, "work", 6144 + 2048 * i) for i in range(2)]
        v_n = [at(f"v_n{i}", [128, NQ], F32, "work", 10240 + 2048 * i) for i in range(2)]
        zero_rows = at("zero_rows_t", [128, 2048], F32, "src_lo")

        dst_row = at("dst_row_t", [128, TURN, G, D], F32, "work")
        msg1 = at("msg1_t", [128, 3, G, D], F32, "work", 12288)
        hotT = at("hotT_t", [128, 2, UE], F32R, "work", 18432)
        msg1n = at("msg1n_t", [128, 2, G, D], F32, "work", 20480)
        msg1T = at("msg1T_t", [128, 2, KD, UE], F32, "work", 24576)
        msg2 = at("msg2_t", [128, 2, G, D], F32, "work", 28672)

        aggT = [at(f"aggT{i}", [128, KD, 4, NP], F32, "work", 4096 * i) for i in range(2)]
        hidT = [at(f"hidT{i}", [128, KD, 4, NP], F32, "work", 8192 + 4096 * i) for i in range(2)]
        xm = at("xm_t", [128, NB, D], F32, "work")
        xmT = [at(f"xmT{i}", [128, KD, NP], F32, "work", NODE + 1024 * i) for i in range(2)]
        w1_sb = at("w1_sb_t", [128, NE, KD, HID], F32, "src_hi")
        b1_bc = at("b1_bc_t", [128, NE, HID], F32, "src_hi", 32768)
        w2_sb = at("w2_sb_t", [128, NE, HC, D], F32, "blocks")
        b2_bc = at("b2_bc_t", [128, NE, D], F32, "blocks", 32768)
        slot_x = [at(f"slot_x{i}", [128, D], F32, "work", 1024 * i) for i in range(4)]
        slot_xT = [at(f"slot_xT{i}", [128, KD, 128], F32, "work", 4096 + 1024 * i) for i in range(2)]
        slot_h = [at(f"slot_h{i}", [128, HID], F32, "work", 6144 + 2048 * i) for i in range(2)]
        slot_hT = [at(f"slot_hT{i}", [128, HC, 128], F32, "work", 10240 + 2048 * i) for i in range(2)]
        slot_y = [at(f"slot_y{i}", [128, D], F32, "work", 14336 + 1024 * i) for i in range(2)]
        pick = [at(f"pick{i}", [128, TOPK, D], F32, "work", 16384 + 2048 * i) for i in range(4)]

        w = lambda n, s, t=F32: inside(n, s, t, "weights")
        mw1_sb = w("mw1_sb", [128, KD, 2, D])
        w2c_raw = w("w2c_raw", [128, KD, D])
        w2c = w("w2c", [128, KD, D])
        hot = at("hot_t", [128, TURN, G, 128], F32, "weights", filled["weights"])
        wkvT = w("wkvT", [128, KD, 2 * NQ])
        wq_nat = w("wq_nat", [128, QC, D])
        woutT = w("woutT", [128, QC, D])
        mixP = w("mixP", [128, QC, D])
        uw1_sb = at("uw1_sb", [128, 2 * KD, D], F32, "weights", filled["weights"] - 4 * QC * D)
        mixP_byte = filled["weights"] - 4 * QC * D
        b2tmp = at("b2tmp", [1, D], F32, "weights", mixP_byte)
        b2lo = at("b2lo", [1, D], F32, "weights", mixP_byte + 1024)
        b2pair = at("b2pair", [2, D], F32, "work", 17408)
        mb2_row = at("mb2_row", [1, D], F32, "weights", mixP_byte + 2048)
        ones2f = at("ones2f", [2, 128], F32, "weights", mixP_byte + 3072)
        pos_i = at("pos_i_t", [128, EC], I32, "weights", filled["weights"])
        mixG = w("mixG", [128, KD, D])
        uw2_sb = w("uw2_sb", [128, KD, D])
        place["late"], size_of["late"], filled["late"] = place["weights"], 4096, 0
        s = lambda n, sh, t=F32: inside(n, sh, t, "small")
        ident = s("ident", [128, 128])
        iota = s("iota", [128, 256])
        earlier = s("earlier", [128, 128])
        ones = s("ones", [128, 128])
        bw = s("bw", [2, D])
        bw_sel = s("bw_sel", [2, 128])
        b2row = s("b2row", [2, D], F32R)
        ones2 = s("ones2", [2, 128], F32R)
        g_col = s("g_col", [128, KD])
        b_col = s("b_col", [128, KD])
        ub1_col = s("ub1_col", [128, KD])
        gamma_col = s("gamma_col", [128, KD])
        beta_col = s("beta_col", [128, KD])
        wr_sb = s("wr_sb", [128, KD, NE])
        br_bc = s("br_bc", [128, NE])
        eps_col = s("eps_col", [128, 1])
        stats = s("stats", [128, NB, 6])
        meanvar = s("meanvar", [128, NB, 2])
        rstd = s("rstd", [128, NB])
        rowcnt = s("rowcnt", [128, NB])
        cum = s("cum", [128, NB])
        ints = s("ints", [128, NB], I32)
        prefix = s("prefix", [128, NB])
        nunits = s("nunits", [128, NB])
        ends = s("ends", [128, NB])
        unit_blk = s("unit_blk", [1, UNITS], I32)
        kv_ss = s("kv_ss", [128, 2 * HEADS])
        kv_rs = s("kv_rs", [128, HEADS])
        wmean = s("wmean", [128, KD * 2 * HEADS])
        scat_idx = s("scat_idx", [128, 2, 8], I32)
        stage_idx = s("stage_idx", [128, G * TURN], I32)
        stage_row = s("stage_row", [128, G * TURN])
        fence = s("fence", [1, TURN])
        est = s("est", [128, TURN, G, 6])
        emv = s("emv", [128, TURN, G, 2])
        nw_v = s("nw_v", [128, 2, G])
        nw_y = s("nw_y", [128, TURN, G])
        nw_t = s("nw_t", [128, 2, G])
        nw_i = s("nw_i", [128, 2, G], I32)
        hot_k = at("hot_k", [128, NE, KT], F32, "edges")
        hot_c = at("hot_c", [128, NE, KT], F32, "edges", 1600)
        hot_p = at("hot_p", [128, NE, KT], F32, "edges", 3200)
        logits = at("logits", [128, NB, NE], F32, "edges", 4800)
        top_v = at("top_v", [128, NB, NE], F32, "edges", 5600)
        top_e = at("top_e", [128, NB, 8], U32, "edges", 6400)
        top_f = inside("top_f", [128, TOPK, NB], F32, "late")
        slot_i = inside("slot_i", [128, TOPK, NB], I32, "late")
        slot_f = inside("slot_f", [128, TOPK, NB], F32, "late")
        wgt = inside("wgt", [128, TOPK, NB], F32, "late")
        wtmp = inside("wtmp", [128, NB], F32, "late")
        rst2 = inside("rst2", [128, NB], F32, "late")
        e_cum = inside("e_cum", [128, NE], F32, "late")
        e_cnt = inside("e_cnt", [128, NE], F32, "late")
        e_int = inside("e_int", [128, NE], I32, "late")
        e_til = inside("e_til", [128, NE], F32, "late")
        e_end = inside("e_end", [128, NE], F32, "late")
        e_le = at("e_le", [1, SLOT_TILES, NE], F32, "edges", 0)
        tile_f = inside("tile_f", [1, SLOT_TILES], F32, "late")
        tile_e = inside("tile_e", [1, SLOT_TILES], I32, "late")
        scat_rec = at("scat_rec", [128, 2, 8, 4], F32, "work", 18432)
        ps = ctx.enter_context(nc.psum_tensor("ps", [128, 8, 512], F32))

        def bank(b, n=512, rows=128, first=0):
            return ps[0:rows, b, first:first + n]

        edges_in, x_in, mw1_in, bw_in = sem("edges_in"), sem("x_in"), sem("mw1_in"), sem("bw_in")
        wmix_in, small_in, upd_w_in, uw1_in = sem("wmix_in"), sem("small_in"), sem("upd_w_in"), sem("uw1_in")
        defaults_out, zeros_out, recs_in, b2row_in = sem("defaults_out"), sem("zeros_out"), sem("recs_in"), sem("b2row_in")
        consts, fills, ident_ok = sem("consts"), sem("fills"), sem("ident_ok")
        dve_step, act_step, pool_step = sem("dve_step"), sem("act_step"), sem("pool_step")
        wT_ps, wT_sb = sem("wT_ps"), sem("wT_sb")
        b2_ps, b2_hl, b2row_ok, ones2_ok, w2c_ok = sem("b2_ps"), sem("b2_hl"), sem("b2row_ok"), sem("ones2_ok"), sem("w2c_ok")
        rowcnt_ok, counts_ps, pos_ok, units_ok = sem("rowcnt_ok"), sem("counts_ps"), sem("pos_ok"), sem("units_ok")
        scattered = [sem(f"scattered{h}") for h in range(2)]
        var_ok, sd_ok, xn_ok, xnT_ps, xnT_sb = sem("var_ok"), sem("sd_ok"), sem("xn_ok"), sem("xnT_ps"), sem("xnT_sb")
        pads_ok, tab_ps, tab_sb, dst_sb = sem("pads_ok"), sem("tab_ps"), sem("tab_sb"), sem("dst_sb")
        dst_out = [sem(f"dst_out{i}") for i in range(2)]
        kv_ps, sq_sb, v_sb, ss_ok, kvsd_ok, kn_ok, dots_ps = (sem(n) for n in (
            "kv_ps", "sq_sb", "v_sb", "ss_ok", "kvsd_ok", "kn_ok", "dots_ps"))
        wkv_centered, diag_ok, mixP_ps, mixP_sb, mixG_ps, mixG_sb = (sem(n) for n in (
            "wkv_centered", "diag_ok", "mixP_ps", "mixP_sb", "mixG_ps", "mixG_sb"))
        row_in = [sem(f"row_in{k}") for k in range(TURN)]
        hot_ready, hotT_ps, hotT_sb, pre_ps, pre_sb, msg1_sb, msg1n_sb = (sem(n) for n in (
            "hot_ready", "hotT_ps", "hotT_sb", "pre_ps", "pre_sb", "msg1_sb", "msg1n_sb"))
        msg1T_ps, msg1T_sb, msg2_ps, msg2_sb, sum_ps, sum_sb = (sem(n) for n in (
            "msg1T_ps", "msg1T_sb", "msg2_ps", "msg2_sb", "sum_ps", "sum_sb"))
        aggT_ps, aggT_sb, hid_ps, hid_sb, upd_ps, x2_ok = (sem(n) for n in (
            "aggT_ps", "aggT_sb", "hid_ps", "hid_sb", "upd_ps", "x2_ok"))
        var1_ok, sd1_ok, var2_ok, sd2_ok, xm_ok, xmT_ps, xmT_sb, logit_ps = (sem(n) for n in (
            "var1_ok", "sd1_ok", "var2_ok", "sd2_ok", "xm_ok", "xmT_ps", "xmT_sb", "logit_ps"))
        gap_ok, exp_ok, hotk_ok, route_ps, slots_ok, tile_ok, sent = (sem(n) for n in (
            "gap_ok", "exp_ok", "hotk_ok", "route_ps", "slots_ok", "tile_ok", "sent"))
        w1_in, w2_in = sem("w1_in"), sem("w2_in")
        slot_in = [sem(f"slot_in{k}") for k in range(4)]
        slot_out = [sem(f"slot_out{k}") for k in range(2)]
        sxT_ps, sxT_sb, sh_ps, sh_pre, sh_sb, shT_ps, shT_sb, sy_ps, sy_sb = (sem(n) for n in (
            "sxT_ps", "sxT_sb", "sh_ps", "sh_pre", "sh_sb", "shT_ps", "shT_sb", "sy_ps", "sy_sb"))
        pick_in = [sem(f"pick_in{k}") for k in range(4)]
        picked, final_ok, stored = sem("picked"), sem("final_ok"), sem("stored")

        N_CONST, N_FILL = 5, 2
        N_DST = [(NB + 1) // 2, NB // 2]
        SMALL = 9
        CH = [list(range(t, min(t + 4, NB))) for t in range(0, NB, 4)]
        LAST = UNITS + 5

        def here(m, count):
            return not isinstance(m, int) or 0 <= m < count

        def steps(engine, body, first, last, trips_lo, trips_hi, turn):
            for n in range(first, turn * trips_lo):
                body(n, n % turn)
            with engine.Fori(trips_lo, trips_hi) as i:
                for k in range(turn):
                    body(turn * i + k, k)
            for n in range(turn * trips_hi, last):
                body(n, n % turn)

        def after(engine, semaphore, count):
            if not isinstance(count, int) or count > 0:
                engine.wait_ge(semaphore, count)

        block = ctx.enter_context(nc.Block())

        @block.sync
        def _(sp):
            sp.dma_start(src_i[0:NP, :], src.rearrange("(p c) -> p c", p=NP)).then_inc(edges_in, 16)
            sp.dma_start(dst_i[0:NP, :], dst.rearrange("(p c) -> p c", p=NP)).then_inc(edges_in, 16)
            sp.dma_start(d2_f[0:NP, :], edge_weight1.rearrange("(p c) a -> p (c a)", p=NP)).then_inc(edges_in, 16)
            sp.dma_start(wkv_nat[:], Wqkv[NQ:3 * NQ, :].rearrange("(q p) c -> p q c", p=128)).then_inc(wmix_in, 16)
            sp.dma_start(wout_nat[:], Wout.rearrange("(o p) f -> p o f", p=128)).then_inc(wmix_in, 16)
            sp.dma_start(wq_nat[:], Wqkv[0:NQ, :].rearrange("(q p) c -> p q c", p=128)).then_inc(wmix_in, 16)
            sp.dma_start(res[0:NP], x.rearrange("(p t) d -> p t d", p=NP)).then_inc(x_in, 16)
            for k in range(KD):
                sp.dma_start(mw1_sb[:, k], mW1[0:2 * D, :].rearrange("(a k p) n -> k p a n", a=2, p=128)[k])\
                  .then_inc(mw1_in, 16)
            sp.dma_start(bw[0:1, :], mb1.rearrange("(a n) -> a n", a=1)).then_inc(bw_in, 16)
            sp.dma_start(bw[1:2, :], mW1[2 * D:2 * D + 1, :]).then_inc(bw_in, 16)
            sp.dma_start(w2c_raw[:], mW2.rearrange("(k p) n -> p k n", p=128)).then_inc(small_in, 16)
            with nc.allow_non_contiguous_dma("vectors of 256 values, one value a partition"):
                for t, v in ((g_col, ln_g), (b_col, ln_b), (ub1_col, ub1), (gamma_col, gamma), (beta_col, beta)):
                    sp.dma_start(t[:], v.rearrange("(k p) -> p k", p=128)).then_inc(small_in, 16)
                sp.dma_start(mb2_row[:], mb2.rearrange("(a n) -> a n", a=1)).then_inc(small_in, 16)
                sp.dma_start(wr_sb[:], Wr.rearrange("(k p) e -> p k e", p=128)).then_inc(small_in, 16)
                sp.dma_start(br_bc[:], br.partition_broadcast(128)).then_inc(small_in, 16)
            sp.dma_start(bias_bc[:], ub2.partition_broadcast(128)).then_inc(upd_w_in, 16)
            sp.dma_start(bout_bc[:], bout.partition_broadcast(128)).then_inc(upd_w_in, 16)
            sp.dma_start(uw2_sb[:], uW2.rearrange("(k p) n -> p k n", p=128)).then_inc(upd_w_in, 16)
            sp.wait_ge(fills, N_FILL)
            reps = 12
            sp.dma_start(sorted_edges.rearrange("(p a b) f -> p a (b f)", p=128, a=reps),
                         defaults[:].rearrange("p b f -> p (b f)").unsqueeze(1)
                         .broadcast_to([128, reps, TILES // 12 * 4])).then_inc(defaults_out, 16)
            reps = SLOT_TILES * D // 2048
            sp.dma_start(expert_in.rearrange("(p s) d -> p (s d)", p=128).rearrange("p (a b) -> p a b", a=reps),
                         zero_rows[:].unsqueeze(1).broadcast_to([128, reps, 2048])).then_inc(zeros_out, 16)
            sp.wait_ge(b2_hl, 1)
            sp.dma_start(b2pair[1:2, :], b2lo[:]).then_inc(b2row_in, 16)
            for t in range(NB):
                sp.wait_ge(dst_sb, t + 1)
                sp.dma_start(dst_table.rearrange("(p t) d -> p t d", p=NP)[:, t, :], dst_stage[t % 2][0:NP, :])\
                  .then_inc(dst_out[t % 2], 16)
            sp.wait_ge(mixG_sb, KD)
            sp.dma_start(uw1_sb[:], uW1.rearrange("(k p) n -> p k n", p=128)).then_inc(uw1_in, 16)
            for h in range(2):
                sp.wait_ge(scattered[h], 16 * EC // 2)
            sp.dma_start(recs[:], sorted_edges.rearrange("(p t) f -> p t f", p=128)).then_inc(recs_in, 16)
            sp.wait_ge(pre_ps, UNITS)
            for e in range(NE):
                sp.dma_start(w1_sb[:, e], W1[e].rearrange("(k p) h -> p k h", p=128)).then_inc(w1_in, 16)
            sp.dma_start(b1_bc[:].rearrange("p e h -> p (e h)"),
                         b1.rearrange("e h -> (e h)").partition_broadcast(128)).then_inc(w1_in, 16)
            sp.wait_ge(x2_ok, NB)
            for e in range(NE):
                sp.dma_start(w2_sb[:, e], W2[e].rearrange("(k p) n -> p k n", p=128)).then_inc(w2_in, 16)
            sp.dma_start(b2_bc[:].rearrange("p e n -> p (e n)"),
                         b2.rearrange("e n -> (e n)").partition_broadcast(128)).then_inc(w2_in, 16)
            sp.wait_ge(sent, 16 * KT)

            def load_slots(m, k):
                if here(m, SLOT_TILES):
                    after(sp, sxT_ps, m - 3)
                    sp.dma_start(slot_x[k % 4][:], expert_in[bass.ts(m, 128), :]).then_inc(slot_in[k % 4], 16)

            def slots_step(n, k):
                load_slots(n + 3, k + 3)
                if here(n, SLOT_TILES):
                    sp.wait_ge(sy_sb, n + 1)
                    sp.dma_start(expert_out[bass.ts(n, 128), :], slot_y[k % 2][:]).then_inc(slot_out[k % 2], 16)

            steps(sp, slots_step, -3, SLOT_TILES, 1, SLOT_TILES // 4 - 1, 4)
            for g in range(5):
                sp.wait_ge(final_ok, 5 * (g + 1))
                sp.dma_start(out.rearrange("(p t) d -> p t d", p=NP)[:, 5 * g:5 * g + 5, :],
                             res[0:NP, 5 * g:5 * g + 5, :]).then_inc(stored, 16)
            sp.wait_ge(stored, 16 * 5)

        @block.gpsimd
        def _(pool):
            st = Steps(pool, pool_step)
            st.did(pool.iota(iota[:], [[1, 256]], channel_multiplier=0, allow_small_or_imprecise_dtypes=True))
            st.did(pool.memset(ident[:], 0.0))
            st.did(pool.memset(ones[:], 1.0))
            st.did(pool.memset(eps_col[:], EPS))
            st.did(pool.memset(defaults[:], 0.0))
            st.join()
            pool.affine_select(out=ident[:], in_=ident[:], compare_op=ALU.not_equal, fill=1.0, base=0,
                               pattern=[[-1, 128]], channel_multiplier=1).then_inc(consts, 1)
            pool.affine_select(out=earlier[:], in_=ones[:], compare_op=ALU.is_gt, fill=0.0, base=0,
                               pattern=[[1, 128]], channel_multiplier=-1).then_inc(consts, 1)
            st.did(pool.affine_select(out=bw_sel[:], in_=ones[0:2, :], compare_op=ALU.is_ge, fill=0.0, base=0,
                                      pattern=[[1, 128]], channel_multiplier=-NP))
            pool.memset(defaults[:, :, 1:2], -1.0).then_inc(fills, 1)
            pool.memset(zero_rows[:], 0.0).then_inc(fills, 1)
            st.join()
            pool.affine_select(out=bw_sel[:], in_=bw_sel[:], compare_op=ALU.is_ge, fill=0.0, base=NP - 1,
                               pattern=[[-1, 128]], channel_multiplier=NP).then_inc(consts, 1)
            pool.memset(ones2f[:], 1.0).then_inc(consts, 1)
            pool.memset(eps_col[:], EPS).then_inc(consts, 1)

            pool.wait_ge(pos_ok, 1)
            pool.wait_ge(defaults_out, 16)
            def carry_wait(k):
                st.did(pool.tensor_tensor(fence[:, k:k + 1], eps_col[0:1, :], eps_col[0:1, :], ALU.add))

            def scatter_group(i):
                for h in range(2):
                    after(pool, scattered[h], i * 128)
                    st.did(pool.tensor_copy(scat_idx[0:NP, h, :], pos_i[0:NP, bass.ds(16 * i + 8 * h, 8)]))
                    st.did(pool.tensor_copy(scat_rec[0:NP, h], rec_sb[0:NP, bass.ds(16 * i + 8 * h, 8), :]))
                    st.join()
                    carry_wait(h)
                    for c in range(8):
                        pool.indirect_dma_start(
                            out=sorted_edges, out_offset=bass.IndirectOffsetOnAxis(scat_idx[0:NP, h, c:c + 1], 0),
                            in_=scat_rec[0:NP, h, c, :], in_offset=None).then_inc(scattered[h], 16)

            scatter_group(0)
            with pool.Fori(1, EC // 16) as i:
                st.enter(i, 1, 6)
                scatter_group(i)
            st.leave(EC // 16 - 1)

            pool.wait_ge(recs_in, 16)
            pool.wait_ge(mixG_sb, KD)
            for i in range(2):
                pool.wait_ge(dst_out[i], 16 * N_DST[i])
            st.did(pool.memset(hot[:], 0.0))
            st.join()

            def edge_group(i):
                for k in range(TURN):
                    after(pool, row_in[k], 32 * i)
                after(pool, hot_ready, 3 * TURN * i)
                st.did(pool.tensor_copy(stage_idx[:], recs[:, bass.ds(G * TURN * i, G * TURN), 0]))
                st.did(pool.tensor_copy(stage_row[:], recs[:, bass.ds(G * TURN * i, G * TURN), 1]))
                st.join()
                for k in range(TURN):
                    after(pool, pre_sb, TURN * (i - 1) + k + 1)
                    carry_wait(k)
                    for j in range(G):
                        pool.indirect_dma_start(
                            out=dst_row[:, k, j, :], out_offset=None, in_=dst_table,
                            in_offset=bass.IndirectOffsetOnAxis(stage_idx[:, 2 * k + j:2 * k + j + 1], 0))\
                            .then_inc(row_in[k], 16)
                    after(pool, sum_ps, TURN * (i - 1) + k + 1)
                    pool.tensor_tensor(hot[:, k, :, NP:NP + 2], recs[:, bass.ds(G * (TURN * i + k), G), 2:4],
                                       ones[:, 0:G * 2].rearrange("p (a b) -> p a b", a=G), ALU.mult)\
                        .then_inc(hot_ready, 1)
                    for j in range(G):
                        pool.tensor_scalar(hot[:, k, j, 0:NP], iota[:, 0:NP], stage_row[:, G * k + j:G * k + j + 1],
                                           None, ALU.is_equal).then_inc(hot_ready, 1)

            edge_group(0)
            with pool.Fori(1, UNITS // TURN) as i:
                st.enter(i, 1, 2 + TURN)
                edge_group(i)
            st.leave(UNITS // TURN - 1)

            pool.wait_ge(slots_ok, 1)
            pool.wait_ge(zeros_out, 16)
            for k in range(TOPK):
                for t in range(NB):
                    pool.indirect_dma_start(
                        out=expert_in, out_offset=bass.IndirectOffsetOnAxis(slot_i[0:NP, k, t:t + 1], 0),
                        in_=xm[0:NP, t, :], in_offset=None).then_inc(sent, 16)
            for i in range(2):
                pool.wait_ge(slot_out[i], 16 * SLOT_TILES // 2)
            for t in range(NB):
                if t >= 4:
                    pool.wait_ge(picked, t - 3)
                for k in range(TOPK):
                    pool.indirect_dma_start(
                        out=pick[t % 4][0:NP, k, :], out_offset=None, in_=expert_out,
                        in_offset=bass.IndirectOffsetOnAxis(slot_i[0:NP, k, t:t + 1], 0))\
                        .then_inc(pick_in[t % 4], 16)

        @block.tensor
        def _(pe):
            def turn(out_, in_, rows):
                return pe.transpose(out_, in_, ident[0:rows, 0:rows])

            pe.wait_ge(consts, N_CONST)
            pe.wait_ge(wmix_in, 48)
            for c in range(KD):
                for q in range(2 * QC):
                    m = turn(bank(4 - 2 * c + q // 4, 128, first=q % 4 * 128), wkv_nat[:, q, c * 128:c * 128 + 128], 128)
                m.then_inc(wT_ps, 1)
            for j in range(QC):
                for o in range(KD):
                    m = turn(bank(j // 2, 128, first=j % 2 * D + o * 128), wout_nat[:, o, j * 128:j * 128 + 128], 128)
            m.then_inc(wT_ps, 1)
            pe.wait_ge(small_in, 16 * SMALL)
            for k in range(KD):
                m = pe.matmul(bank(7, D, rows=1), b_col[:, k:k + 1], w2c_raw[:, k, :], start=(k == 0), stop=(k == KD - 1))
            m.then_inc(b2_ps, 1)
            pe.wait_ge(rowcnt_ok, 1)
            pe.matmul(bank(6, NB), earlier[0:NP, :], rowcnt[0:NP, :], start=True, stop=True)
            pe.matmul(bank(6, NB, first=32), ones[0:NP, :], rowcnt[0:NP, :], start=True, stop=True).then_inc(counts_ps, 1)

            pe.wait_ge(mw1_in, 32)
            pe.wait_ge(bw_in, 32)
            pe.wait_ge(wT_sb, KD + 1)
            pe.wait_ge(pads_ok, 1)

            def turn_xn(t):
                pe.wait_ge(xn_ok, t + 1)
                if t >= 2:
                    pe.wait_ge(xnT_sb, t - 1)
                for k in range(KD):
                    m = turn(bank(t % 2, NP, first=k * NP), xn[0:NP, t, k * 128:k * 128 + 128], NP)
                m.then_inc(xnT_ps, 1)

            def tables(t):
                pe.wait_ge(xnT_sb, t + 1)
                if t >= 2:
                    pe.wait_ge(tab_sb, t - 1)
                    pe.wait_ge(dst_sb, t - 1)
                for a in range(2):
                    o = bank(2 + 2 * a + t % 2, D)
                    for k in range(KD):
                        m = pe.matmul(o, xnT[:, t, k, :], mw1_sb[:, k, a, :], start=(k == 0),
                                      stop=(a == 1 and k == KD - 1))
                    if a == 0:
                        pe.matmul(o, bw_sel[:], bw[:], start=False, stop=True)
                m.then_inc(tab_ps, 1)

            turn_xn(0)
            for t in range(NB):
                if t + 1 < NB:
                    turn_xn(t + 1)
                tables(t)

            pe.wait_ge(wkv_centered, 1)
            pe.wait_ge(units_ok, 1)

            def dots(t):
                pe.wait_ge(kn_ok, t + 1)
                pe.wait_ge(v_sb, t + 1)
                for j in range(QC):
                    m = pe.matmul(bank(6, 128, first=128 * j), v_n[t % 2][0:NP, j * 128:j * 128 + 128],
                                  k_n[t % 2][0:NP, j * 128:j * 128 + 128], start=(t == 0 and j == 0), stop=(t == NB - 1),
                                  skip_group_check=True)
                m.then_inc(dots_ps, 1)

            for t in range(NB):
                b = 2 + 2 * (t % 2)
                if t == 0:
                    pe.wait_ge(tab_sb, NB)
                    pe.wait_ge(dst_sb, NB)
                if t >= 2:
                    pe.wait_ge(kn_ok, t - 1)
                    pe.wait_ge(sq_sb, t - 1)
                    pe.wait_ge(v_sb, t - 1)
                for h in range(2):
                    for k in range(KD):
                        m = pe.matmul(bank(b + h, NQ, rows=NP), xnT[:, t, k, 0:NP], wkvT[:, k, h * NQ:h * NQ + NQ],
                                      start=(k == 0), stop=(k == KD - 1))
                m.then_inc(kv_ps, 1)
                if t >= 1:
                    dots(t - 1)
            dots(NB - 1)
            pe.wait_ge(diag_ok, 1)
            for j in range(QC):
                m = pe.matmul(bank(j // 2, D, first=j % 2 * D), k_n[0][:, j * 128:j * 128 + 128], woutT[:, j, :],
                              start=True, stop=True)
            m.then_inc(mixP_ps, 1)
            pe.wait_ge(mixP_sb, 1)
            for c in range(KD):
                for j in range(QC):
                    m = pe.matmul(bank(2 + c, D), wq_nat[:, j, c * 128:c * 128 + 128], mixP[:, j, :],
                                  start=(j == 0), stop=(j == QC - 1))
                m.then_inc(mixG_ps, 1)

            pe.wait_ge(b2row_ok, 1)
            pe.wait_ge(ones2_ok, 1)
            pe.wait_ge(w2c_ok, 1)
            pe.wait_ge(mixG_sb, KD)
            pe.wait_ge(units_ok, 1)
            blocks_of = {}

            def edge_step(n, k):
                if here(n, UNITS):
                    blk = pe.value_load(unit_blk[0:1, bass.ts(n, 1)], min_val=0, max_val=NB - 1)
                    after(pe, hotT_sb, n + 1)
                    after(pe, pre_sb, n - 1)
                    for j in range(G):
                        for first, table in ((True, src_hi), (False, src_lo)):
                            m = pe.matmul(bank(1 + k % 2, D, first=j * D), hotT[:, k % 2, j * 128:j * 128 + 128],
                                          table[:, bass.ts(blk, 1), :].rearrange("p a n -> p (a n)"),
                                          start=first, stop=not first)
                    m.then_inc(pre_ps, 1)
                m_ = n + 1
                if here(m_, UNITS):
                    pe.wait_ge(hot_ready, 3 * m_ + 3)
                    after(pe, hotT_sb, m_)
                    for j in range(G):
                        m = turn(bank(0, 128, first=j * 128), hot[:, (k + 1) % TURN, j, :], 128)
                    m.then_inc(hotT_ps, 1)
                m_ = n - 3
                if here(m_, UNITS):
                    pe.wait_ge(msg1n_sb, m_ + 1)
                    after(pe, msg1T_sb, m_ - 1)
                    for c in range(KD):
                        for j in range(G):
                            m = turn(bank(3 + (k + 1) % 2, 128, first=c * UE + j * 128),
                                     msg1n[:, (k + 1) % 2, j, c * 128:c * 128 + 128], 128)
                    m.then_inc(msg1T_ps, 1)
                m_ = n - 4
                if here(m_, UNITS):
                    pe.wait_ge(msg2_sb, m_ + 1)
                    after(pe, sum_sb, m_)
                    for j in range(G):
                        m = pe.matmul(bank(7, D, rows=NP), hot[:, (k - 4) % TURN, j, 0:NP], msg2[:, k % 2, j, :],
                                      start=(j == 0), stop=(j == G - 1))
                    m.then_inc(sum_ps, 1)
                m_ = n - 3
                if here(m_, UNITS):
                    pe.wait_ge(msg1T_sb, m_ + 1)
                    after(pe, msg2_sb, m_ - 1)
                    for j in range(G):
                        o = bank(5 + (k + 1) % 2, D, first=j * D)
                        pe.matmul(o, ones2[:], b2row[:], start=True, stop=False)
                        for c in range(KD):
                            m = pe.matmul(o, msg1T[:, (k + 1) % 2, c, j * 128:j * 128 + 128], w2c[:, c, :],
                                          start=False, stop=(c == KD - 1))
                    m.then_inc(msg2_ps, 1)

            steps(pe, edge_step, -1, LAST, 1, UNITS // TURN - 1, TURN)

            pe.wait_ge(uw1_in, 16)
            pe.wait_ge(upd_w_in, 48)
            pe.wait_ge(sum_sb, UNITS)
            done = 0
            for c, blocks in enumerate(CH):
                nb = len(blocks)
                t0 = blocks[0]

                if c >= 1:
                    pe.wait_ge(aggT_sb, c)
                for k in range(KD):
                    for i, t in enumerate(blocks):
                        m = turn(bank(k, NP, first=i * NP), agg[0:NP, t, k * 128:k * 128 + 128], NP)
                m.then_inc(aggT_ps, 1)
                pe.wait_ge(aggT_sb, c + 1)
                if c >= 1:
                    pe.wait_ge(hid_sb, c)
                for f in range(KD):
                    o = bank(2 + f, nb * NP)
                    for k in range(KD):
                        pe.matmul(o, uw1_sb[:, k, f * 128:f * 128 + 128], xnT[:, t0:t0 + nb, k, 0:NP],
                                  start=(k == 0), stop=False)
                    for k in range(KD):
                        m = pe.matmul(o, uw1_sb[:, KD + k, f * 128:f * 128 + 128], aggT[c % 2][:, k, 0:nb, :],
                                      start=False, stop=(k == KD - 1))
                m.then_inc(hid_ps, 1)
                pe.wait_ge(hid_sb, c + 1)
                for i, t in enumerate(blocks):
                    if t >= 4:
                        pe.wait_ge(x2_ok, t - 3)
                    o = bank(4 + t % 4, D, rows=NP)
                    for f in range(KD):
                        pe.matmul(o, hidT[c % 2][:, f, i, :], uw2_sb[:, f, :], start=(f == 0), stop=False)
                    for k in range(KD):
                        m = pe.matmul(o, xnT[:, t, k, 0:NP], mixG[:, k, :], start=False, stop=(k == KD - 1))
                    m.then_inc(upd_ps, 1)

            pe.wait_ge(x2_ok, NB)

            def turn_xm(t):
                pe.wait_ge(xm_ok, t + 1)
                if t >= 2:
                    pe.wait_ge(xmT_sb, t - 1)
                for k in range(KD):
                    m = turn(bank(t % 2, NP, first=k * NP), xm[0:NP, t, k * 128:k * 128 + 128], NP)
                m.then_inc(xmT_ps, 1)

            turn_xm(0)
            for t in range(NB):
                if t + 1 < NB:
                    turn_xm(t + 1)
                pe.wait_ge(xmT_sb, t + 1)
                for k in range(KD):
                    m = pe.matmul(bank(2, NE, rows=NP, first=t * NE), xmT[t % 2][:, k, :], wr_sb[:, k, :],
                                  start=(k == 0), stop=(k == KD - 1))
                m.then_inc(logit_ps, 1)
            pe.wait_ge(hotk_ok, 1)
            flat = hot_k[0:NP].rearrange("p e m -> p (e m)")
            pe.matmul(bank(3, NE * KT, rows=NP), earlier[0:NP, 0:NP], flat, start=True, stop=True)
            pe.matmul(bank(4, NE * KT, rows=NP), ones[0:NP, 0:NP], flat, start=True, stop=True).then_inc(route_ps, 1)

            pe.wait_ge(w1_in, 16 * (NE + 1))
            pe.wait_ge(w2_in, 16 * (NE + 1))
            pe.wait_ge(slots_ok, 1)
            pe.wait_ge(tile_ok, 1)

            def slots_step(n, k):
                m_ = n
                if here(m_, SLOT_TILES):
                    ex = pe.value_load(tile_e[0:1, bass.ts(m_, 1)], min_val=0, max_val=NE - 1)
                    pe.wait_ge(sxT_sb, m_ + 1)
                    after(pe, sh_pre, m_ - 1)
                    for c in range(KD):
                        m = pe.matmul(bank(1 + k % 2, HID), slot_xT[k % 2][:, c, :],
                                      w1_sb[:, bass.ts(ex, 1), c, :].rearrange("p a n -> p (a n)"),
                                      start=(c == 0), stop=(c == KD - 1))
                    m.then_inc(sh_ps, 1)
                m_ = n + 1
                if here(m_, SLOT_TILES):
                    pe.wait_ge(slot_in[(k + 1) % 4], 16 * ((m_ - (k + 1) % 4) // 4) + 16 if isinstance(m_, int)
                               else (m_ - (k + 1) % 4) * 4 + 16)
                    after(pe, sxT_sb, m_)
                    for c in range(KD):
                        m = turn(bank(0, 128, first=c * 128), slot_x[(k + 1) % 4][:, c * 128:c * 128 + 128], 128)
                    m.then_inc(sxT_ps, 1)
                m_ = n - 1
                if here(m_, SLOT_TILES):
                    pe.wait_ge(sh_sb, m_ + 1)
                    after(pe, shT_sb, m_ - 1)
                    for c in range(HC):
                        m = turn(bank(3 + (k + 1) % 2, 128, first=c * 128),
                                 slot_h[(k + 1) % 2][:, c * 128:c * 128 + 128], 128)
                    m.then_inc(shT_ps, 1)
                m_ = n - 2
                if here(m_, SLOT_TILES):
                    ex = pe.value_load(tile_e[0:1, bass.ts(m_, 1)], min_val=0, max_val=NE - 1)
                    pe.wait_ge(shT_sb, m_ + 1)
                    after(pe, sy_sb, m_ - 1)
                    for c in range(HC):
                        m = pe.matmul(bank(5 + k % 2, D), slot_hT[k % 2][:, c, :],
                                      w2_sb[:, bass.ts(ex, 1), c, :].rearrange("p a n -> p (a n)"),
                                      start=(c == 0), stop=(c == HC - 1))
                    m.then_inc(sy_ps, 1)

            steps(pe, slots_step, -1, SLOT_TILES + 2, 1, SLOT_TILES // 4 - 1, 4)

        def stage_dst(act, t):
            act.wait_ge(tab_ps, t + 1)
            if t >= 2:
                act.wait_ge(dst_out[t % 2], 16 * (t // 2))
            act.activation(dst_stage[t % 2][0:NP, :], bank(4 + t % 2, D, rows=NP), ACT.Copy).then_inc(dst_sb, 1)

        @block.scalar
        def _(act):
            A = act.activation
            act.wait_ge(wT_ps, 1)
            A(wkvT[:, 0, :], ps[:, 4:6, :].rearrange("p a n -> p (a n)"), ACT.Copy).then_inc(wT_sb, 1)
            act.wait_ge(wT_ps, 2)
            A(wkvT[:, 1, :], ps[:, 2:4, :].rearrange("p a n -> p (a n)"), ACT.Copy).then_inc(wT_sb, 1)
            act.wait_ge(wT_ps, 3)
            A(woutT[:].rearrange("p j n -> p (j n)"), ps[:, 0:2, :].rearrange("p a n -> p (a n)"), ACT.Copy)\
                .then_inc(wT_sb, 1)
            act.wait_ge(consts, N_CONST)
            act.wait_ge(var_ok, 1)
            A(rstd[0:NP], meanvar[0:NP, :, 1], ACT.Sqrt, bias=eps_col[0:NP, :]).then_inc(sd_ok, 1)
            for t in range(NB):
                act.wait_ge(xnT_ps, t + 1)
                A(xnT[:, t, :, 0:NP], bank(t % 2, KD * NP).rearrange("p (k n) -> p k n", k=KD), ACT.Copy)\
                    .then_inc(xnT_sb, 1)
                if t >= 1:
                    stage_dst(act, t - 1)
            stage_dst(act, NB - 1)
            for t in range(NB):
                b = 2 + 2 * (t % 2)
                act.wait_ge(kv_ps, t + 1)
                if t >= 1:
                    act.wait_ge(ss_ok, t)
                A(kv_sq[0:NP, :], ps[0:NP, b:b + 2, :].rearrange("p a n -> p (a n)"), ACT.Square).then_inc(sq_sb, 1)
                if t >= 2:
                    act.wait_ge(dots_ps, t - 1)
                A(v_n[t % 2][0:NP, :], ps[0:NP, b + 1, :], ACT.Copy).then_inc(v_sb, 1)
                act.wait_ge(ss_ok, t + 1)
                A(kv_ss[0:NP, :], kv_ss[0:NP, :], ACT.Sqrt, bias=eps_col[0:NP, :], scale=1.0 / HD).then_inc(kvsd_ok, 1)
            act.wait_ge(mixP_ps, 1)
            act.wait_ge(b2row_in, 16)
            act.wait_ge(ones2_ok, 1)
            A(mixP[:].rearrange("p j n -> p (j n)"), ps[:, 0:2, :].rearrange("p a n -> p (a n)"), ACT.Copy)\
                .then_inc(mixP_sb, 1)
            for h in range(2):
                act.wait_ge(scattered[h], 16 * EC // 2)
            for c in range(KD):
                act.wait_ge(mixG_ps, c + 1)
                A(mixG[:, c, :], bank(2 + c, D), ACT.Copy, scale=1.0 / N).then_inc(mixG_sb, 1)

            def edge_step(n, k):
                m_ = n - 4
                if here(m_, UNITS):
                    act.wait_ge(msg2_ps, m_ + 1)
                    after(act, sum_ps, m_ - 1)
                    A(msg2[:, k % 2].rearrange("p j n -> p (j n)"), bank(5 + k % 2), ACT.Silu).then_inc(msg2_sb, 1)
                m_ = n + 1
                if here(m_, UNITS):
                    act.wait_ge(hotT_ps, m_ + 1)
                    after(act, pre_ps, m_ - 1)
                    A(hotT[:, (k + 1) % 2, :], bank(0, UE), ACT.Copy).then_inc(hotT_sb, 1)
                m_ = n - 3
                if here(m_, UNITS):
                    act.wait_ge(msg1T_ps, m_ + 1)
                    after(act, msg2_ps, m_ - 1)
                    A(msg1T[:, (k + 1) % 2].rearrange("p c n -> p (c n)"), bank(3 + (k + 1) % 2), ACT.Copy)\
                        .then_inc(msg1T_sb, 1)
                if here(n, UNITS):
                    act.wait_ge(pre_sb, n + 1)
                    v = msg1[:, k % 3].rearrange("p j n -> p (j n)")
                    A(v, v, ACT.Silu).then_inc(msg1_sb, 1)

            steps(act, edge_step, -1, LAST, 1, UNITS // TURN - 1, TURN)

            act.wait_ge(small_in, 16 * SMALL)
            for c, blocks in enumerate(CH):
                nb = len(blocks)
                act.wait_ge(aggT_ps, c + 1)
                if c >= 2:
                    act.wait_ge(hid_ps, c - 1)
                A(aggT[c % 2][:, :, 0:nb, :].rearrange("p k i n -> p k (i n)"), ps[:, 0:2, 0:nb * NP], ACT.Copy)\
                    .then_inc(aggT_sb, 1)
                act.wait_ge(hid_ps, c + 1)
                if c >= 2:
                    act.wait_ge(upd_ps, 4 * (c - 1))
                for f in range(KD):
                    m = A(hidT[c % 2][:, f, 0:nb, :].rearrange("p i n -> p (i n)"), bank(2 + f, nb * NP), ACT.Silu,
                          bias=ub1_col[:, f:f + 1])
                m.then_inc(hid_sb, 1)
            act.wait_ge(var1_ok, 1)
            A(rstd[0:NP], meanvar[0:NP, :, 1], ACT.Sqrt, bias=eps_col[0:NP, :]).then_inc(sd1_ok, 1)
            act.wait_ge(var2_ok, 1)
            A(rst2[0:NP], rst2[0:NP], ACT.Sqrt, bias=eps_col[0:NP, :]).then_inc(sd2_ok, 1)
            for t in range(NB):
                act.wait_ge(xmT_ps, t + 1)
                if t >= 2:
                    act.wait_ge(logit_ps, t - 1)
                for k in range(KD):
                    m = A(xmT[t % 2][:, k, :], bank(t % 2, NP, first=k * NP), ACT.Identity,
                          bias=beta_col[:, k:k + 1], scale=gamma_col[:, k:k + 1])
                m.then_inc(xmT_sb, 1)
            act.wait_ge(gap_ok, 1)
            A(wtmp[0:NP], wtmp[0:NP], ACT.Exp).then_inc(exp_ok, 1)

            def slots_step(n, k):
                m_ = n + 1
                if here(m_, SLOT_TILES):
                    act.wait_ge(sxT_ps, m_ + 1)
                    after(act, sh_ps, m_ - 1)
                    for c in range(KD):
                        m = A(slot_xT[(k + 1) % 2][:, c, :], bank(0, 128, first=c * 128), ACT.Identity,
                              bias=beta_col[:, c:c + 1], scale=gamma_col[:, c:c + 1])
                    m.then_inc(sxT_sb, 1)
                if here(n, SLOT_TILES):
                    act.wait_ge(sh_pre, n + 1)
                    A(slot_h[k % 2][:], slot_h[k % 2][:], ACT.Gelu).then_inc(sh_sb, 1)

            steps(act, slots_step, -1, SLOT_TILES, 1, SLOT_TILES // 4 - 1, 4)

        @block.vector
        def _(dve):
            st = Steps(dve, dve_step)

            def step(ins):
                st.did(ins)
                st.join()

            R = slice(0, NP)
            dve.wait_ge(edges_in, 48)
            dve.wait_ge(consts, N_CONST)
            step(dve.tensor_copy(rank_f[R], src_i[R]))
            step(dve.tensor_scalar(row_f[R], rank_f[R], 1.0 / NB, 0.5 / NB - 0.5, ALU.mult, ALU.add))
            step(dve.tensor_scalar(row_f[R], row_f[R], ROUND, None, ALU.add))
            step(dve.tensor_scalar(row_f[R], row_f[R], -ROUND, None, ALU.add))
            step(dve.scalar_tensor_tensor(blk_f[R], row_f[R], -float(NB), rank_f[R], ALU.mult, ALU.add))
            step(dve.tensor_tensor(onehot[R], blk_f[R].unsqueeze(1).broadcast_to([NP, NB, EC]),
                                   iota[R, 0:NB].unsqueeze(2).broadcast_to([NP, NB, EC]), ALU.is_equal))
            flat = onehot[R].rearrange("p b c -> p (b c)")
            step(dve.tensor_tensor_scan(scanned[R], flat, flat, 0.0, ALU.add, ALU.bypass))
            last = scanned[R].rearrange("p (b c) -> p b c", b=NB)[:, :, EC - 1]
            step(dve.tensor_copy(cum[R], last))
            step(dve.tensor_copy(rowcnt[R, 0:1], cum[R, 0:1]))
            st.did(dve.tensor_tensor(rowcnt[R, 1:NB], cum[R, 1:NB], cum[R, 0:NB - 1], ALU.subtract))
            st.join()
            step(dve.tensor_tensor(cum[R], cum[R], rowcnt[R], ALU.subtract))
            dve.tensor_copy(stats[R, 0, 0:1], cum[R, 0:1]).then_inc(rowcnt_ok, 1)
            step(dve.tensor_copy(rec_sb[R, :, 0], dst_i[R]))
            step(dve.tensor_copy(rec_sb[R, :, 1], row_f[R]))
            step(dve.tensor_copy(d2_r[R], d2_f[R]))
            step(dve.tensor_copy(rec_sb[R, :, 2], d2_r[R].bitcast(F32)))
            step(dve.tensor_tensor(rec_sb[R, :, 3], d2_f[R], d2_r[R].bitcast(F32), ALU.subtract))
            dve.wait_ge(counts_ps, 1)
            step(dve.tensor_copy(prefix[:], bank(6, NB)))
            step(dve.tensor_scalar(ends[:], bank(6, NB, first=32), float(UE - 1), None, ALU.add))
            step(dve.tensor_copy(ints[:], ends[:]))
            step(dve.tensor_scalar(ints[:], ints[:], 8, None, ALU.logical_shift_right))
            step(dve.tensor_copy(nunits[:], ints[:]))
            step(dve.tensor_tensor_scan(ends[:], nunits[:], nunits[:], 0.0, ALU.add, ALU.bypass))
            step(dve.tensor_tensor(nunits[:], ends[:], nunits[:], ALU.subtract))
            step(dve.scalar_tensor_tensor(prefix[:], nunits[:], float(UE), prefix[:], ALU.mult, ALU.add))
            step(dve.scalar_tensor_tensor(prefix[R], prefix[R], -1.0, cum[R], ALU.add, ALU.subtract))
            for b in range(NB):
                st.did(dve.scalar_tensor_tensor(masked[R, b, :], scanned[R, b * EC:b * EC + EC], prefix[R, b:b + 1],
                                                onehot[R, b, :], ALU.add, ALU.mult))
            st.join()
            step(dve.tensor_reduce(rank_f[R], masked[R].rearrange("p b c -> p c b"), AX.X, ALU.add))
            step(dve.tensor_copy(pos_i[R], rank_f[R]))
            step(dve.tensor_scalar(low_i[R], pos_i[R], 127, None, ALU.bitwise_and))
            step(dve.tensor_scalar(top_i[R], pos_i[R], 7, None, ALU.logical_shift_right))
            step(dve.tensor_copy(rank_f[R], low_i[R]))
            step(dve.tensor_copy(blk_f[R], top_i[R]))
            step(dve.scalar_tensor_tensor(rank_f[R], rank_f[R], float(TILES), blk_f[R], ALU.mult, ALU.add))
            dve.tensor_copy(pos_i[R], rank_f[R]).then_inc(pos_ok, 1)
            step(dve.tensor_tensor(unit_le[:], ends[0:1].unsqueeze(1).broadcast_to([1, UNITS, NB]),
                                   iota[0:1, 0:UNITS].unsqueeze(2).broadcast_to([1, UNITS, NB]), ALU.is_le))
            step(dve.tensor_reduce(unit_f[:], unit_le[:], AX.X, ALU.add))
            step(dve.tensor_scalar(unit_f[:], unit_f[:], float(NB - 1), None, ALU.min))
            step(dve.tensor_copy(unit_blk[:], unit_f[:]))
            step(dve.tensor_copy(unit_f[:], unit_blk[:]))
            dve.memset(nw_y[:], 1.0).then_inc(units_ok, 1)

            dve.wait_ge(small_in, 16 * SMALL)
            for k in range(KD):
                st.did(dve.tensor_scalar(w2c[:, k, :], w2c_raw[:, k, :], g_col[:, k:k + 1], None, ALU.mult))
            dve.wait_ge(b2_ps, 1)
            step(dve.tensor_tensor(b2tmp[:], bank(7, D, rows=1), mb2_row[:], ALU.add))
            step(dve.tensor_copy(b2row[0:1, :], b2tmp[:]))
            step(dve.tensor_copy(b2pair[0:1, :], b2row[0:1, :].bitcast(F32)))
            dve.tensor_tensor(b2lo[:], b2tmp[:], b2pair[0:1, :], ALU.subtract).then_inc(b2_hl, 1)
            dve.tensor_copy(ones2[:], ones2f[:]).then_inc(ones2_ok, 1)
            st.join()
            dve.memset(nw_t[:], 0.0).then_inc(w2c_ok, 1)
            step(dve.memset(xnT[:, :, :, NP:128], 0.0))
            dve.memset(nw_v[:], 0.0).then_inc(pads_ok, 1)

            dve.wait_ge(x_in, 16)

            def block_stats(t):
                step(dve.bn_stats(stats[R, t, :], res[R, t, :]))
                st.did(dve.bn_aggr(meanvar[R, t, :], stats[R, t, :]))

            for t in range(NB):
                st.did(dve.bn_stats(stats[R, t, :], res[R, t, :]))
            st.join()
            for t in range(NB):
                st.did(dve.bn_aggr(meanvar[R, t, :], stats[R, t, :]))
            st.join()
            dve.tensor_copy(nw_t[R, 0, 0:1], meanvar[R, 0, 0:1]).then_inc(var_ok, 1)
            dve.wait_ge(sd_ok, 1)
            step(dve.reciprocal(rstd[R], rstd[R]))
            dve.wait_ge(defaults_out, 16)
            for t in range(NB):
                dve.tensor_scalar(xn[R, t, :], res[R, t, :], meanvar[R, t, 0:1], rstd[R, t:t + 1],
                                  ALU.subtract, ALU.mult).then_inc(xn_ok, 1)
            dve.wait_ge(zeros_out, 16)
            for t in range(NB):
                dve.wait_ge(tab_ps, t + 1)
                step(dve.tensor_copy(src_hi[:, t, :], bank(2 + t % 2, D)))
                dve.tensor_tensor(src_lo[:, t, :], bank(2 + t % 2, D), src_hi[:, t, :].bitcast(F32), ALU.subtract)\
                   .then_inc(tab_sb, 1)
            dve.wait_ge(wT_sb, KD + 1)
            heads = wkvT[:].rearrange("p k (h d) -> p (k h) d", d=HD)
            step(dve.tensor_reduce(wmean[:], heads, AX.X, ALU.add))
            step(dve.tensor_scalar(wmean[:], wmean[:], 1.0 / HD, None, ALU.mult))
            dve.tensor_tensor(heads, heads, wmean[:].unsqueeze(2).broadcast_to([128, KD * 2 * HEADS, HD]),
                              ALU.subtract).then_inc(wkv_centered, 1)
            dve.wait_ge(b2row_in, 16)
            dve.tensor_copy(b2row[:], b2pair[:]).then_inc(b2row_ok, 1)
            dve.wait_ge(upd_w_in, 48)
            step(dve.tensor_tensor(bias_bc[:], bias_bc[:], bout_bc[:], ALU.add))
            for t in range(NB):
                b = 2 + 2 * (t % 2)
                dve.wait_ge(sq_sb, t + 1)
                if t >= 1:
                    dve.wait_ge(kn_ok, t)
                dve.tensor_reduce(kv_ss[R], kv_sq[R].rearrange("p (h d) -> p h d", d=HD), AX.X, ALU.add)\
                   .then_inc(ss_ok, 1)
                st.did(dve.tensor_tensor(res[R, t, :], res[R, t, :], bias_bc[R, :], ALU.add))
                dve.wait_ge(kvsd_ok, t + 1)
                step(dve.tensor_tensor(kv_rs[R], kv_ss[R, 0:HEADS], kv_ss[R, HEADS:2 * HEADS], ALU.mult))
                step(dve.reciprocal(kv_rs[R], kv_rs[R]))
                if t >= 2:
                    dve.wait_ge(dots_ps, t - 1)
                dve.tensor_tensor(k_n[t % 2][R].rearrange("p (h d) -> p h d", d=HD),
                                  ps[R, b, :].rearrange("p (h d) -> p h d", d=HD),
                                  kv_rs[R].unsqueeze(2).broadcast_to([NP, HEADS, HD]), ALU.mult).then_inc(kn_ok, 1)
                st.did(dve.tensor_tensor(res[R, t, :], res[R, t, :], xn[R, t, :], ALU.add))
            dve.wait_ge(dots_ps, NB)
            step(dve.memset(k_n[0][:], 0.0))
            pair = lambda ap: ap.rearrange("p (j d) -> p j d", d=128)
            st.did(dve.tensor_copy(pair(k_n[0][0:HD, :])[:, :, 0:HD], pair(bank(6, rows=HD))[:, :, 0:HD]))
            st.did(dve.tensor_copy(pair(k_n[0][HD:128, :])[:, :, HD:128], pair(ps[HD:128, 6, :])[:, :, HD:128]))
            st.join()
            dve.memset(agg[:], 0.0).then_inc(diag_ok, 1)
            dve.wait_ge(diag_ok, 1)

            def rsqrt_pair(s):
                y = nw_y[:, s:s + 2, :]
                step(dve.tensor_scalar(nw_v[:], emv[:, s:s + 2, :, 1], EPS, None, ALU.add))
                step(dve.tensor_scalar(nw_i[:], nw_v[:].bitcast(I32), 1, None, ALU.logical_shift_right))
                step(dve.tensor_scalar(nw_i[:], nw_i[:], -1.0, float(RSQRT_MAGIC), ALU.mult, ALU.add))
                step(dve.tensor_copy(y, nw_i[:].bitcast(F32)))
                for _ in range(3):
                    step(dve.tensor_tensor(nw_t[:], y, y, ALU.mult))
                    step(dve.scalar_tensor_tensor(nw_t[:], nw_t[:], -0.5, nw_v[:], ALU.mult, ALU.mult))
                    step(dve.scalar_tensor_tensor(y, nw_t[:], 1.5, y, ALU.add, ALU.mult))

            def edge_step(n, k, turn_rows):
                if here(n, UNITS):
                    dve.wait_ge(pre_ps, n + 1)
                    dve.wait_ge(row_in[k], (n - k) // TURN * 32 + 32 if isinstance(n, int) else turn_rows)
                    after(dve, msg1n_sb, n - 2)
                    dve.tensor_tensor(msg1[:, k % 3].rearrange("p j n -> p (j n)"), bank(1 + k % 2),
                                      dst_row[:, k].rearrange("p j n -> p (j n)"), ALU.add).then_inc(pre_sb, 1)
                blk = None
                if here(n - 5, UNITS):
                    blk = dve.value_load(unit_blk[0:1, bass.ts(n - 5, 1)], min_val=0, max_val=NB - 1)
                m_ = n - 1
                kk = (k - 1) % TURN
                if here(m_, UNITS):
                    dve.wait_ge(msg1_sb, m_ + 1)
                    for j in range(G):
                        st.did(dve.bn_stats(est[:, kk, j, :], msg1[:, kk % 3, j, :]))
                    st.join()
                if here(n - 5, UNITS):
                    dve.wait_ge(sum_ps, n - 4)
                    after(dve, sum_sb, n - 5)
                    a = agg[0:NP, bass.ts(blk, 1), :].rearrange("p a n -> p (a n)")
                    dve.tensor_tensor(a, a, bank(7, D, rows=NP), ALU.add).then_inc(sum_sb, 1)
                if here(m_, UNITS):
                    for j in range(G):
                        st.did(dve.bn_aggr(emv[:, kk, j, :], est[:, kk, j, :]))
                    st.join()
                    if k % 2 == 0:
                        rsqrt_pair((k - 2) % TURN)
                m_ = n - 2
                kk = (k - 2) % TURN
                if here(m_, UNITS):
                    after(dve, msg1T_ps, m_ - 1)
                    for j in range(G):
                        m = dve.tensor_scalar(msg1n[:, k % 2, j, :], msg1[:, kk % 3, j, :], emv[:, kk, j, 0:1],
                                              nw_y[:, kk, j:j + 1], ALU.subtract, ALU.mult)
                        if j < G - 1:
                            st.did(m)
                    m.then_inc(msg1n_sb, 1)

            for n in range(-1, TURN):
                edge_step(n, n % TURN, 0)
            with dve.Fori(1, UNITS // TURN) as i:
                st.enter(i, 1, TURN * (2 * G + G - 1) + TURN // 2 * 13)
                for k in range(TURN):
                    edge_step(TURN * i + k, k, 32 * i + 32)
            st.leave(UNITS // TURN - 1)
            for n in range(UNITS, LAST):
                edge_step(n, n % TURN, 0)

            for t in range(NB):
                dve.wait_ge(upd_ps, t + 1)
                dve.tensor_tensor(res[R, t, :], res[R, t, :], bank(4 + t % 4, D, rows=NP), ALU.add).then_inc(x2_ok, 1)
                if t >= 1:
                    dve.wait_ge(x2_ok, t)
                    st.did(dve.bn_stats(stats[R, t - 1, :], res[R, t - 1, :]))
            dve.wait_ge(x2_ok, NB)
            step(dve.bn_stats(stats[R, NB - 1, :], res[R, NB - 1, :]))
            for t in range(NB):
                st.did(dve.bn_aggr(meanvar[R, t, :], stats[R, t, :]))
            st.join()
            dve.tensor_copy(nw_t[R, 0, 0:1], meanvar[R, 0, 0:1]).then_inc(var1_ok, 1)
            dve.wait_ge(sd1_ok, 1)
            step(dve.reciprocal(rstd[R], rstd[R]))
            step(dve.tensor_tensor(rst2[R], rstd[R], rstd[R], ALU.mult))
            dve.tensor_tensor(rst2[R], rst2[R], meanvar[R, :, 1], ALU.mult).then_inc(var2_ok, 1)
            dve.wait_ge(sd2_ok, 1)
            step(dve.reciprocal(rst2[R], rst2[R]))
            step(dve.tensor_tensor(rstd[R], rstd[R], rst2[R], ALU.mult))
            for t in range(NB):
                dve.tensor_scalar(xm[R, t, :], res[R, t, :], meanvar[R, t, 0:1], rstd[R, t:t + 1],
                                  ALU.subtract, ALU.mult).then_inc(xm_ok, 1)
            dve.wait_ge(logit_ps, NB)
            step(dve.tensor_tensor(logits[R], bank(2, NB * NE, rows=NP).rearrange("p (t e) -> p t e", e=NE),
                                   br_bc[R].unsqueeze(1).broadcast_to([NP, NB, NE]), ALU.add))
            for t in range(NB):
                st.did(dve.max(top_v[R, t, :], logits[R, t, :]))
            st.join()
            for t in range(NB):
                st.did(dve.max_index(top_e[R, t, :], top_v[R, t, :], logits[R, t, :]))
            st.join()
            dve.tensor_tensor(wtmp[R], top_v[R, :, 1], top_v[R, :, 0], ALU.subtract).then_inc(gap_ok, 1)
            for k in range(TOPK):
                st.did(dve.tensor_copy(top_f[R, k, :], top_e[R, :, k]))
            st.join()
            step(dve.tensor_tensor(hot_k[R], top_f[R].rearrange("p k t -> p (k t)").unsqueeze(1).broadcast_to([NP, NE, KT]),
                                   iota[R, 0:NE].unsqueeze(2).broadcast_to([NP, NE, KT]), ALU.is_equal))
            dve.tensor_copy(nw_t[R, 0, 0:1], hot_k[R, 0, 0:1]).then_inc(hotk_ok, 1)
            dve.wait_ge(exp_ok, 1)
            step(dve.tensor_scalar(wgt[R, 0, :], wtmp[R], 1.0, None, ALU.add))
            step(dve.reciprocal(wgt[R, 0, :], wgt[R, 0, :]))
            step(dve.tensor_tensor(wgt[R, 1, :], wgt[R, 0, :], wtmp[R], ALU.mult))
            dve.wait_ge(route_ps, 1)
            hc = hot_c[R].rearrange("p e m -> p (e m)")
            step(dve.tensor_copy(hc, bank(4, NE * KT, rows=NP)))
            hp = hot_p[R].rearrange("p e m -> p (e m)")
            step(dve.tensor_tensor_scan(hp, hc, hc, 0.0, ALU.add, ALU.bypass))
            step(dve.tensor_copy(e_cum[R], hot_p[R, :, KT - 1]))
            step(dve.tensor_copy(e_cnt[R, 0:1], e_cum[R, 0:1]))
            step(dve.tensor_tensor(e_cnt[R, 1:NE], e_cum[R, 1:NE], e_cum[R, 0:NE - 1], ALU.subtract))
            step(dve.tensor_tensor(e_cum[R], e_cum[R], e_cnt[R], ALU.subtract))
            step(dve.tensor_scalar(e_cnt[R], e_cnt[R], 127.0, None, ALU.add))
            step(dve.tensor_copy(e_int[R], e_cnt[R]))
            step(dve.tensor_scalar(e_int[R], e_int[R], 7, None, ALU.logical_shift_right))
            step(dve.tensor_copy(e_til[R], e_int[R]))
            step(dve.tensor_tensor_scan(e_end[R], e_til[R], e_til[R], 0.0, ALU.add, ALU.bypass))
            step(dve.tensor_tensor(e_til[R], e_end[R], e_til[R], ALU.subtract))
            step(dve.scalar_tensor_tensor(e_cum[R], e_til[R], 128.0, e_cum[R], ALU.mult, ALU.subtract))
            step(dve.tensor_tensor(hp, hp, hc, ALU.subtract))
            step(dve.tensor_tensor(hp, hp, bank(3, NE * KT, rows=NP), ALU.add))
            step(dve.tensor_tensor(hot_p[R], hot_p[R], e_cum[R].unsqueeze(2).broadcast_to([NP, NE, KT]), ALU.add))
            step(dve.tensor_tensor(hot_p[R], hot_p[R], hot_k[R], ALU.mult))
            step(dve.tensor_reduce(slot_f[R].rearrange("p k t -> p (k t)"), hot_p[R].rearrange("p e m -> p m e"),
                                   AX.X, ALU.add))
            dve.tensor_copy(slot_i[R], slot_f[R]).then_inc(slots_ok, 1)
            step(dve.tensor_tensor(e_le[:], e_end[0:1].unsqueeze(1).broadcast_to([1, SLOT_TILES, NE]),
                                   iota[0:1, 0:SLOT_TILES].unsqueeze(2).broadcast_to([1, SLOT_TILES, NE]), ALU.is_le))
            step(dve.tensor_reduce(tile_f[:], e_le[:], AX.X, ALU.add))
            step(dve.tensor_scalar(tile_f[:], tile_f[:], float(NE - 1), None, ALU.min))
            dve.tensor_copy(tile_e[:], tile_f[:]).then_inc(tile_ok, 1)
            dve.wait_ge(tile_ok, 1)

            dve.wait_ge(w1_in, 16 * (NE + 1))
            dve.wait_ge(w2_in, 16 * (NE + 1))
            dve.wait_ge(sent, 16 * KT)

            def slots_step(n, k):
                m_ = n
                if here(m_, SLOT_TILES):
                    ex = dve.value_load(tile_e[0:1, bass.ts(m_, 1)], min_val=0, max_val=NE - 1)
                    dve.wait_ge(sh_ps, m_ + 1)
                    after(dve, shT_ps, m_ - 1)
                    dve.tensor_tensor(slot_h[k % 2][:], bank(1 + k % 2, HID),
                                      b1_bc[:, bass.ts(ex, 1), :].rearrange("p a n -> p (a n)"), ALU.add)\
                       .then_inc(sh_pre, 1)
                m_ = n - 1
                if here(m_, SLOT_TILES):
                    dve.wait_ge(shT_ps, m_ + 1)
                    after(dve, sy_ps, m_ - 1)
                    dve.tensor_copy(slot_hT[(k + 1) % 2][:].rearrange("p c n -> p (c n)"), bank(3 + (k + 1) % 2))\
                       .then_inc(shT_sb, 1)
                m_ = n - 2
                if here(m_, SLOT_TILES):
                    ex = dve.value_load(tile_e[0:1, bass.ts(m_, 1)], min_val=0, max_val=NE - 1)
                    dve.wait_ge(sy_ps, m_ + 1)
                    if isinstance(m_, int):
                        after(dve, slot_out[k % 2], 8 * (m_ - k % 2))
                    else:
                        dve.wait_ge(slot_out[k % 2], 8 * (m_ - k % 2))
                    dve.tensor_tensor(slot_y[k % 2][:], bank(5 + k % 2, D),
                                      b2_bc[:, bass.ts(ex, 1), :].rearrange("p a n -> p (a n)"), ALU.add)\
                       .then_inc(sy_sb, 1)

            steps(dve, slots_step, 0, SLOT_TILES + 2, 1, SLOT_TILES // 4 - 1, 4)
            for t in range(NB):
                dve.wait_ge(pick_in[t % 4], 32 * (t // 4 + 1))
                step(dve.scalar_tensor_tensor(res[R, t, :], pick[t % 4][R, 0, :], wgt[R, 0, t:t + 1], res[R, t, :],
                                              ALU.mult, ALU.add))
                dve.scalar_tensor_tensor(res[R, t, :], pick[t % 4][R, 1, :], wgt[R, 1, t:t + 1], res[R, t, :],
                                         ALU.mult, ALU.add).then_inc(final_ok, 1)
                dve.wait_ge(final_ok, t + 1)
                dve.memset(nw_t[:], 0.0).then_inc(picked, 1)


_INS = ['x', 'src', 'dst', 'edge_weight1', 'L0_gnn_mW1', 'L0_gnn_mb1', 'L0_gnn_ln_g', 'L0_gnn_ln_b', 'L0_gnn_mW2',
        'L0_gnn_mb2', 'L0_gnn_uW1', 'L0_gnn_ub1', 'L0_gnn_uW2', 'L0_gnn_ub2', 'L0_mix_Wqkv', 'L0_mix_Wout',
        'L0_mix_bout', 'L0_ffn_gamma', 'L0_ffn_beta', 'L0_ffn_Wr', 'L0_ffn_br', 'L0_ffn_W1', 'L0_ffn_b1',
        'L0_ffn_W2', 'L0_ffn_b2']


def kernel(**inputs):
    import numpy as _np
    import concourse.bacc as _bacc
    from concourse import mybir as _mybir
    from concourse.bass_utils import run_bass_kernel_spmd as _run

    nc = _bacc.Bacc("TRN2", target_bir_lowering=False, num_devices=1)
    arrays, args = {}, []
    for name in _INS:
        a = _np.ascontiguousarray(inputs[name])
        arrays[f"in_{name}_dram"] = a
        args.append(nc.dram_tensor(f"in_{name}_dram", a.shape, _mybir.dt.from_np(a.dtype), kind="ExternalInput").ap())
    out = nc.dram_tensor("out_0_dram", inputs["x"].shape, _mybir.dt.float32, kind="ExternalOutput").ap()
    gps_layer(nc, *args, out)
    r = _run(nc, [arrays], core_ids=[0])
    return r.results[0]["out_0_dram"]
```

```python
import concourse.bass as bass
from concourse import mybir
from contextlib import ExitStack

F32 = mybir.dt.float32
F32R = mybir.dt.float32r
F16 = mybir.dt.float16
I32 = mybir.dt.int32
U32 = mybir.dt.uint32
U16 = mybir.dt.uint16
ALU = mybir.AluOpType
ACT = mybir.ActivationFunctionType
AX = mybir.AxisListType

EPS = 1e-5
ROUND = 12582912.0
RSQRT_MAGIC = 1597463007


class Steps:

    def __init__(self, engine, semaphore):
        self.engine, self.semaphore, self.count, self.turns = engine, semaphore, 0, None

    def did(self, instruction):
        instruction.then_inc(self.semaphore, 1)
        self.count += 1

    def join(self):
        self.engine.wait_ge(self.semaphore, self.count if self.turns is None else self.turns + self.count)

    def enter(self, index, first, per_turn):
        self.turns, self.start, self.per_turn = (index - first) * per_turn, self.count, per_turn

    def leave(self, trips):
        assert self.count - self.start == self.per_turn, (self.count, self.start)
        self.turns, self.count = None, self.start + self.per_turn * trips


def gps_layer(nc, x, src, dst, edge_weight1, mW1, mb1, ln_g, ln_b, mW2, mb2, uW1, ub1, uW2, ub2,
              Wqkv, Wout, bout, gamma, beta, Wr, br, W1, b1, W2, b2, out):
    N, D = x.shape
    E = src.shape[0]
    NP = 125
    NB = N // NP
    EC = E // NP
    KD = D // 128
    G = 2
    UE = 128 * G
    TURN = 10
    UNITS = -(-((E + NB * (UE - 1)) // UE) // TURN) * TURN
    TILES = UNITS * G
    HD = 64
    NQ = Wqkv.shape[0] // 3
    HEADS = NQ // HD
    QC = NQ // 128
    NE, _, HID = W1.shape
    HC = HID // 128
    TOPK = 2
    SLOT_TILES = (TOPK * N + NE * 127) // 128
    KT = TOPK * NB
    HR = NP + 2
    assert NP * NB == N and NP * EC == E and SLOT_TILES % 2 == 0 and D == 256

    dst_table = nc.dram_tensor("dst_table", [N, D], F32).ap()
    sorted_edges = nc.dram_tensor("sorted_edges", [128 * TILES, 4], F32).ap()
    expert_in = nc.dram_tensor("expert_in", [SLOT_TILES * 128, D], F32).ap()
    expert_out = nc.dram_tensor("expert_out", [SLOT_TILES * 128, D], F32).ap()

    ctx = ExitStack()
    with ctx:
        def sem(name):
            return ctx.enter_context(nc.semaphore(name))

        base = (nc.sbuf_base + 31) // 32 * 32
        place, size_of, filled, cursor = {}, {}, {}, [base]

        def region(name, size):
            place[name], size_of[name], filled[name] = cursor[0], size, 0
            cursor[0] += (size + 31) // 32 * 32

        def at(name, shape, dt, owner, byte=0):
            return nc.alloc_sbuf_tensor_at(name, shape, dt, offset=place[owner] + byte)

        def nbytes(shape, dt):
            n = {F16: 2, U16: 2}.get(dt, 4)
            for k in shape[1:]:
                n *= k
            return (n + 31) // 32 * 32

        def inside(name, shape, dt, owner):
            t = at(name, shape, dt, owner, filled[owner])
            filled[owner] += nbytes(shape, dt)
            assert filled[owner] <= size_of[owner], (owner, name, filled[owner])
            return t

        NODE = NB * D * 4
        region("res", NODE)
        region("blocks", NODE)
        assert KD * 128 == D
        region("turned", NODE)
        region("src_hi", NODE)
        region("src_lo", NODE)
        region("edges", TILES * 16 + 512)
        region("work", 34 * 1024)
        region("weights", 32 * 1024)
        region("small", 9600)
        ctx.enter_context(nc.sbuf_tensor("arena", [128, (cursor[0] - base) // 4], F32))

        res = at("res_t", [128, NB, D], F32, "res")
        xn = at("xn_t", [128, NB, D], F32, "blocks")
        agg = at("agg_t", [128, NB, D], F32, "blocks")
        xnT = at("xnT_t", [128, NB, KD, 128], F32, "turned")
        src_hi = at("src_hi_t", [128, NB, D], F32R, "src_hi")
        src_lo = at("src_lo_t", [128, NB, D], F32R, "src_lo")
        recs = at("recs_t", [128, TILES, 4], F32, "edges")
        rec_sb = at("rec_sb_t", [128, EC, 4], F32, "edges")

        onehot = at("onehot_t", [128, NB, EC], F16, "turned")
        masked = at("masked_t", [128, NB, EC], U16, "turned")
        scanned = at("scanned_t", [128, NB * EC], F16, "work")
        src_i = at("src_i_t", [128, EC], I32, "blocks")
        dst_i = at("dst_i_t", [128, EC], I32, "blocks", 2048)
        blk_f = at("blk_f_t", [128, EC], F32, "blocks", 4096)
        row_f = at("row_f_t", [128, EC], F32, "blocks", 6144)
        rank_f = at("rank_f_t", [128, EC], F32, "blocks", 8192)
        low_i = at("low_i_t", [128, EC], I32, "blocks", 12288)
        top_i = at("top_i_t", [128, EC], I32, "blocks", 14336)
        d2_r = at("d2_r_t", [128, EC], F32R, "blocks", 16384)
        d2_f = at("d2_f_t", [128, EC], F32, "blocks", 18432)
        unit_le = at("unit_le_t", [1, UNITS, NB], F16, "work")
        defaults = at("defaults_t", [128, TILES // 10, 4], F32, "blocks", 20480)
        bias_bc = at("bias_bc_t", [128, D], F32, "work", 32768)
        bout_bc = at("bout_bc_t", [128, D], F32, "work", 33792)
        unit_f = at("unit_f_t", [1, UNITS], F32, "work", 16384)

        wkv_nat = at("wkv_nat_t", [128, 2 * QC, D], F32, "work", 20480)
        wout_nat = at("wout_nat_t", [128, KD, NQ], F32, "work", 28672)
        dst_stage = [at(f"dst_stage{i}", [128, D], F32, "work", 1024 * i) for i in range(2)]
        kv_sq = at("kv_sq_t", [128, 2 * NQ], F32, "work", 2048)
        k_n = [at(f"k_n{i}", [128, NQ], F32, "work", 6144 + 2048 * i) for i in range(2)]
        v_n = [at(f"v_n{i}", [128, NQ], F32, "work", 10240 + 2048 * i) for i in range(2)]
        zero_rows = at("zero_rows_t", [128, 2048], F32, "src_lo")

        msg1 = at("msg1_t", [128, TURN, G, D], F32, "work")
        hotT = at("hotT_t", [128, 2, UE], F32R, "work", 20480)
        msg1n = at("msg1n_t", [128, 2, G, D], F32, "work", 22528)
        msg1T = at("msg1T_t", [128, 2, KD, UE], F32, "work", 26624)
        msg2 = at("msg2_t", [128, 2, G, D], F32, "work", 30720)

        aggT = [at(f"aggT{i}", [128, KD, 4, NP], F32, "work", 4096 * i) for i in range(2)]
        hidT = [at(f"hidT{i}", [128, KD, 4, NP], F32, "work", 8192 + 4096 * i) for i in range(2)]
        xm = at("xm_t", [128, NB, D], F32, "work")
        xmT = [at(f"xmT{i}", [128, KD, NP], F32, "work", NODE + 1024 * i) for i in range(2)]
        w1_sb = at("w1_sb_t", [128, NE, KD, HID], F32, "src_hi")
        b1_bc = at("b1_bc_t", [128, NE, HID], F32, "src_hi", 32768)
        w2_sb = at("w2_sb_t", [128, NE, HC, D], F32, "blocks")
        b2_bc = at("b2_bc_t", [128, NE, D], F32, "blocks", 32768)
        slot_x = [at(f"slot_x{i}", [128, D], F32, "work", 1024 * i) for i in range(4)]
        slot_xT = [at(f"slot_xT{i}", [128, KD, 128], F32, "work", 4096 + 1024 * i) for i in range(2)]
        slot_h = [at(f"slot_h{i}", [128, HID], F32, "work", 6144 + 2048 * i) for i in range(2)]
        slot_hT = [at(f"slot_hT{i}", [128, HC, 128], F32, "work", 10240 + 2048 * i) for i in range(2)]
        slot_y = [at(f"slot_y{i}", [128, D], F32, "work", 14336 + 1024 * i) for i in range(2)]
        pick = [at(f"pick{i}", [128, TOPK, D], F32, "work", 16384 + 2048 * i) for i in range(4)]

        w = lambda n, s, t=F32: inside(n, s, t, "weights")
        mw1_sb = w("mw1_sb", [128, KD, 2, D])
        w2c_raw = w("w2c_raw", [128, KD, D])
        w2c = w("w2c", [128, KD, D])
        hot = at("hot_t", [128, TURN, G, 128], F32, "weights", filled["weights"])
        wkvT = w("wkvT", [128, KD, 2 * NQ])
        wq_nat = w("wq_nat", [128, QC, D])
        woutT = w("woutT", [128, QC, D])
        mixP = w("mixP", [128, QC, D])
        uw1_sb = at("uw1_sb", [128, 2 * KD, D], F32, "weights", filled["weights"] - 4 * QC * D)
        mixP_byte = filled["weights"] - 4 * QC * D
        b2tmp = at("b2tmp", [1, D], F32, "weights", mixP_byte)
        b2lo = at("b2lo", [1, D], F32, "weights", mixP_byte + 1024)
        b2pair = at("b2pair", [2, D], F32, "work", 17408)
        mb2_row = at("mb2_row", [1, D], F32, "weights", mixP_byte + 2048)
        ones2f = at("ones2f", [2, 128], F32, "weights", mixP_byte + 3072)
        pos_i = at("pos_i_t", [128, EC], I32, "weights", filled["weights"])
        mixG = w("mixG", [128, KD, D])
        uw2_sb = w("uw2_sb", [128, KD, D])
        place["late"], size_of["late"], filled["late"] = place["weights"], 4096, 0
        s = lambda n, sh, t=F32: inside(n, sh, t, "small")
        ident = s("ident", [128, 128])
        iota = s("iota", [128, 256])
        earlier = s("earlier", [128, 128])
        ones = s("ones", [128, 128])
        bw = s("bw", [2, D])
        bw_sel = s("bw_sel", [2, 128])
        b2row = s("b2row", [2, D], F32R)
        ones2 = s("ones2", [2, 128], F32R)
        g_col = s("g_col", [128, KD])
        b_col = s("b_col", [128, KD])
        ub1_col = s("ub1_col", [128, KD])
        gamma_col = s("gamma_col", [128, KD])
        beta_col = s("beta_col", [128, KD])
        wr_sb = s("wr_sb", [128, KD, NE])
        br_bc = s("br_bc", [128, NE])
        eps_col = s("eps_col", [128, 1])
        stats = s("stats", [128, NB, 6])
        meanvar = s("meanvar", [128, NB, 2])
        rstd = s("rstd", [128, NB])
        rowcnt = s("rowcnt", [128, NB])
        cum = s("cum", [128, NB])
        ints = s("ints", [128, NB], I32)
        prefix = s("prefix", [128, NB])
        nunits = s("nunits", [128, NB])
        ends = s("ends", [128, NB])
        unit_blk = s("unit_blk", [1, UNITS], I32)
        kv_ss = s("kv_ss", [128, 2 * HEADS])
        kv_rs = s("kv_rs", [128, HEADS])
        wmean = s("wmean", [128, KD * 2 * HEADS])
        scat_idx = s("scat_idx", [128, 2, 8], I32)
        stage_idx = s("stage_idx", [128, 2, TURN], I32)
        fence = s("fence", [1, TURN])
        nw_t = s("nw_t", [128, 2, G])
        place["w2c_raw"], size_of["w2c_raw"], filled["w2c_raw"] = place["weights"] + 4096, 2048, 0
        e = lambda n, sh, t=F32: inside(n, sh, t, "w2c_raw")
        est = e("est", [128, TURN, G, 6])
        emv = e("emv", [128, TURN, G, 2])
        nw_y = e("nw_y", [128, TURN, G])
        nw_b = e("nw_b", [128, TURN, G])
        nw_v = e("nw_v", [128, 2, G])
        nw_s = e("nw_s", [128, 2, G])
        nw_1 = e("nw_1", [128, 2, G])
        nw_2 = e("nw_2", [128, 2, G])
        nw_i = e("nw_i", [128, 2, G], I32)

        hot_k = at("hot_k", [128, NE, KT], F32, "edges")
        hot_c = at("hot_c", [128, NE, KT], F32, "edges", 1600)
        hot_p = at("hot_p", [128, NE, KT], F32, "edges", 3200)
        logits = at("logits", [128, NB, NE], F32, "edges", 4800)
        top_v = at("top_v", [128, NB, NE], F32, "edges", 5600)
        top_e = at("top_e", [128, NB, 8], U32, "edges", 6400)
        top_f = inside("top_f", [128, TOPK, NB], F32, "late")
        slot_i = inside("slot_i", [128, TOPK, NB], I32, "late")
        slot_f = inside("slot_f", [128, TOPK, NB], F32, "late")
        wgt = inside("wgt", [128, TOPK, NB], F32, "late")
        wtmp = inside("wtmp", [128, NB], F32, "late")
        rst2 = inside("rst2", [128, NB], F32, "late")
        e_cum = inside("e_cum", [128, NE], F32, "late")
        e_cnt = inside("e_cnt", [128, NE], F32, "late")
        e_int = inside("e_int", [128, NE], I32, "late")
        e_til = inside("e_til", [128, NE], F32, "late")
        e_end = inside("e_end", [128, NE], F32, "late")
        e_le = at("e_le", [1, SLOT_TILES, NE], F32, "edges", 0)
        tile_f = inside("tile_f", [1, SLOT_TILES], F32, "late")
        tile_e = inside("tile_e", [1, SLOT_TILES], I32, "late")
        scat_rec = at("scat_rec", [128, 2, 8, 4], F32, "work", 18432)
        ps = ctx.enter_context(nc.psum_tensor("ps", [128, 8, 512], F32))

        def bank(b, n=512, rows=128, first=0):
            return ps[0:rows, b, first:first + n]

        edges_in, x_in, mw1_in, bw_in = sem("edges_in"), sem("x_in"), sem("mw1_in"), sem("bw_in")
        wmix_in, small_in, upd_w_in, uw1_in = sem("wmix_in"), sem("small_in"), sem("upd_w_in"), sem("uw1_in")
        defaults_out, zeros_out, recs_in, b2row_in = sem("defaults_out"), sem("zeros_out"), sem("recs_in"), sem("b2row_in")
        consts, fills, ident_ok = sem("consts"), sem("fills"), sem("ident_ok")
        dve_step, act_step, pool_step = sem("dve_step"), sem("act_step"), sem("pool_step")
        wT_ps, wT_sb = sem("wT_ps"), sem("wT_sb")
        b2_ps, b2_hl, b2row_ok, ones2_ok, w2c_ok = sem("b2_ps"), sem("b2_hl"), sem("b2row_ok"), sem("ones2_ok"), sem("w2c_ok")
        rowcnt_ok, counts_ps, pos_ok, units_ok = sem("rowcnt_ok"), sem("counts_ps"), sem("pos_ok"), sem("units_ok")
        scattered = [sem(f"scattered{h}") for h in range(2)]
        var_ok, sd_ok, xn_ok, xnT_ps, xnT_sb = sem("var_ok"), sem("sd_ok"), sem("xn_ok"), sem("xnT_ps"), sem("xnT_sb")
        pads_ok, tab_ps, tab_sb, dst_sb = sem("pads_ok"), sem("tab_ps"), sem("tab_sb"), sem("dst_sb")
        dst_out = [sem(f"dst_out{i}") for i in range(2)]
        kv_ps, sq_sb, v_sb, ss_ok, kvsd_ok, kn_ok, dots_ps = (sem(n) for n in (
            "kv_ps", "sq_sb", "v_sb", "ss_ok", "kvsd_ok", "kn_ok", "dots_ps"))
        wkv_centered, diag_ok, mixP_ps, mixP_sb, mixG_ps, mixG_sb = (sem(n) for n in (
            "wkv_centered", "diag_ok", "mixP_ps", "mixP_sb", "mixG_ps", "mixG_sb"))
        row_in = [sem(f"row_in{k}") for k in range(TURN)]
        hot_ready, hotT_ps, hotT_sb, pre_ps, pre_sb, msg1_sb, msg1n_sb = (sem(n) for n in (
            "hot_ready", "hotT_ps", "hotT_sb", "pre_ps", "pre_sb", "msg1_sb", "msg1n_sb"))
        rstd_ok, newton_step = sem("rstd_ok"), sem("newton_step")
        msg1T_ps, msg1T_sb, msg2_ps, msg2_sb, sum_ps, sum_sb = (sem(n) for n in (
            "msg1T_ps", "msg1T_sb", "msg2_ps", "msg2_sb", "sum_ps", "sum_sb"))
        aggT_ps, aggT_sb, hid_ps, hid_sb, upd_ps, x2_ok = (sem(n) for n in (
            "aggT_ps", "aggT_sb", "hid_ps", "hid_sb", "upd_ps", "x2_ok"))
        var1_ok, sd1_ok, var2_ok, sd2_ok, xm_ok, xmT_ps, xmT_sb, logit_ps = (sem(n) for n in (
            "var1_ok", "sd1_ok", "var2_ok", "sd2_ok", "xm_ok", "xmT_ps", "xmT_sb", "logit_ps"))
        gap_ok, exp_ok, hotk_ok, route_ps, slots_ok, tile_ok, sent = (sem(n) for n in (
            "gap_ok", "exp_ok", "hotk_ok", "route_ps", "slots_ok", "tile_ok", "sent"))
        w1_in, w2_in = sem("w1_in"), sem("w2_in")
        slot_in = [sem(f"slot_in{k}") for k in range(4)]
        slot_out = [sem(f"slot_out{k}") for k in range(2)]
        sxT_ps, sxT_sb, sh_ps, sh_pre, sh_sb, shT_ps, shT_sb, sy_ps, sy_sb = (sem(n) for n in (
            "sxT_ps", "sxT_sb", "sh_ps", "sh_pre", "sh_sb", "shT_ps", "shT_sb", "sy_ps", "sy_sb"))
        pick_in = [sem(f"pick_in{k}") for k in range(4)]
        picked, final_ok, stored = sem("picked"), sem("final_ok"), sem("stored")

        N_CONST, N_FILL = 5, 2
        N_DST = [(NB + 1) // 2, NB // 2]
        SMALL = 9
        CH = [list(range(t, min(t + 4, NB))) for t in range(0, NB, 4)]
        LAST = UNITS + 8

        def here(m, count):
            return not isinstance(m, int) or 0 <= m < count

        def steps(engine, body, first, last, trips_lo, trips_hi, turn):
            for n in range(first, turn * trips_lo):
                body(n, n % turn)
            with engine.Fori(trips_lo, trips_hi) as i:
                for k in range(turn):
                    body(turn * i + k, k)
            for n in range(turn * trips_hi, last):
                body(n, n % turn)

        def after(engine, semaphore, count):
            if not isinstance(count, int) or count > 0:
                engine.wait_ge(semaphore, count)

        def registers(engine, table, first, count, largest):
            _, values = nc.values_load_multi_w_load_instructions(
                table[0:1, bass.ds(first, count)], engines=[engine], min_val=0, max_val=largest)
            return values

        def load_blocks(engine, blk, first, k):
            if k in (0, 4, 8) and here(first, UNITS):
                count = min(4, TURN - k)
                blk.update(zip(range(k, k + count), registers(engine, unit_blk, first, count, NB - 1)))

        def load_experts(engine, ex, n, k):
            if k == 0:
                for name, first in (("wide", n), ("late", n - 2)):
                    if isinstance(n, int):
                        low, high = max(first, 0), min(first + 4, SLOT_TILES)
                    else:
                        low, high = first, first + 4
                    if isinstance(n, int) and high <= low:
                        continue
                    count = high - low if isinstance(n, int) else 4
                    skip = low - first if isinstance(n, int) else 0
                    for j, v in enumerate(registers(engine, tile_e, low, count, NE - 1)):
                        ex[name, skip + j] = v

        block = ctx.enter_context(nc.Block())

        @block.sync
        def _(sp):
            sp.dma_start(src_i[0:NP, :], src.rearrange("(p c) -> p c", p=NP)).then_inc(edges_in, 16)
            sp.dma_start(dst_i[0:NP, :], dst.rearrange("(p c) -> p c", p=NP)).then_inc(edges_in, 16)
            sp.dma_start(d2_f[0:NP, :], edge_weight1.rearrange("(p c) a -> p (c a)", p=NP)).then_inc(edges_in, 16)
            sp.dma_start(wkv_nat[:], Wqkv[NQ:3 * NQ, :].rearrange("(q p) c -> p q c", p=128)).then_inc(wmix_in, 16)
            sp.dma_start(wout_nat[:], Wout.rearrange("(o p) f -> p o f", p=128)).then_inc(wmix_in, 16)
            sp.dma_start(wq_nat[:], Wqkv[0:NQ, :].rearrange("(q p) c -> p q c", p=128)).then_inc(wmix_in, 16)
            sp.dma_start(res[0:NP], x.rearrange("(p t) d -> p t d", p=NP)).then_inc(x_in, 16)
            for k in range(KD):
                sp.dma_start(mw1_sb[:, k], mW1[0:2 * D, :].rearrange("(a k p) n -> k p a n", a=2, p=128)[k])\
                  .then_inc(mw1_in, 16)
            sp.dma_start(bw[0:1, :], mb1.rearrange("(a n) -> a n", a=1)).then_inc(bw_in, 16)
            sp.dma_start(bw[1:2, :], mW1[2 * D:2 * D + 1, :]).then_inc(bw_in, 16)
            sp.dma_start(w2c_raw[:], mW2.rearrange("(k p) n -> p k n", p=128)).then_inc(small_in, 16)
            with nc.allow_non_contiguous_dma("vectors of 256 values, one value a partition"):
                for t, v in ((g_col, ln_g), (b_col, ln_b), (ub1_col, ub1), (gamma_col, gamma), (beta_col, beta)):
                    sp.dma_start(t[:], v.rearrange("(k p) -> p k", p=128)).then_inc(small_in, 16)
                sp.dma_start(mb2_row[:], mb2.rearrange("(a n) -> a n", a=1)).then_inc(small_in, 16)
                sp.dma_start(wr_sb[:], Wr.rearrange("(k p) e -> p k e", p=128)).then_inc(small_in, 16)
                sp.dma_start(br_bc[:], br.partition_broadcast(128)).then_inc(small_in, 16)
            sp.dma_start(bias_bc[:], ub2.partition_broadcast(128)).then_inc(upd_w_in, 16)
            sp.dma_start(bout_bc[:], bout.partition_broadcast(128)).then_inc(upd_w_in, 16)
            sp.dma_start(uw2_sb[:], uW2.rearrange("(k p) n -> p k n", p=128)).then_inc(upd_w_in, 16)
            sp.wait_ge(fills, N_FILL)
            reps = 10
            sp.dma_start(sorted_edges.rearrange("(p a b) f -> p a (b f)", p=128, a=reps),
                         defaults[:].rearrange("p b f -> p (b f)").unsqueeze(1)
                         .broadcast_to([128, reps, TILES // 10 * 4])).then_inc(defaults_out, 16)
            reps = SLOT_TILES * D // 2048
            sp.dma_start(expert_in.rearrange("(p s) d -> p (s d)", p=128).rearrange("p (a b) -> p a b", a=reps),
                         zero_rows[:].unsqueeze(1).broadcast_to([128, reps, 2048])).then_inc(zeros_out, 16)
            sp.wait_ge(b2_hl, 1)
            sp.dma_start(b2pair[1:2, :], b2lo[:]).then_inc(b2row_in, 16)
            for t in range(NB):
                sp.wait_ge(dst_sb, t + 1)
                sp.dma_start(dst_table.rearrange("(p t) d -> p t d", p=NP)[:, t, :], dst_stage[t % 2][0:NP, :])\
                  .then_inc(dst_out[t % 2], 16)
            sp.wait_ge(mixG_sb, KD)
            sp.dma_start(uw1_sb[:], uW1.rearrange("(k p) n -> p k n", p=128)).then_inc(uw1_in, 16)
            for h in range(2):
                sp.wait_ge(scattered[h], 16 * EC // 2)
            sp.dma_start(recs[:], sorted_edges.rearrange("(p t) f -> p t f", p=128)).then_inc(recs_in, 16)
            sp.wait_ge(pre_ps, UNITS)
            for e in range(NE):
                sp.dma_start(w1_sb[:, e], W1[e].rearrange("(k p) h -> p k h", p=128)).then_inc(w1_in, 16)
            sp.dma_start(b1_bc[:].rearrange("p e h -> p (e h)"),
                         b1.rearrange("e h -> (e h)").partition_broadcast(128)).then_inc(w1_in, 16)
            sp.wait_ge(x2_ok, NB)
            for e in range(NE):
                sp.dma_start(w2_sb[:, e], W2[e].rearrange("(k p) n -> p k n", p=128)).then_inc(w2_in, 16)
            sp.dma_start(b2_bc[:].rearrange("p e n -> p (e n)"),
                         b2.rearrange("e n -> (e n)").partition_broadcast(128)).then_inc(w2_in, 16)
            sp.wait_ge(sent, 16 * KT)

            def slots_step(n, k):
                after(sp, sxT_ps, n - 3)
                sp.dma_start(slot_x[k][:], expert_in[bass.ts(n, 128), :]).then_inc(slot_in[k], 16)

            steps(sp, slots_step, 0, SLOT_TILES, 1, SLOT_TILES // 4, 4)
            for g in range(5):
                sp.wait_ge(final_ok, 5 * (g + 1))
                sp.dma_start(out.rearrange("(p t) d -> p t d", p=NP)[:, 5 * g:5 * g + 5, :],
                             res[0:NP, 5 * g:5 * g + 5, :]).then_inc(stored, 16)
            sp.wait_ge(stored, 16 * 5)

        @block.gpsimd
        def _(pool):
            st = Steps(pool, pool_step)
            st.did(pool.iota(iota[:], [[1, 256]], channel_multiplier=0, allow_small_or_imprecise_dtypes=True))
            st.did(pool.memset(ident[:], 0.0))
            st.did(pool.memset(ones[:], 1.0))
            st.did(pool.memset(eps_col[:], EPS))
            st.did(pool.memset(defaults[:], 0.0))
            st.join()
            pool.affine_select(out=ident[:], in_=ident[:], compare_op=ALU.not_equal, fill=1.0, base=0,
                               pattern=[[-1, 128]], channel_multiplier=1).then_inc(consts, 1)
            pool.affine_select(out=earlier[:], in_=ones[:], compare_op=ALU.is_gt, fill=0.0, base=0,
                               pattern=[[1, 128]], channel_multiplier=-1).then_inc(consts, 1)
            st.did(pool.affine_select(out=bw_sel[:], in_=ones[0:2, :], compare_op=ALU.is_ge, fill=0.0, base=0,
                                      pattern=[[1, 128]], channel_multiplier=-NP))
            pool.memset(defaults[:, :, 1:2], -1.0).then_inc(fills, 1)
            pool.memset(zero_rows[:], 0.0).then_inc(fills, 1)
            st.join()
            pool.affine_select(out=bw_sel[:], in_=bw_sel[:], compare_op=ALU.is_ge, fill=0.0, base=NP - 1,
                               pattern=[[-1, 128]], channel_multiplier=NP).then_inc(consts, 1)
            pool.memset(ones2f[:], 1.0).then_inc(consts, 1)
            pool.memset(eps_col[:], EPS).then_inc(consts, 1)

            pool.wait_ge(pos_ok, 1)
            pool.wait_ge(defaults_out, 16)
            def carry_wait(k):
                st.did(pool.tensor_tensor(fence[:, k:k + 1], eps_col[0:1, :], eps_col[0:1, :], ALU.add))

            def scatter_group(i):
                for h in range(2):
                    after(pool, scattered[h], i * 128)
                    st.did(pool.tensor_copy(scat_idx[0:NP, h, :], pos_i[0:NP, bass.ds(16 * i + 8 * h, 8)]))
                    st.did(pool.tensor_copy(scat_rec[0:NP, h], rec_sb[0:NP, bass.ds(16 * i + 8 * h, 8), :]))
                    st.join()
                    carry_wait(h)
                    for c in range(8):
                        pool.indirect_dma_start(
                            out=sorted_edges, out_offset=bass.IndirectOffsetOnAxis(scat_idx[0:NP, h, c:c + 1], 0),
                            in_=scat_rec[0:NP, h, c, :], in_offset=None).then_inc(scattered[h], 16)

            scatter_group(0)
            with pool.Fori(1, EC // 16) as i:
                st.enter(i, 1, 6)
                scatter_group(i)
            st.leave(EC // 16 - 1)

            pool.wait_ge(recs_in, 16)
            pool.wait_ge(mixG_sb, KD)
            for i in range(2):
                pool.wait_ge(dst_out[i], 16 * N_DST[i])
            HALF = TURN // 2

            def edge_group(i):
                for k in range(TURN):
                    half = k // HALF
                    if k % HALF == 0:
                        for q in range(k, k + HALF):
                            after(pool, row_in[q], 32 * i)
                        st.did(pool.tensor_copy(stage_idx[:, half, :],
                                                recs[:, bass.ds(G * (TURN * i + k), TURN), 0]))
                        st.join()
                    after(pool, msg1n_sb, TURN * (i - 1) + k + 1)
                    carry_wait(k)
                    for j in range(G):
                        q = G * (k % HALF) + j
                        pool.indirect_dma_start(
                            out=msg1[:, k, j, :], out_offset=None, in_=dst_table,
                            in_offset=bass.IndirectOffsetOnAxis(stage_idx[:, half, q:q + 1], 0))\
                            .then_inc(row_in[k], 16)

            edge_group(0)
            with pool.Fori(1, UNITS // TURN) as i:
                st.enter(i, 1, 2 + TURN)
                edge_group(i)
            st.leave(UNITS // TURN - 1)

            pool.wait_ge(slots_ok, 1)
            pool.wait_ge(zeros_out, 16)
            for k in range(TOPK):
                for t in range(NB):
                    pool.indirect_dma_start(
                        out=expert_in, out_offset=bass.IndirectOffsetOnAxis(slot_i[0:NP, k, t:t + 1], 0),
                        in_=xm[0:NP, t, :], in_offset=None).then_inc(sent, 16)
            def slots_step(n, k):
                pool.wait_ge(sy_sb, n + 1)
                pool.dma_start(expert_out[bass.ts(n, 128), :], slot_y[k % 2][:]).then_inc(slot_out[k % 2], 16)

            steps(pool, slots_step, 0, SLOT_TILES, 1, SLOT_TILES // 4, 4)
            for i in range(2):
                pool.wait_ge(slot_out[i], 16 * SLOT_TILES // 2)
            for t in range(NB):
                if t >= 4:
                    pool.wait_ge(picked, t - 3)
                for k in range(TOPK):
                    pool.indirect_dma_start(
                        out=pick[t % 4][0:NP, k, :], out_offset=None, in_=expert_out,
                        in_offset=bass.IndirectOffsetOnAxis(slot_i[0:NP, k, t:t + 1], 0))\
                        .then_inc(pick_in[t % 4], 16)

        @block.tensor
        def _(pe):
            def turn(out_, in_, rows):
                return pe.transpose(out_, in_, ident[0:rows, 0:rows])

            pe.wait_ge(consts, N_CONST)
            pe.wait_ge(wmix_in, 48)
            for c in range(KD):
                for q in range(2 * QC):
                    m = turn(bank(4 - 2 * c + q // 4, 128, first=q % 4 * 128), wkv_nat[:, q, c * 128:c * 128 + 128], 128)
                m.then_inc(wT_ps, 1)
            for j in range(QC):
                for o in range(KD):
                    m = turn(bank(j // 2, 128, first=j % 2 * D + o * 128), wout_nat[:, o, j * 128:j * 128 + 128], 128)
            m.then_inc(wT_ps, 1)
            pe.wait_ge(small_in, 16 * SMALL)
            for k in range(KD):
                m = pe.matmul(bank(7, D, rows=1), b_col[:, k:k + 1], w2c_raw[:, k, :], start=(k == 0), stop=(k == KD - 1))
            m.then_inc(b2_ps, 1)
            pe.wait_ge(rowcnt_ok, 1)
            pe.matmul(bank(6, NB), earlier[0:NP, :], rowcnt[0:NP, :], start=True, stop=True)
            pe.matmul(bank(6, NB, first=32), ones[0:NP, :], rowcnt[0:NP, :], start=True, stop=True).then_inc(counts_ps, 1)

            pe.wait_ge(mw1_in, 32)
            pe.wait_ge(bw_in, 32)
            pe.wait_ge(wT_sb, KD + 1)
            pe.wait_ge(pads_ok, 1)

            def turn_xn(t):
                pe.wait_ge(xn_ok, t + 1)
                if t >= 2:
                    pe.wait_ge(xnT_sb, t - 1)
                for k in range(KD):
                    m = turn(bank(t % 2, NP, first=k * NP), xn[0:NP, t, k * 128:k * 128 + 128], NP)
                m.then_inc(xnT_ps, 1)

            def tables(t):
                pe.wait_ge(xnT_sb, t + 1)
                if t >= 2:
                    pe.wait_ge(tab_sb, t - 1)
                    pe.wait_ge(dst_sb, t - 1)
                for a in range(2):
                    o = bank(2 + 2 * a + t % 2, D)
                    for k in range(KD):
                        m = pe.matmul(o, xnT[:, t, k, :], mw1_sb[:, k, a, :], start=(k == 0),
                                      stop=(a == 1 and k == KD - 1))
                    if a == 0:
                        pe.matmul(o, bw_sel[:], bw[:], start=False, stop=True)
                m.then_inc(tab_ps, 1)

            turn_xn(0)
            for t in range(NB):
                if t + 1 < NB:
                    turn_xn(t + 1)
                tables(t)

            pe.wait_ge(wkv_centered, 1)
            pe.wait_ge(units_ok, 1)

            def dots(t):
                pe.wait_ge(kn_ok, t + 1)
                pe.wait_ge(v_sb, t + 1)
                for j in range(QC):
                    m = pe.matmul(bank(6, 128, first=128 * j), v_n[t % 2][0:NP, j * 128:j * 128 + 128],
                                  k_n[t % 2][0:NP, j * 128:j * 128 + 128], start=(t == 0 and j == 0), stop=(t == NB - 1),
                                  skip_group_check=True)
                m.then_inc(dots_ps, 1)

            for t in range(NB):
                b = 2 + 2 * (t % 2)
                if t == 0:
                    pe.wait_ge(tab_sb, NB)
                    pe.wait_ge(dst_sb, NB)
                if t >= 2:
                    pe.wait_ge(kn_ok, t - 1)
                    pe.wait_ge(sq_sb, t - 1)
                    pe.wait_ge(v_sb, t - 1)
                for h in range(2):
                    for k in range(KD):
                        m = pe.matmul(bank(b + h, NQ, rows=NP), xnT[:, t, k, 0:NP], wkvT[:, k, h * NQ:h * NQ + NQ],
                                      start=(k == 0), stop=(k == KD - 1))
                m.then_inc(kv_ps, 1)
                if t >= 1:
                    dots(t - 1)
            dots(NB - 1)
            pe.wait_ge(diag_ok, 1)
            for j in range(QC):
                m = pe.matmul(bank(j // 2, D, first=j % 2 * D), k_n[0][:, j * 128:j * 128 + 128], woutT[:, j, :],
                              start=True, stop=True)
            m.then_inc(mixP_ps, 1)
            pe.wait_ge(mixP_sb, 1)
            for c in range(KD):
                for j in range(QC):
                    m = pe.matmul(bank(2 + c, D), wq_nat[:, j, c * 128:c * 128 + 128], mixP[:, j, :],
                                  start=(j == 0), stop=(j == QC - 1))
                m.then_inc(mixG_ps, 1)

            pe.wait_ge(b2row_ok, 1)
            pe.wait_ge(ones2_ok, 1)
            pe.wait_ge(w2c_ok, 1)
            pe.wait_ge(mixG_sb, KD)
            pe.wait_ge(units_ok, 1)
            blk = {}

            def edge_step(n, k):
                load_blocks(mybir.EngineType.PE, blk, n, k)
                if here(n, UNITS):
                    after(pe, hotT_sb, n + 1)
                    after(pe, pre_sb, n - 1)
                    for j in range(G):
                        for first, table in ((True, src_hi), (False, src_lo)):
                            m = pe.matmul(bank(1 + k % 2, D, first=j * D), hotT[0:HR, k % 2, j * 128:j * 128 + 128],
                                          table[0:HR, bass.ts(blk[k], 1), :].rearrange("p a n -> p (a n)"),
                                          start=first, stop=not first)
                    m.then_inc(pre_ps, 1)
                m_ = n - 6
                if here(m_, UNITS):
                    pe.wait_ge(msg1n_sb, m_ + 1)
                    after(pe, msg1T_sb, m_ - 1)
                    for c in range(KD):
                        for j in range(G):
                            m = turn(bank(3 + k % 2, 128, first=c * UE + j * 128),
                                     msg1n[:, k % 2, j, c * 128:c * 128 + 128], 128)
                    m.then_inc(msg1T_ps, 1)
                m_ = n + 1
                if here(m_, UNITS):
                    pe.wait_ge(hot_ready, 2 * m_ + 2)
                    after(pe, hotT_sb, m_)
                    for j in range(G):
                        m = turn(bank(0, 128, rows=HR, first=j * 128), hot[:, (k + 1) % TURN, j, 0:HR], 128)
                    m.then_inc(hotT_ps, 1)
                m_ = n - 7
                if here(m_, UNITS):
                    pe.wait_ge(msg2_sb, m_ + 1)
                    after(pe, sum_sb, m_)
                    for j in range(G):
                        m = pe.matmul(bank(7, D, rows=NP), hot[:, (k - 7) % TURN, j, 0:NP], msg2[:, (k + 1) % 2, j, :],
                                      start=(j == 0), stop=(j == G - 1))
                    m.then_inc(sum_ps, 1)
                m_ = n - 6
                if here(m_, UNITS):
                    pe.wait_ge(msg1T_sb, m_ + 1)
                    after(pe, msg2_sb, m_ - 1)
                    for j in range(G):
                        o = bank(5 + k % 2, D, first=j * D)
                        pe.matmul(o, ones2[:], b2row[:], start=True, stop=False)
                        for c in range(KD):
                            m = pe.matmul(o, msg1T[:, k % 2, c, j * 128:j * 128 + 128], w2c[:, c, :],
                                          start=False, stop=(c == KD - 1))
                    m.then_inc(msg2_ps, 1)

            steps(pe, edge_step, -2, LAST, 1, UNITS // TURN - 1, TURN)

            pe.wait_ge(uw1_in, 16)
            pe.wait_ge(upd_w_in, 48)
            pe.wait_ge(sum_sb, UNITS)
            done = 0
            for c, blocks in enumerate(CH):
                nb = len(blocks)
                t0 = blocks[0]

                if c >= 1:
                    pe.wait_ge(aggT_sb, c)
                for k in range(KD):
                    for i, t in enumerate(blocks):
                        m = turn(bank(k, NP, first=i * NP), agg[0:NP, t, k * 128:k * 128 + 128], NP)
                m.then_inc(aggT_ps, 1)
                pe.wait_ge(aggT_sb, c + 1)
                if c >= 1:
                    pe.wait_ge(hid_sb, c)
                for f in range(KD):
                    o = bank(2 + f, nb * NP)
                    for k in range(KD):
                        pe.matmul(o, uw1_sb[:, k, f * 128:f * 128 + 128], xnT[:, t0:t0 + nb, k, 0:NP],
                                  start=(k == 0), stop=False)
                    for k in range(KD):
                        m = pe.matmul(o, uw1_sb[:, KD + k, f * 128:f * 128 + 128], aggT[c % 2][:, k, 0:nb, :],
                                      start=False, stop=(k == KD - 1))
                m.then_inc(hid_ps, 1)
                pe.wait_ge(hid_sb, c + 1)
                for i, t in enumerate(blocks):
                    if t >= 4:
                        pe.wait_ge(x2_ok, t - 3)
                    o = bank(4 + t % 4, D, rows=NP)
                    for f in range(KD):
                        pe.matmul(o, hidT[c % 2][:, f, i, :], uw2_sb[:, f, :], start=(f == 0), stop=False)
                    for k in range(KD):
                        m = pe.matmul(o, xnT[:, t, k, 0:NP], mixG[:, k, :], start=False, stop=(k == KD - 1))
                    m.then_inc(upd_ps, 1)

            pe.wait_ge(x2_ok, NB)

            def turn_xm(t):
                pe.wait_ge(xm_ok, t + 1)
                if t >= 2:
                    pe.wait_ge(xmT_sb, t - 1)
                for k in range(KD):
                    m = turn(bank(t % 2, NP, first=k * NP), xm[0:NP, t, k * 128:k * 128 + 128], NP)
                m.then_inc(xmT_ps, 1)

            turn_xm(0)
            for t in range(NB):
                if t + 1 < NB:
                    turn_xm(t + 1)
                pe.wait_ge(xmT_sb, t + 1)
                for k in range(KD):
                    m = pe.matmul(bank(2, NE, rows=NP, first=t * NE), xmT[t % 2][:, k, :], wr_sb[:, k, :],
                                  start=(k == 0), stop=(k == KD - 1))
                m.then_inc(logit_ps, 1)
            pe.wait_ge(hotk_ok, 1)
            flat = hot_k[0:NP].rearrange("p e m -> p (e m)")
            pe.matmul(bank(3, NE * KT, rows=NP), earlier[0:NP, 0:NP], flat, start=True, stop=True)
            pe.matmul(bank(4, NE * KT, rows=NP), ones[0:NP, 0:NP], flat, start=True, stop=True).then_inc(route_ps, 1)

            pe.wait_ge(w1_in, 16 * (NE + 1))
            pe.wait_ge(w2_in, 16 * (NE + 1))
            pe.wait_ge(slots_ok, 1)
            pe.wait_ge(tile_ok, 1)

            ex = {}

            def slots_step(n, k):
                load_experts(mybir.EngineType.PE, ex, n, k)
                m_ = n
                if here(m_, SLOT_TILES):
                    pe.wait_ge(sxT_sb, m_ + 1)
                    after(pe, sh_pre, m_ - 1)
                    for c in range(KD):
                        m = pe.matmul(bank(1 + k % 2, HID), slot_xT[k % 2][:, c, :],
                                      w1_sb[:, bass.ts(ex["wide", k], 1), c, :].rearrange("p a n -> p (a n)"),
                                      start=(c == 0), stop=(c == KD - 1))
                    m.then_inc(sh_ps, 1)
                m_ = n + 1
                if here(m_, SLOT_TILES):
                    pe.wait_ge(slot_in[(k + 1) % 4], 16 * ((m_ - (k + 1) % 4) // 4) + 16 if isinstance(m_, int)
                               else (m_ - (k + 1) % 4) * 4 + 16)
                    after(pe, sxT_sb, m_)
                    for c in range(KD):
                        m = turn(bank(0, 128, first=c * 128), slot_x[(k + 1) % 4][:, c * 128:c * 128 + 128], 128)
                    m.then_inc(sxT_ps, 1)
                m_ = n - 1
                if here(m_, SLOT_TILES):
                    pe.wait_ge(sh_sb, m_ + 1)
                    after(pe, shT_sb, m_ - 1)
                    for c in range(HC):
                        m = turn(bank(3 + (k + 1) % 2, 128, first=c * 128),
                                 slot_h[(k + 1) % 2][:, c * 128:c * 128 + 128], 128)
                    m.then_inc(shT_ps, 1)
                m_ = n - 2
                if here(m_, SLOT_TILES):
                    pe.wait_ge(shT_sb, m_ + 1)
                    after(pe, sy_sb, m_ - 1)
                    for c in range(HC):
                        m = pe.matmul(bank(5 + k % 2, D), slot_hT[k % 2][:, c, :],
                                      w2_sb[:, bass.ts(ex["late", k], 1), c, :].rearrange("p a n -> p (a n)"),
                                      start=(c == 0), stop=(c == HC - 1))
                    m.then_inc(sy_ps, 1)

            steps(pe, slots_step, -1, SLOT_TILES + 2, 1, SLOT_TILES // 4 - 1, 4)

        def stage_dst(act, t):
            act.wait_ge(tab_ps, t + 1)
            if t >= 2:
                act.wait_ge(dst_out[t % 2], 16 * (t // 2))
            act.activation(dst_stage[t % 2][0:NP, :], bank(4 + t % 2, D, rows=NP), ACT.Copy).then_inc(dst_sb, 1)

        @block.scalar
        def _(act):
            A = act.activation
            act.wait_ge(wT_ps, 1)
            A(wkvT[:, 0, :], ps[:, 4:6, :].rearrange("p a n -> p (a n)"), ACT.Copy).then_inc(wT_sb, 1)
            act.wait_ge(wT_ps, 2)
            A(wkvT[:, 1, :], ps[:, 2:4, :].rearrange("p a n -> p (a n)"), ACT.Copy).then_inc(wT_sb, 1)
            act.wait_ge(wT_ps, 3)
            A(woutT[:].rearrange("p j n -> p (j n)"), ps[:, 0:2, :].rearrange("p a n -> p (a n)"), ACT.Copy)\
                .then_inc(wT_sb, 1)
            act.wait_ge(consts, N_CONST)
            act.wait_ge(var_ok, 1)
            A(rstd[0:NP], meanvar[0:NP, :, 1], ACT.Sqrt, bias=eps_col[0:NP, :]).then_inc(sd_ok, 1)
            for t in range(NB):
                act.wait_ge(xnT_ps, t + 1)
                A(xnT[:, t, :, 0:NP], bank(t % 2, KD * NP).rearrange("p (k n) -> p k n", k=KD), ACT.Copy)\
                    .then_inc(xnT_sb, 1)
                if t >= 1:
                    stage_dst(act, t - 1)
            stage_dst(act, NB - 1)
            for t in range(NB):
                b = 2 + 2 * (t % 2)
                act.wait_ge(kv_ps, t + 1)
                if t >= 1:
                    act.wait_ge(ss_ok, t)
                A(kv_sq[0:NP, :], ps[0:NP, b:b + 2, :].rearrange("p a n -> p (a n)"), ACT.Square).then_inc(sq_sb, 1)
                if t >= 2:
                    act.wait_ge(dots_ps, t - 1)
                A(v_n[t % 2][0:NP, :], ps[0:NP, b + 1, :], ACT.Copy).then_inc(v_sb, 1)
                act.wait_ge(ss_ok, t + 1)
                A(kv_ss[0:NP, :], kv_ss[0:NP, :], ACT.Sqrt, bias=eps_col[0:NP, :], scale=1.0 / HD).then_inc(kvsd_ok, 1)
            act.wait_ge(mixP_ps, 1)
            act.wait_ge(b2row_in, 16)
            act.wait_ge(ones2_ok, 1)
            A(mixP[:].rearrange("p j n -> p (j n)"), ps[:, 0:2, :].rearrange("p a n -> p (a n)"), ACT.Copy)\
                .then_inc(mixP_sb, 1)
            for h in range(2):
                act.wait_ge(scattered[h], 16 * EC // 2)
            for c in range(KD):
                act.wait_ge(mixG_ps, c + 1)
                A(mixG[:, c, :], bank(2 + c, D), ACT.Copy, scale=1.0 / N).then_inc(mixG_sb, 1)

            def edge_step(n, k):
                m_ = n - 7
                if here(m_, UNITS):
                    act.wait_ge(msg2_ps, m_ + 1)
                    after(act, sum_ps, m_ - 1)
                    A(msg2[:, (k + 1) % 2].rearrange("p j n -> p (j n)"), bank(5 + (k + 1) % 2), ACT.Silu)\
                        .then_inc(msg2_sb, 1)
                m_ = n - 6
                if here(m_, UNITS):
                    act.wait_ge(msg1T_ps, m_ + 1)
                    after(act, msg2_ps, m_ - 1)
                    A(msg1T[:, k % 2].rearrange("p c n -> p (c n)"), bank(3 + k % 2), ACT.Copy)\
                        .then_inc(msg1T_sb, 1)
                m_ = n + 1
                if here(m_, UNITS):
                    act.wait_ge(hotT_ps, m_ + 1)
                    after(act, pre_ps, m_ - 1)
                    A(hotT[0:HR, (k + 1) % 2, :], bank(0, UE, rows=HR), ACT.Copy).then_inc(hotT_sb, 1)
                m_ = n - 5
                kk = (k - 5) % TURN
                if here(m_, UNITS):
                    act.wait_ge(rstd_ok, m_ // 2 + 1 if isinstance(m_, int) else pairs + (k - 5) // 2 + 1)
                    after(act, msg1T_ps, m_ - 1)
                    for j in range(G):
                        m = A(msg1n[:, (k + 1) % 2, j, :], msg1[:, kk, j, :], ACT.Identity,
                              bias=nw_b[:, kk, j:j + 1], scale=nw_y[:, kk, j:j + 1])
                    m.then_inc(msg1n_sb, 1)
                if here(n, UNITS):
                    act.wait_ge(pre_sb, n + 1)
                    v = msg1[:, k].rearrange("p j n -> p (j n)")
                    A(v, v, ACT.Silu).then_inc(msg1_sb, 1)

            pairs = 0
            for n in range(-2, TURN):
                edge_step(n, n % TURN)
            with act.Fori(1, UNITS // TURN - 1) as i:
                pairs = TURN // 2 * i
                for k in range(TURN):
                    edge_step(TURN * i + k, k)
            for n in range(UNITS - TURN, LAST):
                edge_step(n, n % TURN)


            act.wait_ge(small_in, 16 * SMALL)
            for c, blocks in enumerate(CH):
                nb = len(blocks)
                act.wait_ge(aggT_ps, c + 1)
                if c >= 2:
                    act.wait_ge(hid_ps, c - 1)
                A(aggT[c % 2][:, :, 0:nb, :].rearrange("p k i n -> p k (i n)"), ps[:, 0:2, 0:nb * NP], ACT.Copy)\
                    .then_inc(aggT_sb, 1)
                act.wait_ge(hid_ps, c + 1)
                if c >= 2:
                    act.wait_ge(upd_ps, 4 * (c - 1))
                for f in range(KD):
                    m = A(hidT[c % 2][:, f, 0:nb, :].rearrange("p i n -> p (i n)"), bank(2 + f, nb * NP), ACT.Silu,
                          bias=ub1_col[:, f:f + 1])
                m.then_inc(hid_sb, 1)
            act.wait_ge(var1_ok, 1)
            A(rstd[0:NP], meanvar[0:NP, :, 1], ACT.Sqrt, bias=eps_col[0:NP, :]).then_inc(sd1_ok, 1)
            act.wait_ge(var2_ok, 1)
            A(rst2[0:NP], rst2[0:NP], ACT.Sqrt, bias=eps_col[0:NP, :]).then_inc(sd2_ok, 1)
            for t in range(NB):
                act.wait_ge(xmT_ps, t + 1)
                if t >= 2:
                    act.wait_ge(logit_ps, t - 1)
                for k in range(KD):
                    m = A(xmT[t % 2][:, k, :], bank(t % 2, NP, first=k * NP), ACT.Identity,
                          bias=beta_col[:, k:k + 1], scale=gamma_col[:, k:k + 1])
                m.then_inc(xmT_sb, 1)
            act.wait_ge(gap_ok, 1)
            A(wtmp[0:NP], wtmp[0:NP], ACT.Exp).then_inc(exp_ok, 1)

            def slots_step(n, k):
                m_ = n + 1
                if here(m_, SLOT_TILES):
                    act.wait_ge(sxT_ps, m_ + 1)
                    after(act, sh_ps, m_ - 1)
                    for c in range(KD):
                        m = A(slot_xT[(k + 1) % 2][:, c, :], bank(0, 128, first=c * 128), ACT.Identity,
                              bias=beta_col[:, c:c + 1], scale=gamma_col[:, c:c + 1])
                    m.then_inc(sxT_sb, 1)
                if here(n, SLOT_TILES):
                    act.wait_ge(sh_pre, n + 1)
                    A(slot_h[k % 2][:], slot_h[k % 2][:], ACT.Gelu).then_inc(sh_sb, 1)

            steps(act, slots_step, -1, SLOT_TILES, 1, SLOT_TILES // 4 - 1, 4)

        @block.vector
        def _(dve):
            st = Steps(dve, dve_step)

            def step(ins):
                st.did(ins)
                st.join()

            R = slice(0, NP)
            dve.wait_ge(edges_in, 48)
            dve.wait_ge(consts, N_CONST)
            step(dve.tensor_copy(rank_f[R], src_i[R]))
            step(dve.tensor_scalar(row_f[R], rank_f[R], 1.0 / NB, 0.5 / NB - 0.5, ALU.mult, ALU.add))
            step(dve.tensor_scalar(row_f[R], row_f[R], ROUND, None, ALU.add))
            step(dve.tensor_scalar(row_f[R], row_f[R], -ROUND, None, ALU.add))
            step(dve.scalar_tensor_tensor(blk_f[R], row_f[R], -float(NB), rank_f[R], ALU.mult, ALU.add))
            step(dve.tensor_tensor(onehot[R], blk_f[R].unsqueeze(1).broadcast_to([NP, NB, EC]),
                                   iota[R, 0:NB].unsqueeze(2).broadcast_to([NP, NB, EC]), ALU.is_equal))
            flat = onehot[R].rearrange("p b c -> p (b c)")
            step(dve.tensor_tensor_scan(scanned[R], flat, flat, 0.0, ALU.add, ALU.bypass))
            last = scanned[R].rearrange("p (b c) -> p b c", b=NB)[:, :, EC - 1]
            step(dve.tensor_copy(cum[R], last))
            step(dve.tensor_copy(rowcnt[R, 0:1], cum[R, 0:1]))
            st.did(dve.tensor_tensor(rowcnt[R, 1:NB], cum[R, 1:NB], cum[R, 0:NB - 1], ALU.subtract))
            st.join()
            step(dve.tensor_tensor(cum[R], cum[R], rowcnt[R], ALU.subtract))
            dve.tensor_copy(stats[R, 0, 0:1], cum[R, 0:1]).then_inc(rowcnt_ok, 1)
            step(dve.tensor_copy(rec_sb[R, :, 0], dst_i[R]))
            step(dve.tensor_copy(rec_sb[R, :, 1], row_f[R]))
            step(dve.tensor_copy(d2_r[R], d2_f[R]))
            step(dve.tensor_copy(rec_sb[R, :, 2], d2_r[R].bitcast(F32)))
            step(dve.tensor_tensor(rec_sb[R, :, 3], d2_f[R], d2_r[R].bitcast(F32), ALU.subtract))
            dve.wait_ge(counts_ps, 1)
            step(dve.tensor_copy(prefix[:], bank(6, NB)))
            step(dve.tensor_scalar(ends[:], bank(6, NB, first=32), float(UE - 1), None, ALU.add))
            step(dve.tensor_copy(ints[:], ends[:]))
            step(dve.tensor_scalar(ints[:], ints[:], 8, None, ALU.logical_shift_right))
            step(dve.tensor_copy(nunits[:], ints[:]))
            step(dve.tensor_tensor_scan(ends[:], nunits[:], nunits[:], 0.0, ALU.add, ALU.bypass))
            step(dve.tensor_tensor(nunits[:], ends[:], nunits[:], ALU.subtract))
            step(dve.scalar_tensor_tensor(prefix[:], nunits[:], float(UE), prefix[:], ALU.mult, ALU.add))
            step(dve.scalar_tensor_tensor(prefix[R], prefix[R], -1.0, cum[R], ALU.add, ALU.subtract))
            for b in range(NB):
                st.did(dve.scalar_tensor_tensor(masked[R, b, :], scanned[R, b * EC:b * EC + EC], prefix[R, b:b + 1],
                                                onehot[R, b, :], ALU.add, ALU.mult))
            st.join()
            step(dve.tensor_reduce(rank_f[R], masked[R].rearrange("p b c -> p c b"), AX.X, ALU.add))
            step(dve.tensor_copy(pos_i[R], rank_f[R]))
            step(dve.tensor_scalar(low_i[R], pos_i[R], 127, None, ALU.bitwise_and))
            step(dve.tensor_scalar(top_i[R], pos_i[R], 7, None, ALU.logical_shift_right))
            step(dve.tensor_copy(rank_f[R], low_i[R]))
            step(dve.tensor_copy(blk_f[R], top_i[R]))
            step(dve.scalar_tensor_tensor(rank_f[R], rank_f[R], float(TILES), blk_f[R], ALU.mult, ALU.add))
            dve.tensor_copy(pos_i[R], rank_f[R]).then_inc(pos_ok, 1)
            step(dve.tensor_tensor(unit_le[:], ends[0:1].unsqueeze(1).broadcast_to([1, UNITS, NB]),
                                   iota[0:1, 0:UNITS].unsqueeze(2).broadcast_to([1, UNITS, NB]), ALU.is_le))
            step(dve.tensor_reduce(unit_f[:], unit_le[:], AX.X, ALU.add))
            step(dve.tensor_scalar(unit_f[:], unit_f[:], float(NB - 1), None, ALU.min))
            step(dve.tensor_copy(unit_blk[:], unit_f[:]))
            step(dve.tensor_copy(unit_f[:], unit_blk[:]))
            dve.memset(nw_t[:], 1.0).then_inc(units_ok, 1)

            dve.wait_ge(small_in, 16 * SMALL)
            for k in range(KD):
                st.did(dve.tensor_scalar(w2c[:, k, :], w2c_raw[:, k, :], g_col[:, k:k + 1], None, ALU.mult))
            dve.wait_ge(b2_ps, 1)
            step(dve.tensor_tensor(b2tmp[:], bank(7, D, rows=1), mb2_row[:], ALU.add))
            step(dve.tensor_copy(b2row[0:1, :], b2tmp[:]))
            step(dve.tensor_copy(b2pair[0:1, :], b2row[0:1, :].bitcast(F32)))
            dve.tensor_tensor(b2lo[:], b2tmp[:], b2pair[0:1, :], ALU.subtract).then_inc(b2_hl, 1)
            dve.tensor_copy(ones2[:], ones2f[:]).then_inc(ones2_ok, 1)
            st.join()
            dve.memset(nw_t[:], 0.0).then_inc(w2c_ok, 1)
            step(dve.memset(xnT[:, :, :, NP:128], 0.0))
            dve.memset(nw_t[:], 0.0).then_inc(pads_ok, 1)

            dve.wait_ge(x_in, 16)

            def block_stats(t):
                step(dve.bn_stats(stats[R, t, :], res[R, t, :]))
                st.did(dve.bn_aggr(meanvar[R, t, :], stats[R, t, :]))

            for t in range(NB):
                st.did(dve.bn_stats(stats[R, t, :], res[R, t, :]))
            st.join()
            for t in range(NB):
                st.did(dve.bn_aggr(meanvar[R, t, :], stats[R, t, :]))
            st.join()
            dve.tensor_copy(nw_t[R, 0, 0:1], meanvar[R, 0, 0:1]).then_inc(var_ok, 1)
            dve.wait_ge(sd_ok, 1)
            step(dve.reciprocal(rstd[R], rstd[R]))
            dve.wait_ge(defaults_out, 16)
            for t in range(NB):
                dve.tensor_scalar(xn[R, t, :], res[R, t, :], meanvar[R, t, 0:1], rstd[R, t:t + 1],
                                  ALU.subtract, ALU.mult).then_inc(xn_ok, 1)
            dve.wait_ge(zeros_out, 16)
            for t in range(NB):
                dve.wait_ge(tab_ps, t + 1)
                step(dve.tensor_copy(src_hi[:, t, :], bank(2 + t % 2, D)))
                dve.tensor_tensor(src_lo[:, t, :], bank(2 + t % 2, D), src_hi[:, t, :].bitcast(F32), ALU.subtract)\
                   .then_inc(tab_sb, 1)
            dve.wait_ge(wT_sb, KD + 1)
            heads = wkvT[:].rearrange("p k (h d) -> p (k h) d", d=HD)
            step(dve.tensor_reduce(wmean[:], heads, AX.X, ALU.add))
            step(dve.tensor_scalar(wmean[:], wmean[:], 1.0 / HD, None, ALU.mult))
            dve.tensor_tensor(heads, heads, wmean[:].unsqueeze(2).broadcast_to([128, KD * 2 * HEADS, HD]),
                              ALU.subtract).then_inc(wkv_centered, 1)
            dve.wait_ge(b2row_in, 16)
            dve.tensor_copy(b2row[:], b2pair[:]).then_inc(b2row_ok, 1)
            dve.wait_ge(upd_w_in, 48)
            step(dve.tensor_tensor(bias_bc[:], bias_bc[:], bout_bc[:], ALU.add))
            for t in range(NB):
                b = 2 + 2 * (t % 2)
                dve.wait_ge(sq_sb, t + 1)
                if t >= 1:
                    dve.wait_ge(kn_ok, t)
                dve.tensor_reduce(kv_ss[R], kv_sq[R].rearrange("p (h d) -> p h d", d=HD), AX.X, ALU.add)\
                   .then_inc(ss_ok, 1)
                st.did(dve.tensor_tensor(res[R, t, :], res[R, t, :], bias_bc[R, :], ALU.add))
                dve.wait_ge(kvsd_ok, t + 1)
                step(dve.tensor_tensor(kv_rs[R], kv_ss[R, 0:HEADS], kv_ss[R, HEADS:2 * HEADS], ALU.mult))
                step(dve.reciprocal(kv_rs[R], kv_rs[R]))
                if t >= 2:
                    dve.wait_ge(dots_ps, t - 1)
                dve.tensor_tensor(k_n[t % 2][R].rearrange("p (h d) -> p h d", d=HD),
                                  ps[R, b, :].rearrange("p (h d) -> p h d", d=HD),
                                  kv_rs[R].unsqueeze(2).broadcast_to([NP, HEADS, HD]), ALU.mult).then_inc(kn_ok, 1)
                st.did(dve.tensor_tensor(res[R, t, :], res[R, t, :], xn[R, t, :], ALU.add))
            dve.wait_ge(dots_ps, NB)
            step(dve.memset(k_n[0][:], 0.0))
            pair = lambda ap: ap.rearrange("p (j d) -> p j d", d=128)
            st.did(dve.tensor_copy(pair(k_n[0][0:HD, :])[:, :, 0:HD], pair(bank(6, rows=HD))[:, :, 0:HD]))
            st.did(dve.tensor_copy(pair(k_n[0][HD:128, :])[:, :, HD:128], pair(ps[HD:128, 6, :])[:, :, HD:128]))
            st.join()
            dve.memset(agg[:], 0.0).then_inc(diag_ok, 1)
            dve.wait_ge(diag_ok, 1)

            blk = {}
            nw = Steps(dve, newton_step)

            def rstd_step(q, s, pair_exists):
                if not pair_exists:
                    return
                nw.join()
                y = (nw_i[:].bitcast(F32), nw_1[:], nw_2[:], nw_y[:, s:s + 2, :])
                r, part = divmod(q - 3, 3)
                if q == 0:
                    m = dve.tensor_scalar(nw_v[:], emv[:, s:s + 2, :, 1], EPS, None, ALU.add)
                elif q == 1:
                    m = dve.tensor_scalar(nw_i[:], nw_v[:].bitcast(I32), 1, None, ALU.logical_shift_right)
                elif q == 2:
                    m = dve.tensor_scalar(nw_i[:], nw_i[:], -1.0, float(RSQRT_MAGIC), ALU.mult, ALU.add)
                elif q == 12:
                    m = dve.scalar_tensor_tensor(nw_b[:, s:s + 2, :], emv[:, s:s + 2, :, 0], -1.0, y[3],
                                                 ALU.mult, ALU.mult)
                    m.then_inc(rstd_ok, 1)
                    return
                elif part == 0:
                    m = dve.tensor_tensor(nw_s[:], y[r], y[r], ALU.mult)
                elif part == 1:
                    m = dve.scalar_tensor_tensor(nw_s[:], nw_s[:], -0.5, nw_v[:], ALU.mult, ALU.mult)
                else:
                    m = dve.scalar_tensor_tensor(y[r + 1], nw_s[:], 1.5, y[r], ALU.add, ALU.mult)
                nw.did(m)

            def edge_step(n, k, turn_rows):
                behind = 3 if k % 2 else 4
                first_q = 1 if k % 2 else 7
                pair_on = here(n - behind, UNITS)
                slot = (k - behind) % TURN
                load_blocks(mybir.EngineType.DVE, blk, n - 8, k)
                m_ = n - 8
                if here(m_, UNITS):
                    dve.wait_ge(sum_ps, m_ + 1)
                    after(dve, sum_sb, m_)
                    a = agg[0:NP, bass.ts(blk[k], 1), :].rearrange("p a n -> p (a n)")
                    dve.tensor_tensor(a, a, bank(7, D, rows=NP), ALU.add).then_inc(sum_sb, 1)
                rstd_step(first_q, slot, pair_on)
                m_ = n + 2
                kk = (k + 2) % TURN
                if here(m_, UNITS):
                    after(dve, sum_ps, m_ - TURN + 1)
                    r = recs[:, bass.ds(G * m_, G), :]
                    dve.tensor_tensor(hot[:, kk, :, 0:NP], iota[:, 0:NP].unsqueeze(1).broadcast_to([128, G, NP]),
                                      r[:, :, 1:2].broadcast_to([128, G, NP]), ALU.is_equal).then_inc(hot_ready, 1)
                    dve.tensor_copy(hot[:, kk, :, NP:HR], r[:, :, 2:4]).then_inc(hot_ready, 1)
                rstd_step(first_q + 1, slot, pair_on)
                if here(n, UNITS):
                    dve.wait_ge(pre_ps, n + 1)
                    dve.wait_ge(row_in[k], turn_rows)
                    v = msg1[:, k].rearrange("p j n -> p (j n)")
                    dve.tensor_tensor(v, bank(1 + k % 2), v, ALU.add).then_inc(pre_sb, 1)
                rstd_step(first_q + 2, slot, pair_on)
                m_ = n - 1
                kk = (k - 1) % TURN
                if here(m_, UNITS):
                    dve.wait_ge(msg1_sb, m_ + 1)
                    st.did(dve.bn_stats(est[:, kk, 0, :], msg1[:, kk, 0, :]))
                rstd_step(first_q + 3, slot, pair_on)
                if here(m_, UNITS):
                    st.did(dve.bn_stats(est[:, kk, 1, :], msg1[:, kk, 1, :]))
                rstd_step(first_q + 4, slot, pair_on)
                if here(m_, UNITS):
                    st.join()
                rstd_step(first_q + 5, slot, pair_on)
                if here(m_, UNITS):
                    for j in range(G):
                        st.did(dve.bn_aggr(emv[:, kk, j, :], est[:, kk, j, :]))
                    if k % 2 == 0:
                        st.join()
                        rstd_step(0, (k - 2) % TURN, True)

            dve.wait_ge(recs_in, 16)
            for n in range(-2, TURN):
                edge_step(n, n % TURN, 32)
            with dve.Fori(1, UNITS // TURN - 1) as i:
                st.enter(i, 1, TURN * 2 * G)
                nw.enter(i, 1, TURN // 2 * 12)
                for k in range(TURN):
                    edge_step(TURN * i + k, k, 32 * i + 32)
            st.leave(UNITS // TURN - 2)
            nw.leave(UNITS // TURN - 2)
            for n in range(UNITS - TURN, LAST):
                edge_step(n, n % TURN, 32 * (n // TURN) + 32)

            for t in range(NB):
                dve.wait_ge(upd_ps, t + 1)
                dve.tensor_tensor(res[R, t, :], res[R, t, :], bank(4 + t % 4, D, rows=NP), ALU.add).then_inc(x2_ok, 1)
                if t >= 1:
                    dve.wait_ge(x2_ok, t)
                    st.did(dve.bn_stats(stats[R, t - 1, :], res[R, t - 1, :]))
            dve.wait_ge(x2_ok, NB)
            step(dve.bn_stats(stats[R, NB - 1, :], res[R, NB - 1, :]))
            for t in range(NB):
                st.did(dve.bn_aggr(meanvar[R, t, :], stats[R, t, :]))
            st.join()
            dve.tensor_copy(nw_t[R, 0, 0:1], meanvar[R, 0, 0:1]).then_inc(var1_ok, 1)
            dve.wait_ge(sd1_ok, 1)
            step(dve.reciprocal(rstd[R], rstd[R]))
            step(dve.tensor_tensor(rst2[R], rstd[R], rstd[R], ALU.mult))
            dve.tensor_tensor(rst2[R], rst2[R], meanvar[R, :, 1], ALU.mult).then_inc(var2_ok, 1)
            dve.wait_ge(sd2_ok, 1)
            step(dve.reciprocal(rst2[R], rst2[R]))
            step(dve.tensor_tensor(rstd[R], rstd[R], rst2[R], ALU.mult))
            for t in range(NB):
                dve.tensor_scalar(xm[R, t, :], res[R, t, :], meanvar[R, t, 0:1], rstd[R, t:t + 1],
                                  ALU.subtract, ALU.mult).then_inc(xm_ok, 1)
            dve.wait_ge(logit_ps, NB)
            step(dve.tensor_tensor(logits[R], bank(2, NB * NE, rows=NP).rearrange("p (t e) -> p t e", e=NE),
                                   br_bc[R].unsqueeze(1).broadcast_to([NP, NB, NE]), ALU.add))
            for t in range(NB):
                st.did(dve.max(top_v[R, t, :], logits[R, t, :]))
            st.join()
            for t in range(NB):
                st.did(dve.max_index(top_e[R, t, :], top_v[R, t, :], logits[R, t, :]))
            st.join()
            dve.tensor_tensor(wtmp[R], top_v[R, :, 1], top_v[R, :, 0], ALU.subtract).then_inc(gap_ok, 1)
            for k in range(TOPK):
                st.did(dve.tensor_copy(top_f[R, k, :], top_e[R, :, k]))
            st.join()
            step(dve.tensor_tensor(hot_k[R], top_f[R].rearrange("p k t -> p (k t)").unsqueeze(1).broadcast_to([NP, NE, KT]),
                                   iota[R, 0:NE].unsqueeze(2).broadcast_to([NP, NE, KT]), ALU.is_equal))
            dve.tensor_copy(nw_t[R, 0, 0:1], hot_k[R, 0, 0:1]).then_inc(hotk_ok, 1)
            dve.wait_ge(exp_ok, 1)
            step(dve.tensor_scalar(wgt[R, 0, :], wtmp[R], 1.0, None, ALU.add))
            step(dve.reciprocal(wgt[R, 0, :], wgt[R, 0, :]))
            step(dve.tensor_tensor(wgt[R, 1, :], wgt[R, 0, :], wtmp[R], ALU.mult))
            dve.wait_ge(route_ps, 1)
            hc = hot_c[R].rearrange("p e m -> p (e m)")
            step(dve.tensor_copy(hc, bank(4, NE * KT, rows=NP)))
            hp = hot_p[R].rearrange("p e m -> p (e m)")
            step(dve.tensor_tensor_scan(hp, hc, hc, 0.0, ALU.add, ALU.bypass))
            step(dve.tensor_copy(e_cum[R], hot_p[R, :, KT - 1]))
            step(dve.tensor_copy(e_cnt[R, 0:1], e_cum[R, 0:1]))
            step(dve.tensor_tensor(e_cnt[R, 1:NE], e_cum[R, 1:NE], e_cum[R, 0:NE - 1], ALU.subtract))
            step(dve.tensor_tensor(e_cum[R], e_cum[R], e_cnt[R], ALU.subtract))
            step(dve.tensor_scalar(e_cnt[R], e_cnt[R], 127.0, None, ALU.add))
            step(dve.tensor_copy(e_int[R], e_cnt[R]))
            step(dve.tensor_scalar(e_int[R], e_int[R], 7, None, ALU.logical_shift_right))
            step(dve.tensor_copy(e_til[R], e_int[R]))
            step(dve.tensor_tensor_scan(e_end[R], e_til[R], e_til[R], 0.0, ALU.add, ALU.bypass))
            step(dve.tensor_tensor(e_til[R], e_end[R], e_til[R], ALU.subtract))
            step(dve.scalar_tensor_tensor(e_cum[R], e_til[R], 128.0, e_cum[R], ALU.mult, ALU.subtract))
            step(dve.tensor_tensor(hp, hp, hc, ALU.subtract))
            step(dve.tensor_tensor(hp, hp, bank(3, NE * KT, rows=NP), ALU.add))
            step(dve.tensor_tensor(hot_p[R], hot_p[R], e_cum[R].unsqueeze(2).broadcast_to([NP, NE, KT]), ALU.add))
            step(dve.tensor_tensor(hot_p[R], hot_p[R], hot_k[R], ALU.mult))
            step(dve.tensor_reduce(slot_f[R].rearrange("p k t -> p (k t)"), hot_p[R].rearrange("p e m -> p m e"),
                                   AX.X, ALU.add))
            dve.tensor_copy(slot_i[R], slot_f[R]).then_inc(slots_ok, 1)
            step(dve.tensor_tensor(e_le[:], e_end[0:1].unsqueeze(1).broadcast_to([1, SLOT_TILES, NE]),
                                   iota[0:1, 0:SLOT_TILES].unsqueeze(2).broadcast_to([1, SLOT_TILES, NE]), ALU.is_le))
            step(dve.tensor_reduce(tile_f[:], e_le[:], AX.X, ALU.add))
            step(dve.tensor_scalar(tile_f[:], tile_f[:], float(NE - 1), None, ALU.min))
            dve.tensor_copy(tile_e[:], tile_f[:]).then_inc(tile_ok, 1)
            dve.wait_ge(tile_ok, 1)

            dve.wait_ge(w1_in, 16 * (NE + 1))
            dve.wait_ge(w2_in, 16 * (NE + 1))
            dve.wait_ge(sent, 16 * KT)

            ex = {}

            def slots_step(n, k):
                load_experts(mybir.EngineType.DVE, ex, n, k)
                m_ = n
                if here(m_, SLOT_TILES):
                    dve.wait_ge(sh_ps, m_ + 1)
                    after(dve, shT_ps, m_ - 1)
                    dve.tensor_tensor(slot_h[k % 2][:], bank(1 + k % 2, HID),
                                      b1_bc[:, bass.ts(ex["wide", k], 1), :].rearrange("p a n -> p (a n)"), ALU.add)\
                       .then_inc(sh_pre, 1)
                m_ = n - 1
                if here(m_, SLOT_TILES):
                    dve.wait_ge(shT_ps, m_ + 1)
                    after(dve, sy_ps, m_ - 1)
                    dve.tensor_copy(slot_hT[(k + 1) % 2][:].rearrange("p c n -> p (c n)"), bank(3 + (k + 1) % 2))\
                       .then_inc(shT_sb, 1)
                m_ = n - 2
                if here(m_, SLOT_TILES):
                    dve.wait_ge(sy_ps, m_ + 1)
                    if isinstance(m_, int):
                        after(dve, slot_out[k % 2], 8 * (m_ - k % 2))
                    else:
                        dve.wait_ge(slot_out[k % 2], 8 * (m_ - k % 2))
                    dve.tensor_tensor(slot_y[k % 2][:], bank(5 + k % 2, D),
                                      b2_bc[:, bass.ts(ex["late", k], 1), :].rearrange("p a n -> p (a n)"), ALU.add)\
                       .then_inc(sy_sb, 1)

            steps(dve, slots_step, 0, SLOT_TILES + 2, 1, SLOT_TILES // 4 - 1, 4)
            for t in range(NB):
                dve.wait_ge(pick_in[t % 4], 32 * (t // 4 + 1))
                step(dve.scalar_tensor_tensor(res[R, t, :], pick[t % 4][R, 0, :], wgt[R, 0, t:t + 1], res[R, t, :],
                                              ALU.mult, ALU.add))
                dve.scalar_tensor_tensor(res[R, t, :], pick[t % 4][R, 1, :], wgt[R, 1, t:t + 1], res[R, t, :],
                                         ALU.mult, ALU.add).then_inc(final_ok, 1)
                dve.wait_ge(final_ok, t + 1)
                dve.memset(nw_t[:], 0.0).then_inc(picked, 1)


_INS = ['x', 'src', 'dst', 'edge_weight1', 'L0_gnn_mW1', 'L0_gnn_mb1', 'L0_gnn_ln_g', 'L0_gnn_ln_b', 'L0_gnn_mW2',
        'L0_gnn_mb2', 'L0_gnn_uW1', 'L0_gnn_ub1', 'L0_gnn_uW2', 'L0_gnn_ub2', 'L0_mix_Wqkv', 'L0_mix_Wout',
        'L0_mix_bout', 'L0_ffn_gamma', 'L0_ffn_beta', 'L0_ffn_Wr', 'L0_ffn_br', 'L0_ffn_W1', 'L0_ffn_b1',
        'L0_ffn_W2', 'L0_ffn_b2']


def kernel(**inputs):
    import numpy as _np
    import concourse.bacc as _bacc
    from concourse import mybir as _mybir
    from concourse.bass_utils import run_bass_kernel_spmd as _run

    nc = _bacc.Bacc("TRN2", target_bir_lowering=False, num_devices=1)
    arrays, args = {}, []
    for name in _INS:
        a = _np.ascontiguousarray(inputs[name])
        arrays[f"in_{name}_dram"] = a
        args.append(nc.dram_tensor(f"in_{name}_dram", a.shape, _mybir.dt.from_np(a.dtype), kind="ExternalInput").ap())
    out = nc.dram_tensor("out_0_dram", inputs["x"].shape, _mybir.dt.float32, kind="ExternalOutput").ap()
    gps_layer(nc, *args, out)
    r = _run(nc, [arrays], core_ids=[0])
    return r.results[0]["out_0_dram"]
```

```python
import concourse.bass as bass
from concourse import mybir
from contextlib import ExitStack

F32 = mybir.dt.float32
F32R = mybir.dt.float32r
F16 = mybir.dt.float16
I32 = mybir.dt.int32
U32 = mybir.dt.uint32
U16 = mybir.dt.uint16
ALU = mybir.AluOpType
ACT = mybir.ActivationFunctionType
AX = mybir.AxisListType

EPS = 1e-5
ROUND = 12582912.0
RSQRT_MAGIC = 1597463007


class Steps:

    def __init__(self, engine, semaphore):
        self.engine, self.semaphore, self.count, self.turns = engine, semaphore, 0, None

    def did(self, instruction):
        instruction.then_inc(self.semaphore, 1)
        self.count += 1

    def join(self):
        self.engine.wait_ge(self.semaphore, self.count if self.turns is None else self.turns + self.count)

    def enter(self, index, first, per_turn):
        self.turns, self.start, self.per_turn = (index - first) * per_turn, self.count, per_turn

    def leave(self, trips):
        assert self.count - self.start == self.per_turn, (self.count, self.start)
        self.turns, self.count = None, self.start + self.per_turn * trips


def gps_layer(nc, x, src, dst, edge_weight1, mW1, mb1, ln_g, ln_b, mW2, mb2, uW1, ub1, uW2, ub2,
              Wqkv, Wout, bout, gamma, beta, Wr, br, W1, b1, W2, b2, out):
    N, D = x.shape
    E = src.shape[0]
    NP = 125
    NB = N // NP
    EC = E // NP
    KD = D // 128
    G = 2
    UE = 128 * G
    TURN = 10
    UNITS = -(-((E + NB * (UE - 1)) // UE) // TURN) * TURN
    TILES = UNITS * G
    SC = 20
    HD = 64
    NQ = Wqkv.shape[0] // 3
    HEADS = NQ // HD
    QC = NQ // 128
    NE, _, HID = W1.shape
    HC = HID // 128
    TOPK = 2
    SLOT_TILES = (TOPK * N + NE * 127) // 128
    KT = TOPK * NB
    HR = NP + 2
    assert NP * NB == N and NP * EC == E and SLOT_TILES % 2 == 0 and D == 256

    dst_table = nc.dram_tensor("dst_table", [N, D], F32).ap()
    sorted_edges = nc.dram_tensor("sorted_edges", [128 * TILES, 4], F32).ap()
    expert_in = nc.dram_tensor("expert_in", [SLOT_TILES * 128, D], F32).ap()
    expert_out = nc.dram_tensor("expert_out", [SLOT_TILES * 128, D], F32).ap()

    ctx = ExitStack()
    with ctx:
        def sem(name):
            return ctx.enter_context(nc.semaphore(name))

        base = (nc.sbuf_base + 31) // 32 * 32
        place, size_of, filled, cursor = {}, {}, {}, [base]

        def region(name, size):
            place[name], size_of[name], filled[name] = cursor[0], size, 0
            cursor[0] += (size + 31) // 32 * 32

        def at(name, shape, dt, owner, byte=0):
            return nc.alloc_sbuf_tensor_at(name, shape, dt, offset=place[owner] + byte)

        def nbytes(shape, dt):
            n = {F16: 2, U16: 2}.get(dt, 4)
            for k in shape[1:]:
                n *= k
            return (n + 31) // 32 * 32

        def inside(name, shape, dt, owner):
            t = at(name, shape, dt, owner, filled[owner])
            filled[owner] += nbytes(shape, dt)
            assert filled[owner] <= size_of[owner], (owner, name, filled[owner])
            return t

        NODE = NB * D * 4
        region("res", NODE)
        region("blocks", NODE)
        region("turned", NODE)
        region("src_hi", NODE)
        region("src_lo", NODE)
        region("edges", TILES * 16 + 512)
        region("work", 34 * 1024)
        region("weights", 32 * 1024)
        region("small", 9600)
        ctx.enter_context(nc.sbuf_tensor("arena", [128, (cursor[0] - base) // 4], F32))

        res = at("res_t", [128, NB, D], F32, "res")
        xn = at("xn_t", [128, NB, D], F32, "blocks")
        agg = at("agg_t", [128, NB, D], F32, "blocks")
        xnT = at("xnT_t", [128, NB, KD, 128], F32, "turned")
        src_hi = at("src_hi_t", [128, NB, D], F32R, "src_hi")
        src_lo = at("src_lo_t", [128, NB, D], F32R, "src_lo")
        recs = at("recs_t", [128, TILES, 4], F32, "edges")
        rec_sb = at("rec_sb_t", [128, EC, 4], F32, "edges")

        place_u = at("place_u_t", [128, EC], U16, "edges", EC * 16)
        assert 128 * TILES < 65536
        onehot = at("onehot_t", [128, NB, EC], F16, "turned")
        masked = at("masked_t", [128, NB, EC], U16, "turned")
        scanned = at("scanned_t", [128, NB * EC], F16, "work")
        src_i = at("src_i_t", [128, EC], I32, "blocks")
        dst_i = at("dst_i_t", [128, EC], I32, "blocks", 2048)
        blk_f = at("blk_f_t", [128, EC], F32, "blocks", 4096)
        row_f = at("row_f_t", [128, EC], F32, "blocks", 6144)
        rank_f = at("rank_f_t", [128, EC], F32, "blocks", 8192)
        pos_i = at("pos_i_t", [128, EC], I32, "blocks", 10240)
        blk_h = at("blk_h_t", [128, EC], F16, "blocks", 22528)
        low_i = at("low_i_t", [128, EC], I32, "blocks", 12288)
        top_i = at("top_i_t", [128, EC], I32, "blocks", 14336)
        d2_r = at("d2_r_t", [128, EC], F32R, "blocks", 16384)
        d2_f = at("d2_f_t", [128, EC], F32, "blocks", 18432)
        unit_le = at("unit_le_t", [1, UNITS, NB], F16, "work")
        defaults = at("defaults_t", [128, TILES // 10, 4], F32, "blocks", 23552)
        bias_bc = at("bias_bc_t", [128, D], F32, "work", 32768)
        bout_bc = at("bout_bc_t", [128, D], F32, "work", 33792)
        unit_f = at("unit_f_t", [1, UNITS], F32, "work", 16384)

        wkv_nat = at("wkv_nat_t", [128, 2 * QC, D], F32, "work", 20480)
        wout_nat = at("wout_nat_t", [128, KD, NQ], F32, "work", 28672)
        dst_stage = [at(f"dst_stage{i}", [128, D], F32, "work", 1024 * i) for i in range(2)]
        kv_sq = at("kv_sq_t", [128, 2 * NQ], F32, "work", 2048)
        k_n = [at(f"k_n{i}", [128, NQ], F32, "work", 6144 + 2048 * i) for i in range(2)]
        v_n = [at(f"v_n{i}", [128, NQ], F32, "work", 10240 + 2048 * i) for i in range(2)]
        zero_rows = at("zero_rows_t", [128, 2048], F32, "src_lo")

        msg1 = at("msg1_t", [128, TURN, G, D], F32, "work")
        hotT = at("hotT_t", [128, 2, UE], F32R, "work", 20480)
        msg1n = at("msg1n_t", [128, 2, G, D], F32, "work", 22528)
        SPLIT = (KD * G - 1) * 128
        msg1T_hi = at("msg1T_hi_t", [128, 2, SPLIT], F32R, "work", 26624)
        msg1T_f = at("msg1T_f_t", [128, 2, 128], F32, "work", 29696)
        msg1T_lo = at("msg1T_lo_t", [128, 2, SPLIT], F32R, "weights")
        msg2 = at("msg2_t", [128, 2, G, D], F32, "work", 30720)

        aggT = [at(f"aggT{i}", [128, KD, 4, NP], F32, "work", 4096 * i) for i in range(2)]
        hidT = [at(f"hidT{i}", [128, KD, 4, NP], F32, "work", 8192 + 4096 * i) for i in range(2)]
        xm = at("xm_t", [128, NB, D], F32, "work")
        x2T = [at(f"x2T{i}", [128, KD, NP], F32, "work", NODE + 1024 * i) for i in range(2)]
        assert 8192 + 4096 * 2 <= NODE
        w1_sb = at("w1_sb_t", [128, NE, KD, HID], F32, "src_hi")
        b1_bc = at("b1_bc_t", [128, NE, HID], F32, "src_hi", 32768)
        w2_sb = at("w2_sb_t", [128, NE, HC, D], F32, "blocks")
        w2_rest = at("w2_rest_t", [128, NE, HC, D], F32R, "blocks")
        w2_lead = at("w2_lead_t", [128, NE, HC, D], F32R, "weights")
        b2_bc = at("b2_bc_t", [128, NE, D], F32, "blocks", 32768)
        slot_x = [at(f"slot_x{i}", [128, D], F32, "work", 1024 * i) for i in range(4)]
        slot_xT = [at(f"slot_xT{i}", [128, KD, 128], F32, "work", 4096 + 1024 * i) for i in range(2)]
        slot_h = [at(f"slot_h{i}", [128, HID], F32, "work", 6144 + 2048 * i) for i in range(2)]
        slot_hT = [at(f"slot_hT{i}", [128, HC, 128], F32R, "work", 10240 + 2048 * i) for i in range(2)]
        slot_hR = [at(f"slot_hR{i}", [128, HC, 128], F32R, "work", 24576 + 2048 * i) for i in range(2)]
        slot_y = [at(f"slot_y{i}", [128, D], F32, "work", 14336 + 1024 * i) for i in range(2)]
        pick = [at(f"pick{i}", [128, TOPK, D], F32, "work", 16384 + 2048 * i) for i in range(4)]

        w = lambda n, s, t=F32: inside(n, s, t, "weights")
        mw1_sb = w("mw1_sb", [128, KD, 2, D])
        w2c_raw = w("w2c_raw", [128, KD, D])
        w2c = w("w2c", [128, KD, D])
        hot = at("hot_t", [128, TURN, G, 128], F32R, "weights", filled["weights"])
        wkvT = w("wkvT", [128, KD, 2 * NQ])
        wq_nat = w("wq_nat", [128, QC, D])
        ident_r = at("ident_r", [128, 128], F32R, "weights", filled["weights"] - 2048)
        w2_hi = at("w2_hi_t", [128, KD, D], F32R, "weights", filled["weights"])
        w2_lo = at("w2_lo_t", [128, KD, D], F32R, "weights", filled["weights"] + 2048)
        woutT = w("woutT", [128, QC, D])
        mixP = w("mixP", [128, QC, D])
        uw1_sb = at("uw1_sb", [128, 2 * KD, D], F32, "weights", filled["weights"] - 4 * QC * D)
        mixP_byte = filled["weights"] - 4 * QC * D
        mixG = w("mixG", [128, KD, D])
        uw2_sb = w("uw2_sb", [128, KD, D])
        place["late"], size_of["late"], filled["late"] = place["blocks"] + 40960, 2 * NODE - 40960, 0
        s = lambda n, sh, t=F32: inside(n, sh, t, "small")
        ident = s("ident", [128, 128])
        iota = s("iota", [128, 256])
        earlier = s("earlier", [128, 128])
        ones = s("ones", [128, 128])
        bw = s("bw", [2, D])
        bw_sel = s("bw_sel", [2, 128])
        g_col = s("g_col", [128, KD])
        b_col = s("b_col", [128, KD])
        mb2_bc = s("mb2_bc", [128, D])
        ub1_col = s("ub1_col", [128, KD])
        gamma_col = s("gamma_col", [128, KD])
        beta_col = s("beta_col", [128, KD])
        wr_sb = s("wr_sb", [128, KD, NE])
        wrc = s("wrc", [128, KD, NE])
        logit0 = s("logit0", [128, NE])
        eps2_col = s("eps2_col", [128, 1])
        br_bc = s("br_bc", [128, NE])
        eps_col = s("eps_col", [128, 1])
        stats = s("stats", [128, NB, 6])
        meanvar = s("meanvar", [128, NB, 2])
        rstd = s("rstd", [128, NB])
        rowcnt = s("rowcnt", [128, NB])
        cum = s("cum", [128, NB])
        ints = at("ints", [128, NB], I32, "blocks", 24704)
        prefix = s("prefix", [128, NB])
        nunits = at("nunits", [128, NB], F32, "blocks", 24576)
        ends = s("ends", [128, NB])
        unit_blk = s("unit_blk", [1, UNITS], I32)
        kv_ss = s("kv_ss", [128, 2 * HEADS])
        kv_rs = s("kv_rs", [128, HEADS])
        wmean = at("wmean", [128, KD * 2 * HEADS], F32, "work", 15360)
        lb_bc = at("lb_bc_t", [128, KD, 128], F32, "work", 17408)
        shift = at("shift_t", [128, D], F32, "work", 18432)
        beta_bc = at("beta_bc_t", [128, KD, 128], F32, "work", 14336)
        scat_idx = s("scat_idx", [128, 2, SC], I32)
        stage_idx = s("stage_idx", [128, 2, TURN], I32)
        fence = s("fence", [1, TURN])
        nw_t = s("nw_t", [128, 2, G])
        place["w2c_raw"], size_of["w2c_raw"], filled["w2c_raw"] = place["weights"] + 4096, 2048, 0
        e = lambda n, sh, t=F32: inside(n, sh, t, "w2c_raw")
        est = e("est", [128, TURN, G, 6])
        emv = e("emv", [128, TURN, G, 2])
        nw_y = e("nw_y", [128, TURN, G])
        nw_b = e("nw_b", [128, TURN, G])
        nw_v = e("nw_v", [128, 2, G])
        nw_s = e("nw_s", [128, 2, G])
        nw_1 = e("nw_1", [128, 2, G])
        nw_2 = e("nw_2", [128, 2, G])
        nw_i = e("nw_i", [128, 2, G], I32)

        hot_k = at("hot_k", [128, NE, KT], F32, "edges")
        hot_c = at("hot_c", [128, NE, KT], F32, "edges", 1600)
        hot_p = at("hot_p", [128, NE, KT], F32, "edges", 3200)
        logits = at("logits", [128, NB, NE], F32, "edges", 4800)
        top_v = at("top_v", [128, NB, NE], F32, "edges", 5600)
        top_e = at("top_e", [128, NB, 8], U32, "edges", 6400)
        top_f = inside("top_f", [128, TOPK, NB], F32, "late")
        slot_i = inside("slot_i", [128, TOPK, NB], I32, "late")
        slot_f = inside("slot_f", [128, TOPK, NB], F32, "late")
        wgt = inside("wgt", [128, TOPK, NB], F32, "late")
        wtmp = inside("wtmp", [128, NB], F32, "late")
        nbias = inside("nbias", [128, NB], F32, "late")
        e_cum = inside("e_cum", [128, NE], F32, "late")
        e_cnt = inside("e_cnt", [128, NE], F32, "late")
        e_int = inside("e_int", [128, NE], I32, "late")
        e_til = inside("e_til", [128, NE], F32, "late")
        e_end = inside("e_end", [128, NE], F32, "late")
        e_le = at("e_le", [1, SLOT_TILES, NE], F32, "edges", 0)
        tile_f = inside("tile_f", [1, SLOT_TILES], F32, "late")
        tile_e = inside("tile_e", [1, SLOT_TILES], I32, "late")
        scat_rec = inside("scat_rec", [128, 2, SC, 4], F32, "small")
        ps = ctx.enter_context(nc.psum_tensor("ps", [128, 8, 512], F32))

        def bank(b, n=512, rows=128, first=0):
            return ps[0:rows, b, first:first + n]

        edges_in, x_in, mw1_in, bw_in = sem("edges_in"), sem("x_in"), sem("mw1_in"), sem("bw_in")
        wmix_in, small_in, upd_w_in, uw1_in = sem("wmix_in"), sem("small_in"), sem("upd_w_in"), sem("uw1_in")
        defaults_out, zeros_out, recs_in = sem("defaults_out"), sem("zeros_out"), sem("recs_in")
        consts, fills = sem("consts"), sem("fills")
        dve_step, pool_step = sem("dve_step"), sem("pool_step")
        wT_ps, wT_sb = sem("wT_ps"), sem("wT_sb")
        rowcnt_ok, counts_ps, pos_ok, units_ok = sem("rowcnt_ok"), sem("counts_ps"), sem("pos_ok"), sem("units_ok")
        scattered = [sem(f"scattered{h}") for h in range(2)]
        var_ok, sd_ok, xn_ok, xnT_ps, xnT_sb = sem("var_ok"), sem("sd_ok"), sem("xn_ok"), sem("xnT_ps"), sem("xnT_sb")
        pads_ok, tab_ps, tab_sb, dst_sb = sem("pads_ok"), sem("tab_ps"), sem("tab_sb"), sem("dst_sb")
        dst_out = [sem(f"dst_out{i}") for i in range(2)]
        kv_ps, sq_sb, v_sb, ss_ok, kvsd_ok, kn_ok, dots_ps = (sem(n) for n in (
            "kv_ps", "sq_sb", "v_sb", "ss_ok", "kvsd_ok", "kn_ok", "dots_ps"))
        wrg_ok, router_ps, logit0_ok, hpre_ps, mixed_ps, mixed_ok, hpre_sb = (sem(n) for n in (
            "wrg_ok", "router_ps", "logit0_ok", "hpre_ps", "mixed_ps", "mixed_ok", "hpre_sb"))
        wkv_centered, diag_ok, mixP_ps, mixP_sb, mixG_ps, mixG_sb = (sem(n) for n in (
            "wkv_centered", "diag_ok", "mixP_ps", "mixP_sb", "mixG_ps", "mixG_sb"))
        row_in = [sem(f"row_in{k}") for k in range(TURN)]
        hot_ready, hotT_ps, hotT_sb, pre_ps, pre_sb, msg1_sb, msg1n_sb = (sem(n) for n in (
            "hot_ready", "hotT_ps", "hotT_sb", "pre_ps", "pre_sb", "msg1_sb", "msg1n_sb"))
        hot_weight, rstd_ok, newton_step = sem("hot_weight"), sem("rstd_ok"), sem("newton_step")
        msg1T_ps, msg1T_sb, msg1T_lo_sb, w2_split, msg2_ps, msg2_sb, sum_ps, sum_sb = (sem(n) for n in (
            "msg1T_ps", "msg1T_sb", "msg1T_lo_sb", "w2_split", "msg2_ps", "msg2_sb", "sum_ps", "sum_sb"))
        aggT_ps, aggT_sb, hid_ps, hid_pre, hid_sb, upd_ps, x2_ok = (sem(n) for n in (
            "aggT_ps", "aggT_sb", "hid_ps", "hid_pre", "hid_sb", "upd_ps", "x2_ok"))
        var2_ok, sd2_ok, rstd2_ok, xm_ok, x2T_ps, x2T_sb, logit_ps = (sem(n) for n in (
            "var2_ok", "sd2_ok", "rstd2_ok", "xm_ok", "x2T_ps", "x2T_sb", "logit_ps"))
        gap_ok, exp_ok, hotk_ok, route_ps, slots_ok, tile_ok, sent = (sem(n) for n in (
            "gap_ok", "exp_ok", "hotk_ok", "route_ps", "slots_ok", "tile_ok", "sent"))
        w1_in, w2_in = sem("w1_in"), sem("w2_in")
        slot_in = [sem(f"slot_in{k}") for k in range(4)]
        slot_out = [sem(f"slot_out{k}") for k in range(2)]
        sxT_ps, sxT_sb, sh_ps, sh_pre, sh_sb, shT_ps, shT_lead, shT_sb, sy_ps, sy_sb = (sem(n) for n in (
            "sxT_ps", "sxT_sb", "sh_ps", "sh_pre", "sh_sb", "shT_ps", "shT_lead", "shT_sb", "sy_ps", "sy_sb"))
        pick_in = [sem(f"pick_in{k}") for k in range(4)]
        w2_lead_ok, w2_rest_ok = sem("w2_lead_ok"), sem("w2_rest_ok")
        picked, final_ok, stored = sem("picked"), sem("final_ok"), sem("stored")

        N_CONST, N_FILL = 4, 2
        N_DST = [(NB + 1) // 2, NB // 2]
        SMALL = 9
        CH = [list(range(t, min(t + 4, NB))) for t in range(0, NB, 4)]
        LAST = UNITS + 9

        def here(m, count):
            return not isinstance(m, int) or 0 <= m < count

        def steps(engine, body, first, last, trips_lo, trips_hi, turn):
            for n in range(first, turn * trips_lo):
                body(n, n % turn)
            with engine.Fori(trips_lo, trips_hi) as i:
                for k in range(turn):
                    body(turn * i + k, k)
            for n in range(turn * trips_hi, last):
                body(n, n % turn)

        def after(engine, semaphore, count):
            if not isinstance(count, int) or count > 0:
                engine.wait_ge(semaphore, count)

        def registers(engine, table, first, count, largest):
            _, values = nc.values_load_multi_w_load_instructions(
                table[0:1, bass.ds(first, count)], engines=[engine], min_val=0, max_val=largest,
                skip_runtime_bounds_check_because="the table is written with a minimum against its largest index")
            return values

        def load_blocks(engine, blk, first, k, count):
            if isinstance(first, int):
                skip = max(0, -first)
                first, k, count = first + skip, k + skip, min(count - skip, UNITS - first - skip)
                if count <= 0:
                    return
            blk.update(zip(range(k, k + count), registers(engine, unit_blk, first, count, NB - 1)))

        def load_experts(engine, ex, n, k):
            if k == 0:
                for name, first in (("wide", n), ("late", n - 2)):
                    if isinstance(n, int):
                        low, high = max(first, 0), min(first + 4, SLOT_TILES)
                    else:
                        low, high = first, first + 4
                    if isinstance(n, int) and high <= low:
                        continue
                    count = high - low if isinstance(n, int) else 4
                    skip = low - first if isinstance(n, int) else 0
                    for j, v in enumerate(registers(engine, tile_e, low, count, NE - 1)):
                        ex[name, skip + j] = v

        block = ctx.enter_context(nc.Block())


        @block.sync
        def _(sp):
            sp.dma_start(src_i[0:NP, :], src.rearrange("(p c) -> p c", p=NP)).then_inc(edges_in, 16)
            sp.dma_start(dst_i[0:NP, :], dst.rearrange("(p c) -> p c", p=NP)).then_inc(edges_in, 16)
            sp.dma_start(d2_f[0:NP, :], edge_weight1.rearrange("(p c) a -> p (c a)", p=NP)).then_inc(edges_in, 16)
            sp.dma_start(wkv_nat[:], Wqkv[NQ:3 * NQ, :].rearrange("(q p) c -> p q c", p=128)).then_inc(wmix_in, 16)
            sp.dma_start(wout_nat[:], Wout.rearrange("(o p) f -> p o f", p=128)).then_inc(wmix_in, 16)
            sp.dma_start(wq_nat[:], Wqkv[0:NQ, :].rearrange("(q p) c -> p q c", p=128)).then_inc(wmix_in, 16)
            sp.dma_start(res[0:NP], x.rearrange("(p t) d -> p t d", p=NP)).then_inc(x_in, 16)
            for k in range(KD):
                sp.dma_start(mw1_sb[:, k], mW1[0:2 * D, :].rearrange("(a k p) n -> k p a n", a=2, p=128)[k])\
                  .then_inc(mw1_in, 16)
            sp.dma_start(bw[0:1, :], mb1.rearrange("(a n) -> a n", a=1)).then_inc(bw_in, 16)
            sp.dma_start(bw[1:2, :], mW1[2 * D:2 * D + 1, :]).then_inc(bw_in, 16)
            sp.dma_start(w2c_raw[:], mW2.rearrange("(k p) n -> p k n", p=128)).then_inc(small_in, 16)
            with nc.allow_non_contiguous_dma("vectors of 256 values, one value a partition"):
                for t, v in ((g_col, ln_g), (b_col, ln_b), (ub1_col, ub1), (gamma_col, gamma), (beta_col, beta)):
                    sp.dma_start(t[:], v.rearrange("(k p) -> p k", p=128)).then_inc(small_in, 16)
                sp.dma_start(mb2_bc[:], mb2.partition_broadcast(128)).then_inc(small_in, 16)
                sp.dma_start(wr_sb[:], Wr.rearrange("(k p) e -> p k e", p=128)).then_inc(small_in, 16)
                sp.dma_start(br_bc[:], br.partition_broadcast(128)).then_inc(small_in, 16)
            sp.dma_start(bias_bc[:], ub2.partition_broadcast(128)).then_inc(upd_w_in, 16)
            sp.dma_start(bout_bc[:], bout.partition_broadcast(128)).then_inc(upd_w_in, 16)
            sp.dma_start(uw2_sb[:], uW2.rearrange("(k p) n -> p k n", p=128)).then_inc(upd_w_in, 16)
            sp.wait_ge(fills, N_FILL)
            reps = 10
            sp.dma_start(sorted_edges.rearrange("(p a b) f -> p a (b f)", p=128, a=reps),
                         defaults[:].rearrange("p b f -> p (b f)").unsqueeze(1)
                         .broadcast_to([128, reps, TILES // 10 * 4])).then_inc(defaults_out, 16)
            reps = SLOT_TILES * D // 2048
            sp.dma_start(expert_in.rearrange("(p s) d -> p (s d)", p=128).rearrange("p (a b) -> p a b", a=reps),
                         zero_rows[:].unsqueeze(1).broadcast_to([128, reps, 2048])).then_inc(zeros_out, 16)
            for t in range(NB):
                sp.wait_ge(dst_sb, t + 1)
                sp.dma_start(dst_table.rearrange("(p t) d -> p t d", p=NP)[:, t, :], dst_stage[t % 2][0:NP, :])\
                  .then_inc(dst_out[t % 2], 16)
            sp.wait_ge(mixG_sb, KD)
            sp.dma_start(uw1_sb[:], uW1.rearrange("(k p) n -> p k n", p=128)).then_inc(uw1_in, 16)
            for h in range(2):
                sp.wait_ge(scattered[h], 16 * EC // 2)
            sp.dma_start(recs[:], sorted_edges.rearrange("(p t) f -> p t f", p=128)).then_inc(recs_in, 16)
            sp.wait_ge(pre_ps, UNITS)
            for e in range(NE):
                sp.dma_start(w1_sb[:, e], W1[e].rearrange("(k p) h -> p k h", p=128)).then_inc(w1_in, 16)
            sp.dma_start(b1_bc[:].rearrange("p e h -> p (e h)"),
                         b1.rearrange("e h -> (e h)").partition_broadcast(128)).then_inc(w1_in, 16)
            sp.wait_ge(x2_ok, NB)
            for e in range(NE):
                sp.dma_start(w2_sb[:, e], W2[e].rearrange("(k p) n -> p k n", p=128)).then_inc(w2_in, 16)
            sp.dma_start(b2_bc[:].rearrange("p e n -> p (e n)"),
                         b2.rearrange("e n -> (e n)").partition_broadcast(128)).then_inc(w2_in, 16)
            sp.wait_ge(sent, 16 * KT)

            def slots_step(n, k):
                after(sp, sxT_ps, n - 3)
                sp.dma_start(slot_x[k][:], expert_in[bass.ts(n, 128), :]).then_inc(slot_in[k], 16)

            steps(sp, slots_step, 0, SLOT_TILES, 1, SLOT_TILES // 4, 4)
            for g in range(5):
                sp.wait_ge(final_ok, 5 * (g + 1))
                sp.dma_start(out.rearrange("(p t) d -> p t d", p=NP)[:, 5 * g:5 * g + 5, :],
                             res[0:NP, 5 * g:5 * g + 5, :]).then_inc(stored, 16)
            sp.wait_ge(stored, 16 * 5)

        @block.gpsimd
        def _(pool):
            st = Steps(pool, pool_step)
            st.did(pool.iota(iota[:], [[1, 256]], channel_multiplier=0, allow_small_or_imprecise_dtypes=True))
            st.did(pool.memset(ident[:], 0.0))
            st.did(pool.memset(ones[:], 1.0))
            st.did(pool.memset(eps_col[:], EPS))
            st.did(pool.memset(defaults[:], 0.0))
            st.join()
            pool.affine_select(out=ident[:], in_=ident[:], compare_op=ALU.not_equal, fill=1.0, base=0,
                               pattern=[[-1, 128]], channel_multiplier=1).then_inc(consts, 1)
            pool.affine_select(out=earlier[:], in_=ones[:], compare_op=ALU.is_gt, fill=0.0, base=0,
                               pattern=[[1, 128]], channel_multiplier=-1).then_inc(consts, 1)
            st.did(pool.affine_select(out=bw_sel[:], in_=ones[0:2, :], compare_op=ALU.is_ge, fill=0.0, base=0,
                                      pattern=[[1, 128]], channel_multiplier=-NP))
            pool.memset(defaults[:, :, 1:2], -1.0).then_inc(fills, 1)
            pool.memset(zero_rows[:], 0.0).then_inc(fills, 1)
            st.join()
            pool.affine_select(out=bw_sel[:], in_=bw_sel[:], compare_op=ALU.is_ge, fill=0.0, base=NP - 1,
                               pattern=[[-1, 128]], channel_multiplier=NP).then_inc(consts, 1)
            pool.memset(eps2_col[:], EPS * EPS).then_inc(consts, 1)

            pool.wait_ge(pos_ok, 1)
            pool.wait_ge(defaults_out, 16)
            def carry_wait(k):
                st.did(pool.tensor_tensor(fence[:, k:k + 1], eps_col[0:1, :], eps_col[0:1, :], ALU.add))

            def scatter_group(i):
                for h in range(2):
                    after(pool, scattered[h], i * 16 * SC)
                    st.did(pool.tensor_copy(scat_idx[0:NP, h, :], place_u[0:NP, bass.ds(SC * (2 * i + h), SC)]))
                    st.did(pool.tensor_copy(scat_rec[0:NP, h], rec_sb[0:NP, bass.ds(SC * (2 * i + h), SC), :]))
                    st.join()
                    carry_wait(h)
                    for c in range(SC):
                        pool.indirect_dma_start(
                            out=sorted_edges, out_offset=bass.IndirectOffsetOnAxis(scat_idx[0:NP, h, c:c + 1], 0),
                            in_=scat_rec[0:NP, h, c, :], in_offset=None).then_inc(scattered[h], 16)

            scatter_group(0)
            pool.wait_ge(pos_ok, 2)
            with pool.Fori(1, EC // (2 * SC)) as i:
                st.enter(i, 1, 6)
                scatter_group(i)
            st.leave(EC // (2 * SC) - 1)

            pool.wait_ge(recs_in, 16)
            pool.wait_ge(mixG_sb, KD)
            for i in range(2):
                pool.wait_ge(dst_out[i], 16 * N_DST[i])
            HALF = TURN // 2
            LATER = 3

            def edge_weights(m, k):
                if here(m, UNITS):
                    after(pool, sum_ps, m - TURN + 1)
                    pool.tensor_tensor(hot[:, k, :, NP:HR], recs[:, bass.ds(G * m, G), 2:4],
                                       ones[:, 0:G * 2].rearrange("p (a b) -> p a b", a=G), ALU.mult)\
                        .then_inc(hot_weight, 1)

            def edge_group(i):
                for k in range(TURN):
                    half = k // HALF
                    if k % HALF == 0:
                        for q in range(k, k + HALF):
                            after(pool, row_in[q], 32 * i)
                        st.did(pool.tensor_copy(stage_idx[:, half, :],
                                                recs[:, bass.ds(G * (TURN * i + k), TURN), 0]))
                        st.join()
                    after(pool, msg1n_sb, TURN * (i - 1) + k + 1)
                    carry_wait(k)
                    for j in range(G):
                        q = G * (k % HALF) + j
                        pool.indirect_dma_start(
                            out=msg1[:, k, j, :], out_offset=None, in_=dst_table,
                            in_offset=bass.IndirectOffsetOnAxis(stage_idx[:, half, q:q + 1], 0))\
                            .then_inc(row_in[k], 16)
                    edge_weights(TURN * i + k - LATER, (k - LATER) % TURN)

            edge_group(0)
            edge_group(1)
            with pool.Fori(2, UNITS // TURN) as i:
                st.enter(i, 2, 2 + TURN)
                edge_group(i)
            st.leave(UNITS // TURN - 2)
            for m in range(UNITS - LATER, UNITS):
                edge_weights(m, m % TURN)

            pool.wait_ge(slots_ok, 1)
            pool.wait_ge(xm_ok, NB)
            pool.wait_ge(zeros_out, 16)
            for k in range(TOPK):
                for t in range(NB):
                    pool.indirect_dma_start(
                        out=expert_in, out_offset=bass.IndirectOffsetOnAxis(slot_i[0:NP, k, t:t + 1], 0),
                        in_=xm[0:NP, t, :], in_offset=None).then_inc(sent, 16)
            def slots_step(n, k):
                pool.wait_ge(sy_sb, n + 1)
                pool.dma_start(expert_out[bass.ts(n, 128), :], slot_y[k % 2][:]).then_inc(slot_out[k % 2], 16)

            steps(pool, slots_step, 0, SLOT_TILES, 1, SLOT_TILES // 4, 4)
            for i in range(2):
                pool.wait_ge(slot_out[i], 16 * SLOT_TILES // 2)
            for t in range(NB):
                if t >= 4:
                    pool.wait_ge(picked, t - 3)
                for k in range(TOPK):
                    pool.indirect_dma_start(
                        out=pick[t % 4][0:NP, k, :], out_offset=None, in_=expert_out,
                        in_offset=bass.IndirectOffsetOnAxis(slot_i[0:NP, k, t:t + 1], 0))\
                        .then_inc(pick_in[t % 4], 16)

        @block.tensor
        def _(pe):
            def turn(out_, in_, rows):
                return pe.transpose(out_, in_, ident[0:rows, 0:rows])

            pe.wait_ge(consts, N_CONST)
            pe.wait_ge(wmix_in, 48)
            for c in range(KD):
                for q in range(2 * QC):
                    m = turn(bank(4 - 2 * c + q // 4, 128, first=q % 4 * 128), wkv_nat[:, q, c * 128:c * 128 + 128], 128)
                m.then_inc(wT_ps, 1)
            for j in range(QC):
                for o in range(KD):
                    m = turn(bank(j // 2, 128, first=j % 2 * D + o * 128), wout_nat[:, o, j * 128:j * 128 + 128], 128)
            m.then_inc(wT_ps, 1)
            pe.wait_ge(rowcnt_ok, 1)
            pe.matmul(bank(6, NB), earlier[0:NP, :], rowcnt[0:NP, :], start=True, stop=True)
            pe.matmul(bank(6, NB, first=32), ones[0:NP, :], rowcnt[0:NP, :], start=True, stop=True).then_inc(counts_ps, 1)

            pe.wait_ge(wrg_ok, 1)
            for k in range(KD):
                pe.matmul(bank(7, NE, first=256), ones[:], wrc[:, k, :], start=(k == 0), stop=(k == KD - 1))
            for k in range(KD):
                m = pe.matmul(bank(7, NE, first=288), beta_bc[:, k, :], wr_sb[:, k, :], start=(k == 0), stop=(k == KD - 1))
            for k in range(KD):
                m = pe.matmul(bank(7, D), lb_bc[:, k, :], w2c_raw[:, k, :], start=(k == 0), stop=(k == KD - 1))
            m.then_inc(router_ps, 1)

            pe.wait_ge(mw1_in, 32)
            pe.wait_ge(bw_in, 32)
            pe.wait_ge(wT_sb, KD + 1)
            pe.wait_ge(pads_ok, 1)

            def turn_xn(t):
                pe.wait_ge(xn_ok, t + 1)
                if t >= 2:
                    pe.wait_ge(xnT_sb, t - 1)
                for k in range(KD):
                    m = turn(bank(t % 2, NP, first=k * NP), xn[0:NP, t, k * 128:k * 128 + 128], NP)
                m.then_inc(xnT_ps, 1)

            def tables(t):
                pe.wait_ge(xnT_sb, t + 1)
                if t >= 2:
                    pe.wait_ge(tab_sb, t - 1)
                    pe.wait_ge(dst_sb, t - 1)
                for a in range(2):
                    o = bank(2 + 2 * a + t % 2, D)
                    for k in range(KD):
                        m = pe.matmul(o, xnT[:, t, k, :], mw1_sb[:, k, a, :], start=(k == 0),
                                      stop=(a == 1 and k == KD - 1))
                    if a == 0:
                        pe.matmul(o, bw_sel[:], bw[:], start=False, stop=True)
                m.then_inc(tab_ps, 1)

            turn_xn(0)
            for t in range(NB):
                if t + 1 < NB:
                    turn_xn(t + 1)
                tables(t)

            pe.wait_ge(wkv_centered, 1)
            pe.wait_ge(units_ok, 1)

            def dots(t):
                pe.wait_ge(kn_ok, t + 1)
                pe.wait_ge(v_sb, t + 1)
                for j in range(QC):
                    m = pe.matmul(bank(6, 128, first=128 * j), v_n[t % 2][0:NP, j * 128:j * 128 + 128],
                                  k_n[t % 2][0:NP, j * 128:j * 128 + 128], start=(t == 0 and j == 0), stop=(t == NB - 1),
                                  skip_group_check=True)
                m.then_inc(dots_ps, 1)

            for t in range(NB):
                b = 2 + 2 * (t % 2)
                if t == 0:
                    pe.wait_ge(tab_sb, NB)
                    pe.wait_ge(dst_sb, NB)
                if t >= 2:
                    pe.wait_ge(kn_ok, t - 1)
                    pe.wait_ge(sq_sb, t - 1)
                    pe.wait_ge(v_sb, t - 1)
                for h in range(2):
                    for k in range(KD):
                        m = pe.matmul(bank(b + h, NQ, rows=NP), xnT[:, t, k, 0:NP], wkvT[:, k, h * NQ:h * NQ + NQ],
                                      start=(k == 0), stop=(k == KD - 1))
                m.then_inc(kv_ps, 1)
                if t >= 1:
                    dots(t - 1)
            dots(NB - 1)
            pe.wait_ge(diag_ok, 1)
            for j in range(QC):
                m = pe.matmul(bank(j // 2, D, first=j % 2 * D), k_n[0][:, j * 128:j * 128 + 128], woutT[:, j, :],
                              start=True, stop=True)
            m.then_inc(mixP_ps, 1)
            pe.wait_ge(mixP_sb, 1)
            for c in range(KD):
                for j in range(QC):
                    m = pe.matmul(bank(2 + c, D), wq_nat[:, j, c * 128:c * 128 + 128], mixP[:, j, :],
                                  start=(j == 0), stop=(j == QC - 1))
                m.then_inc(mixG_ps, 1)

            pe.wait_ge(mixG_sb, KD)
            pe.wait_ge(uw1_in, 16)
            for c, blocks in enumerate(CH):
                t0, nb = blocks[0], len(blocks)
                for t in blocks:
                    if t >= 2:
                        pe.wait_ge(mixed_ok, t - 1)
                    for k in range(KD):
                        m = pe.matmul(bank(t % 2, D, rows=NP), xnT[:, t, k, 0:NP], mixG[:, k, :],
                                      start=(k == 0), stop=(k == KD - 1))
                    m.then_inc(mixed_ps, 1)
                if c >= 2:
                    pe.wait_ge(hpre_sb, c - 1)
                for f in range(KD):
                    for k in range(KD):
                        m = pe.matmul(bank(2 + 2 * (c % 2) + f, nb * NP), uw1_sb[:, k, f * 128:f * 128 + 128],
                                      xnT[:, t0:t0 + nb, k, 0:NP], start=(k == 0), stop=(k == KD - 1))
                m.then_inc(hpre_ps, 1)

            pe.wait_ge(w2_split, 1)
            pe.wait_ge(mixed_ok, NB)
            pe.wait_ge(hpre_sb, len(CH))
            blk = {}

            def edge_step(n, k):
                m_ = n - 6
                if here(m_, UNITS):
                    pe.wait_ge(msg1n_sb, m_ + 1)
                    after(pe, msg1T_lo_sb, m_ - 1)
                    for c in range(KD):
                        for j in range(G):
                            m = turn(bank(3 + k % 2, 128, first=c * UE + j * 128),
                                     msg1n[:, k % 2, j, c * 128:c * 128 + 128], 128)
                    m.then_inc(msg1T_ps, 1)
                m_ = n - 7
                if here(m_, UNITS):
                    pe.wait_ge(msg1T_sb, m_ + 1)
                    after(pe, msg2_sb, m_ - 1)
                    o = [bank(5 + (k + 1) % 2, D, first=j * D) for j in range(G)]
                    part = lambda t, j, c: t[:, (k + 1) % 2, c * UE + j * 128:c * UE + j * 128 + 128]
                    for j in range(G):
                        split = [c for c in range(KD) if c * UE + j * 128 < SPLIT]
                        for c in split:
                            pe.matmul(o[j], part(msg1T_hi, j, c), w2_hi[:, c, :], start=(c == 0), stop=False)
                            pe.matmul(o[j], part(msg1T_hi, j, c), w2_lo[:, c, :], start=False, stop=False)
                        if j == 0:
                            pe.wait_ge(msg1T_lo_sb, m_ + 1)
                        for c in split:
                            m = pe.matmul(o[j], part(msg1T_lo, j, c), w2_hi[:, c, :], start=False,
                                          stop=(c == KD - 1))
                        if len(split) < KD:
                            m = pe.matmul(o[j], msg1T_f[:, (k + 1) % 2, :], w2c[:, KD - 1, :], start=False, stop=True)
                    m.then_inc(msg2_ps, 1)
                if k == 0:
                    load_blocks(mybir.EngineType.PE, blk, n, 0, 3)
                if here(n, UNITS):
                    after(pe, hotT_sb, n + 1)
                    after(pe, pre_sb, n - 1)
                    for j in range(G):
                        for first, table in ((True, src_hi), (False, src_lo)):
                            m = pe.matmul(bank(1 + k % 2, D, first=j * D), hotT[0:HR, k % 2, j * 128:j * 128 + 128],
                                          table[0:HR, bass.ts(blk[k], 1), :].rearrange("p a n -> p (a n)"),
                                          start=first, stop=not first)
                    m.then_inc(pre_ps, 1)
                m_ = n + 1
                if here(m_, UNITS):
                    pe.wait_ge(hot_ready, m_ + 1)
                    pe.wait_ge(hot_weight, m_ + 1)
                    after(pe, hotT_sb, m_)
                    for j in range(G):
                        m = pe.matmul(bank(0, 128, rows=HR, first=j * 128), hot[:, (k + 1) % TURN, j, 0:HR], ident_r[:],
                                      start=True, stop=True)
                    m.then_inc(hotT_ps, 1)
                if k in (1, 5):
                    load_blocks(mybir.EngineType.PE, blk, n + 2, k + 2, 4 if k == 1 else 3)
                m_ = n - 8
                if here(m_, UNITS):
                    pe.wait_ge(msg2_sb, m_ + 1)
                    after(pe, sum_sb, m_)
                    for j in range(G):
                        m = pe.matmul(bank(7, D, rows=NP), hot[:, (k - 8) % TURN, j, 0:NP].bitcast(F32), msg2[:, k % 2, j, :],
                                      start=(j == 0), stop=(j == G - 1))
                    m.then_inc(sum_ps, 1)

            steps(pe, edge_step, -1, LAST, 1, UNITS // TURN - 1, TURN)

            pe.wait_ge(upd_w_in, 48)
            pe.wait_ge(logit0_ok, 1)
            pe.wait_ge(sum_sb, UNITS)

            def turn_sums(c):
                if c >= 1:
                    pe.wait_ge(aggT_sb, c)
                for k in range(KD):
                    for i, t in enumerate(CH[c]):
                        m = turn(bank(k, NP, first=i * NP), agg[0:NP, t, k * 128:k * 128 + 128], NP)
                m.then_inc(aggT_ps, 1)

            def hidden(c):
                pe.wait_ge(aggT_sb, c + 1)
                if c >= 1:
                    pe.wait_ge(hid_pre, c)
                for f in range(KD):
                    for k in range(KD):
                        m = pe.matmul(bank(2 + f, len(CH[c]) * NP), uw1_sb[:, KD + k, f * 128:f * 128 + 128],
                                      aggT[c % 2][:, k, 0:len(CH[c]), :], start=(k == 0), stop=(k == KD - 1))
                m.then_inc(hid_ps, 1)

            def turn_x2(t):
                pe.wait_ge(x2_ok, t + 1)
                if t >= 1:
                    pe.wait_ge(x2T_sb, t)
                for k in range(KD):
                    m = turn(bank(6, NP, first=k * NP), res[0:NP, t, k * 128:k * 128 + 128], NP)
                m.then_inc(x2T_ps, 1)

            def route(t):
                pe.wait_ge(x2T_sb, t + 1)
                for k in range(KD):
                    m = pe.matmul(bank(7, NE, rows=NP, first=t * NE), x2T[t % 2][:, k, :], wrc[:, k, :],
                                  start=(k == 0), stop=(k == KD - 1))
                m.then_inc(logit_ps, 1)

            turn_sums(0)
            hidden(0)
            for c, blocks in enumerate(CH):
                if c + 1 < len(CH):
                    turn_sums(c + 1)
                    hidden(c + 1)
                pe.wait_ge(hid_sb, c + 1)
                for i, t in enumerate(blocks):
                    if t >= 2:
                        pe.wait_ge(x2_ok, t - 1)
                    for f in range(KD):
                        m = pe.matmul(bank(4 + t % 2, D, rows=NP), hidT[c % 2][:, f, i, :], uw2_sb[:, f, :],
                                      start=(f == 0), stop=(f == KD - 1))
                    m.then_inc(upd_ps, 1)
                    if t >= 1:
                        turn_x2(t - 1)
                    if t >= 2:
                        route(t - 2)
            turn_x2(NB - 1)
            route(NB - 2)
            route(NB - 1)
            pe.wait_ge(hotk_ok, 1)
            flat = hot_k[0:NP].rearrange("p e m -> p (e m)")
            pe.matmul(bank(3, NE * KT, rows=NP), earlier[0:NP, 0:NP], flat, start=True, stop=True)
            pe.matmul(bank(4, NE * KT, rows=NP), ones[0:NP, 0:NP], flat, start=True, stop=True).then_inc(route_ps, 1)

            pe.wait_ge(w1_in, 16 * (NE + 1))
            pe.wait_ge(w2_rest_ok, NE)
            pe.wait_ge(slots_ok, 1)
            pe.wait_ge(tile_ok, 1)

            ex = {}

            def slots_step(n, k):
                load_experts(mybir.EngineType.PE, ex, n, k)
                m_ = n
                if here(m_, SLOT_TILES):
                    pe.wait_ge(sxT_sb, m_ + 1)
                    after(pe, sh_pre, m_ - 1)
                    for c in range(KD):
                        m = pe.matmul(bank(1 + k % 2, HID), slot_xT[k % 2][:, c, :],
                                      w1_sb[:, bass.ts(ex["wide", k], 1), c, :].rearrange("p a n -> p (a n)"),
                                      start=(c == 0), stop=(c == KD - 1))
                    m.then_inc(sh_ps, 1)
                m_ = n + 1
                if here(m_, SLOT_TILES):
                    pe.wait_ge(slot_in[(k + 1) % 4], 16 * ((m_ - (k + 1) % 4) // 4) + 16 if isinstance(m_, int)
                               else (m_ - (k + 1) % 4) * 4 + 16)
                    after(pe, sxT_sb, m_)
                    for c in range(KD):
                        m = turn(bank(0, 128, first=c * 128), slot_x[(k + 1) % 4][:, c * 128:c * 128 + 128], 128)
                    m.then_inc(sxT_ps, 1)
                m_ = n - 1
                if here(m_, SLOT_TILES):
                    pe.wait_ge(sh_sb, m_ + 1)
                    after(pe, shT_sb, m_ - 1)
                    for c in range(HC):
                        m = turn(bank(3 + (k + 1) % 2, 128, first=c * 128),
                                 slot_h[(k + 1) % 2][:, c * 128:c * 128 + 128], 128)
                    m.then_inc(shT_ps, 1)
                m_ = n - 2
                if here(m_, SLOT_TILES):
                    pe.wait_ge(shT_sb, m_ + 1)
                    after(pe, sy_sb, m_ - 1)
                    w = lambda t, c: t[:, bass.ts(ex["late", k], 1), c, :].rearrange("p a n -> p (a n)")
                    for c in range(HC):
                        pe.matmul(bank(5 + k % 2, D), slot_hT[k % 2][:, c, :], w(w2_lead, c), start=(c == 0), stop=False)
                        pe.matmul(bank(5 + k % 2, D), slot_hT[k % 2][:, c, :], w(w2_rest, c), start=False, stop=False)
                        m = pe.matmul(bank(5 + k % 2, D), slot_hR[k % 2][:, c, :], w(w2_lead, c), start=False,
                                      stop=(c == HC - 1))
                    m.then_inc(sy_ps, 1)

            steps(pe, slots_step, -1, SLOT_TILES + 2, 1, SLOT_TILES // 4 - 1, 4)

        def stage_dst(act, t):
            act.wait_ge(tab_ps, t + 1)
            if t >= 2:
                act.wait_ge(dst_out[t % 2], 16 * (t // 2))
            act.activation(dst_stage[t % 2][0:NP, :], bank(4 + t % 2, D, rows=NP), ACT.Copy).then_inc(dst_sb, 1)

        @block.scalar
        def _(act):
            A = act.activation
            act.wait_ge(wT_ps, 1)
            A(wkvT[:, 0, :], ps[:, 4:6, :].rearrange("p a n -> p (a n)"), ACT.Copy).then_inc(wT_sb, 1)
            act.wait_ge(wT_ps, 2)
            A(wkvT[:, 1, :], ps[:, 2:4, :].rearrange("p a n -> p (a n)"), ACT.Copy).then_inc(wT_sb, 1)
            act.wait_ge(wT_ps, 3)
            A(woutT[:].rearrange("p j n -> p (j n)"), ps[:, 0:2, :].rearrange("p a n -> p (a n)"), ACT.Copy)\
                .then_inc(wT_sb, 1)
            act.wait_ge(consts, N_CONST)
            act.wait_ge(var_ok, 1)
            A(rstd[0:NP], meanvar[0:NP, :, 1], ACT.Sqrt, bias=eps_col[0:NP, :]).then_inc(sd_ok, 1)
            for t in range(NB):
                act.wait_ge(xnT_ps, t + 1)
                A(xnT[:, t, :, 0:NP], bank(t % 2, KD * NP).rearrange("p (k n) -> p k n", k=KD), ACT.Copy)\
                    .then_inc(xnT_sb, 1)
                if t >= 1:
                    stage_dst(act, t - 1)
            stage_dst(act, NB - 1)
            for t in range(NB):
                b = 2 + 2 * (t % 2)
                act.wait_ge(kv_ps, t + 1)
                if t >= 1:
                    act.wait_ge(ss_ok, t)
                A(kv_sq[0:NP, :], ps[0:NP, b:b + 2, :].rearrange("p a n -> p (a n)"), ACT.Square).then_inc(sq_sb, 1)
                if t >= 2:
                    act.wait_ge(dots_ps, t - 1)
                A(v_n[t % 2][0:NP, :], ps[0:NP, b + 1, :], ACT.Copy).then_inc(v_sb, 1)
                act.wait_ge(ss_ok, t + 1)
                A(kv_ss[0:NP, :], kv_ss[0:NP, :], ACT.Sqrt, bias=eps_col[0:NP, :], scale=1.0 / HD).then_inc(kvsd_ok, 1)
            act.wait_ge(mixP_ps, 1)
            A(mixP[:].rearrange("p j n -> p (j n)"), ps[:, 0:2, :].rearrange("p a n -> p (a n)"), ACT.Copy)\
                .then_inc(mixP_sb, 1)
            for c in range(KD):
                act.wait_ge(mixG_ps, c + 1)
                A(mixG[:, c, :], bank(2 + c, D), ACT.Copy, scale=1.0 / N).then_inc(mixG_sb, 1)
            act.wait_ge(small_in, 16 * SMALL)
            for c, blocks in enumerate(CH):
                act.wait_ge(hpre_ps, c + 1)
                for f in range(KD):
                    m = A(xnT[:, blocks[0]:blocks[0] + len(blocks), f, 0:NP],
                          bank(2 + 2 * (c % 2) + f, len(blocks) * NP).rearrange("p (i n) -> p i n", n=NP),
                          ACT.Identity, bias=ub1_col[:, f:f + 1])
                m.then_inc(hpre_sb, 1)

            def edge_step(n, k):
                m_ = n - 6
                if here(m_, UNITS):
                    act.wait_ge(msg1T_ps, m_ + 1)
                    after(act, msg2_ps, m_ - 1)
                    A(msg1T_hi[:, k % 2], bank(3 + k % 2, SPLIT), ACT.Copy)
                    A(msg1T_f[:, k % 2], bank(3 + k % 2, 128, first=SPLIT), ACT.Copy).then_inc(msg1T_sb, 1)
                m_ = n - 5
                kk = (k - 5) % TURN
                if here(m_, UNITS):
                    act.wait_ge(rstd_ok, m_ // 2 + 1 if isinstance(m_, int) else pairs + (k - 5) // 2 + 1)
                    after(act, msg1T_ps, m_ - 1)
                    for j in range(G):
                        m = A(msg1n[:, (k + 1) % 2, j, :], msg1[:, kk, j, :], ACT.Identity,
                              bias=nw_b[:, kk, j:j + 1], scale=nw_y[:, kk, j:j + 1])
                    m.then_inc(msg1n_sb, 1)
                m_ = n - 7
                if here(m_, UNITS):
                    act.wait_ge(msg2_ps, m_ + 1)
                    after(act, sum_ps, m_ - 1)
                    A(msg2[:, (k + 1) % 2].rearrange("p j n -> p (j n)"), bank(5 + (k + 1) % 2), ACT.Silu)\
                        .then_inc(msg2_sb, 1)
                m_ = n + 1
                if here(m_, UNITS):
                    act.wait_ge(hotT_ps, m_ + 1)
                    after(act, pre_ps, m_ - 1)
                    A(hotT[0:HR, (k + 1) % 2, :], bank(0, UE, rows=HR), ACT.Copy).then_inc(hotT_sb, 1)
                if here(n, UNITS):
                    act.wait_ge(pre_sb, n + 1)
                    v = msg1[:, k].rearrange("p j n -> p (j n)")
                    A(v, v, ACT.Silu).then_inc(msg1_sb, 1)

            pairs = 0
            for n in range(-1, TURN):
                edge_step(n, n % TURN)
            with act.Fori(1, UNITS // TURN - 1) as i:
                pairs = TURN // 2 * i
                for k in range(TURN):
                    edge_step(TURN * i + k, k)
            for n in range(UNITS - TURN, LAST):
                edge_step(n, n % TURN)


            def copy_sums(c):
                act.wait_ge(aggT_ps, c + 1)
                if c >= 2:
                    act.wait_ge(hid_ps, c - 1)
                A(aggT[c % 2][:, :, 0:len(CH[c]), :].rearrange("p k i n -> p k (i n)"), ps[:, 0:2, 0:len(CH[c]) * NP],
                  ACT.Copy).then_inc(aggT_sb, 1)

            def copy_x2(t):
                act.wait_ge(x2T_ps, t + 1)
                if t >= 2:
                    act.wait_ge(logit_ps, t - 1)
                A(x2T[t % 2][:].rearrange("p k n -> p (k n)"), bank(6, KD * NP), ACT.Copy).then_inc(x2T_sb, 1)

            copy_sums(0)
            for c, blocks in enumerate(CH):
                if c + 1 < len(CH):
                    copy_sums(c + 1)
                act.wait_ge(hid_pre, c + 1)
                v = hidT[c % 2][:, :, 0:len(blocks), :]
                A(v, v, ACT.Silu).then_inc(hid_sb, 1)
                for t in blocks:
                    if t >= 1:
                        copy_x2(t - 1)
            copy_x2(NB - 1)
            act.wait_ge(var2_ok, 1)
            A(rstd[0:NP], meanvar[0:NP, :, 1], ACT.Sqrt, bias=eps2_col[0:NP, :], scale=1.0 + EPS).then_inc(sd2_ok, 1)
            act.wait_ge(rstd2_ok, 1)
            for t in range(NB):
                A(xm[0:NP, t, :], res[0:NP, t, :], ACT.Identity, bias=nbias[0:NP, t:t + 1], scale=rstd[0:NP, t:t + 1])\
                    .then_inc(xm_ok, 1)
            act.wait_ge(gap_ok, 1)
            A(wtmp[0:NP], wtmp[0:NP], ACT.Exp).then_inc(exp_ok, 1)
            act.wait_ge(w2_in, 16 * (NE + 1))
            for e in range(NE):
                A(w2_lead[:, e], w2_sb[:, e], ACT.Copy).then_inc(w2_lead_ok, 1)

            def slots_step(n, k):
                m_ = n + 1
                if here(m_, SLOT_TILES):
                    act.wait_ge(sxT_ps, m_ + 1)
                    after(act, sh_ps, m_ - 1)
                    for c in range(KD):
                        m = A(slot_xT[(k + 1) % 2][:, c, :], bank(0, 128, first=c * 128), ACT.Identity,
                              bias=beta_col[:, c:c + 1], scale=gamma_col[:, c:c + 1])
                    m.then_inc(sxT_sb, 1)
                m_ = n - 1
                if here(m_, SLOT_TILES):
                    act.wait_ge(shT_ps, m_ + 1)
                    after(act, sy_ps, m_ - 1)
                    A(slot_hT[(k + 1) % 2][:].rearrange("p c n -> p (c n)"), bank(3 + (k + 1) % 2), ACT.Copy)\
                        .then_inc(shT_lead, 1)
                if here(n, SLOT_TILES):
                    act.wait_ge(sh_pre, n + 1)
                    A(slot_h[k % 2][:], slot_h[k % 2][:], ACT.Gelu).then_inc(sh_sb, 1)

            steps(act, slots_step, -1, SLOT_TILES + 1, 1, SLOT_TILES // 4 - 1, 4)

        @block.vector
        def _(dve):
            st = Steps(dve, dve_step)

            def step(ins):
                st.did(ins)
                st.join()

            R = slice(0, NP)
            dve.wait_ge(edges_in, 48)
            dve.wait_ge(consts, N_CONST)
            step(dve.tensor_copy(rank_f[R], src_i[R]))
            step(dve.tensor_scalar(row_f[R], rank_f[R], 1.0 / NB, 0.5 / NB - 0.5, ALU.mult, ALU.add))
            step(dve.tensor_scalar(row_f[R], row_f[R], ROUND, None, ALU.add))
            step(dve.tensor_scalar(row_f[R], row_f[R], -ROUND, None, ALU.add))
            step(dve.scalar_tensor_tensor(blk_f[R], row_f[R], -float(NB), rank_f[R], ALU.mult, ALU.add))
            step(dve.tensor_copy(blk_h[R], blk_f[R]))
            for b in range(NB):
                st.did(dve.tensor_scalar(onehot[R, b, :], blk_h[R], float(b), None, ALU.is_equal))
            st.join()
            flat = onehot[R].rearrange("p b c -> p (b c)")
            step(dve.tensor_tensor_scan(scanned[R], flat, flat, 0.0, ALU.add, ALU.bypass))
            last = scanned[R].rearrange("p (b c) -> p b c", b=NB)[:, :, EC - 1]
            step(dve.tensor_copy(cum[R], last))
            step(dve.tensor_copy(rowcnt[R, 0:1], cum[R, 0:1]))
            st.did(dve.tensor_tensor(rowcnt[R, 1:NB], cum[R, 1:NB], cum[R, 0:NB - 1], ALU.subtract))
            st.join()
            step(dve.tensor_tensor(cum[R], cum[R], rowcnt[R], ALU.subtract))
            dve.tensor_copy(stats[R, 0, 0:1], cum[R, 0:1]).then_inc(rowcnt_ok, 1)
            step(dve.tensor_copy(rec_sb[R, :, 0], dst_i[R]))
            step(dve.tensor_copy(rec_sb[R, :, 1], row_f[R]))
            step(dve.tensor_copy(d2_r[R], d2_f[R]))
            step(dve.tensor_copy(rec_sb[R, :, 2], d2_r[R].bitcast(F32)))
            step(dve.tensor_tensor(rec_sb[R, :, 3], d2_f[R], d2_r[R].bitcast(F32), ALU.subtract))
            dve.wait_ge(counts_ps, 1)
            step(dve.tensor_copy(prefix[:], bank(6, NB)))
            step(dve.tensor_scalar(ends[:], bank(6, NB, first=32), float(UE - 1), None, ALU.add))
            step(dve.tensor_copy(ints[:], ends[:]))
            step(dve.tensor_scalar(ints[:], ints[:], 8, None, ALU.logical_shift_right))
            step(dve.tensor_copy(nunits[:], ints[:]))
            step(dve.tensor_tensor_scan(ends[:], nunits[:], nunits[:], 0.0, ALU.add, ALU.bypass))
            step(dve.tensor_tensor(nunits[:], ends[:], nunits[:], ALU.subtract))
            step(dve.scalar_tensor_tensor(prefix[:], nunits[:], float(UE), prefix[:], ALU.mult, ALU.add))
            step(dve.scalar_tensor_tensor(prefix[R], prefix[R], -1.0, cum[R], ALU.add, ALU.subtract))
            for first, end in ((0, 2 * SC), (2 * SC, EC)):
                C = slice(first, end)
                for b in range(NB):
                    st.did(dve.scalar_tensor_tensor(masked[R, b, C], scanned[R, b * EC + first:b * EC + end],
                                                    prefix[R, b:b + 1], onehot[R, b, C], ALU.add, ALU.mult))
                st.join()
                step(dve.tensor_reduce(rank_f[R, C], masked[R, :, C].rearrange("p b c -> p c b"), AX.X, ALU.add))
                step(dve.tensor_copy(pos_i[R, C], rank_f[R, C]))
                step(dve.tensor_scalar(low_i[R, C], pos_i[R, C], 127, None, ALU.bitwise_and))
                step(dve.tensor_scalar(top_i[R, C], pos_i[R, C], 7, None, ALU.logical_shift_right))
                step(dve.tensor_copy(rank_f[R, C], low_i[R, C]))
                step(dve.tensor_copy(blk_f[R, C], top_i[R, C]))
                step(dve.scalar_tensor_tensor(rank_f[R, C], rank_f[R, C], float(TILES), blk_f[R, C],
                                              ALU.mult, ALU.add))
                dve.tensor_copy(place_u[R, C], rank_f[R, C]).then_inc(pos_ok, 1)
            step(dve.tensor_tensor(unit_le[:], ends[0:1].unsqueeze(1).broadcast_to([1, UNITS, NB]),
                                   iota[0:1, 0:UNITS].unsqueeze(2).broadcast_to([1, UNITS, NB]), ALU.is_le))
            step(dve.tensor_reduce(unit_f[:], unit_le[:], AX.X, ALU.add))
            step(dve.tensor_scalar(unit_f[:], unit_f[:], float(NB - 1), None, ALU.min))
            step(dve.tensor_copy(unit_blk[:], unit_f[:]))
            step(dve.tensor_copy(unit_f[:], unit_blk[:]))
            dve.memset(nw_t[:], 1.0).then_inc(units_ok, 1)

            dve.wait_ge(small_in, 16 * SMALL)
            for k in range(KD):
                st.did(dve.tensor_scalar(w2c[:, k, :], w2c_raw[:, k, :], g_col[:, k:k + 1], None, ALU.mult))
            step(dve.tensor_tensor(b_col[:], b_col[:], g_col[:], ALU.subtract))
            for k in range(KD):
                st.did(dve.tensor_scalar(lb_bc[:, k, :], ones[:], b_col[:, k:k + 1], None, ALU.mult))
            for k in range(KD):
                st.did(dve.tensor_scalar(wrc[:, k, :], wr_sb[:, k, :], gamma_col[:, k:k + 1], None, ALU.mult))
                st.did(dve.tensor_scalar(beta_bc[:, k, :], ones[:], beta_col[:, k:k + 1], None, ALU.mult))
            st.join()
            dve.memset(nw_t[:], 0.0).then_inc(wrg_ok, 1)
            dve.wait_ge(router_ps, 1)
            step(dve.tensor_tensor(shift[:], bank(7, D), mb2_bc[:], ALU.add))
            for k in range(KD):
                st.did(dve.scalar_tensor_tensor(w2c[:, k, :], shift[:], 1.0 / D, w2c[:, k, :], ALU.mult, ALU.add))
            step(dve.tensor_scalar(cum[:, 0:NE], bank(7, NE, first=256), -1.0 / D, None, ALU.mult))
            for k in range(KD):
                st.did(dve.tensor_tensor(wrc[:, k, :], wrc[:, k, :], cum[:, 0:NE], ALU.add))
            st.did(dve.tensor_tensor(logit0[:], bank(7, NE, first=288), br_bc[:], ALU.add))
            st.join()
            dve.memset(nw_t[:], 0.0).then_inc(logit0_ok, 1)
            step(dve.memset(xnT[:, :, :, NP:128], 0.0))
            dve.memset(nw_t[:], 0.0).then_inc(pads_ok, 1)

            dve.wait_ge(x_in, 16)

            for t in range(NB):
                st.did(dve.bn_stats(stats[R, t, :], res[R, t, :]))
            st.join()
            for t in range(NB):
                st.did(dve.bn_aggr(meanvar[R, t, :], stats[R, t, :]))
            st.join()
            dve.tensor_copy(nw_t[R, 0, 0:1], meanvar[R, 0, 0:1]).then_inc(var_ok, 1)
            dve.wait_ge(sd_ok, 1)
            step(dve.reciprocal(rstd[R], rstd[R]))
            dve.wait_ge(defaults_out, 16)
            for t in range(NB):
                dve.tensor_scalar(xn[R, t, :], res[R, t, :], meanvar[R, t, 0:1], rstd[R, t:t + 1],
                                  ALU.subtract, ALU.mult).then_inc(xn_ok, 1)
            dve.wait_ge(zeros_out, 16)
            for t in range(NB):
                dve.wait_ge(tab_ps, t + 1)
                step(dve.tensor_copy(src_hi[:, t, :], bank(2 + t % 2, D)))
                dve.tensor_tensor(src_lo[:, t, :], bank(2 + t % 2, D), src_hi[:, t, :].bitcast(F32), ALU.subtract)\
                   .then_inc(tab_sb, 1)
            dve.wait_ge(wT_sb, KD + 1)
            heads = wkvT[:].rearrange("p k (h d) -> p (k h) d", d=HD)
            step(dve.tensor_reduce(wmean[:], heads, AX.X, ALU.add))
            step(dve.tensor_scalar(wmean[:], wmean[:], 1.0 / HD, None, ALU.mult))
            dve.tensor_tensor(heads, heads, wmean[:].unsqueeze(2).broadcast_to([128, KD * 2 * HEADS, HD]),
                              ALU.subtract).then_inc(wkv_centered, 1)
            dve.wait_ge(upd_w_in, 48)
            step(dve.tensor_tensor(bias_bc[:], bias_bc[:], bout_bc[:], ALU.add))
            for t in range(NB):
                b = 2 + 2 * (t % 2)
                dve.wait_ge(sq_sb, t + 1)
                if t >= 1:
                    dve.wait_ge(kn_ok, t)
                dve.tensor_reduce(kv_ss[R], kv_sq[R].rearrange("p (h d) -> p h d", d=HD), AX.X, ALU.add)\
                   .then_inc(ss_ok, 1)
                st.did(dve.tensor_tensor(res[R, t, :], res[R, t, :], bias_bc[R, :], ALU.add))
                dve.wait_ge(kvsd_ok, t + 1)
                step(dve.tensor_tensor(kv_rs[R], kv_ss[R, 0:HEADS], kv_ss[R, HEADS:2 * HEADS], ALU.mult))
                step(dve.reciprocal(kv_rs[R], kv_rs[R]))
                if t >= 2:
                    dve.wait_ge(dots_ps, t - 1)
                dve.tensor_tensor(k_n[t % 2][R].rearrange("p (h d) -> p h d", d=HD),
                                  ps[R, b, :].rearrange("p (h d) -> p h d", d=HD),
                                  kv_rs[R].unsqueeze(2).broadcast_to([NP, HEADS, HD]), ALU.mult).then_inc(kn_ok, 1)
                st.did(dve.tensor_tensor(res[R, t, :], res[R, t, :], xn[R, t, :], ALU.add))
            dve.wait_ge(dots_ps, NB)
            step(dve.memset(k_n[0][:], 0.0))
            pair = lambda ap: ap.rearrange("p (j d) -> p j d", d=128)
            st.did(dve.tensor_copy(pair(k_n[0][0:HD, :])[:, :, 0:HD], pair(bank(6, rows=HD))[:, :, 0:HD]))
            st.did(dve.tensor_copy(pair(k_n[0][HD:128, :])[:, :, HD:128], pair(ps[HD:128, 6, :])[:, :, HD:128]))
            st.join()
            dve.memset(agg[:], 0.0).then_inc(diag_ok, 1)
            dve.wait_ge(diag_ok, 1)
            for t in range(NB):
                dve.wait_ge(mixed_ps, t + 1)
                dve.tensor_tensor(res[R, t, :], res[R, t, :], bank(t % 2, D, rows=NP), ALU.add).then_inc(mixed_ok, 1)

            blk = {}
            nw = Steps(dve, newton_step)

            def rstd_step(q, s, pair_exists):
                if not pair_exists:
                    return
                if q == 0:
                    st.join()
                nw.join()
                y = (nw_i[:].bitcast(F32), nw_1[:], nw_2[:], nw_y[:, s:s + 2, :])
                r, part = divmod(q - 3, 3)
                if q == 0:
                    m = dve.tensor_scalar(nw_v[:], emv[:, s:s + 2, :, 1], EPS, None, ALU.add)
                elif q == 1:
                    m = dve.tensor_scalar(nw_i[:], nw_v[:].bitcast(I32), 1, None, ALU.logical_shift_right)
                elif q == 2:
                    m = dve.tensor_scalar(nw_i[:], nw_i[:], -1.0, float(RSQRT_MAGIC), ALU.mult, ALU.add)
                elif q == 12:
                    m = dve.scalar_tensor_tensor(nw_b[:, s:s + 2, :], emv[:, s:s + 2, :, 0], -1.0, y[3],
                                                 ALU.mult, ALU.mult)
                elif q == 13:
                    dve.tensor_scalar(nw_b[:, s:s + 2, :], nw_b[:, s:s + 2, :], 1.0, None, ALU.add).then_inc(rstd_ok, 1)
                    return
                elif part == 0:
                    m = dve.tensor_tensor(nw_s[:], y[r], y[r], ALU.mult)
                elif part == 1:
                    m = dve.scalar_tensor_tensor(nw_s[:], nw_s[:], -0.5, nw_v[:], ALU.mult, ALU.mult)
                else:
                    m = dve.scalar_tensor_tensor(y[r + 1], nw_s[:], 1.5, y[r], ALU.add, ALU.mult)
                nw.did(m)

            def edge_step(n, k, turn_rows):
                behind = 3 if k % 2 else 4
                first_q = 1 if k % 2 else 7
                pair_on = here(n - behind, UNITS)
                slot = (k - behind) % TURN
                m_ = n + 1
                kk = (k + 1) % TURN
                if here(m_, UNITS):
                    after(dve, sum_ps, m_ - TURN + 1)
                    rows = recs[:, bass.ds(G * m_, G), 1:2]
                    dve.tensor_tensor(hot[:, kk, :, 0:NP], iota[:, 0:NP].unsqueeze(1).broadcast_to([128, G, NP]),
                                      rows.broadcast_to([128, G, NP]), ALU.is_equal).then_inc(hot_ready, 1)
                if k % 2:
                    rstd_step(0, slot, pair_on)
                if k == 0:
                    load_blocks(mybir.EngineType.DVE, blk, n - 9, 0, 4)
                rstd_step(first_q, slot, pair_on)
                m_ = n - 9
                if here(m_, UNITS):
                    dve.wait_ge(sum_ps, m_ + 1)
                    after(dve, sum_sb, m_)
                    a = agg[0:NP, bass.ts(blk[k], 1), :].rearrange("p a n -> p (a n)")
                    dve.tensor_tensor(a, a, bank(7, D, rows=NP), ALU.add).then_inc(sum_sb, 1)
                rstd_step(first_q + 1, slot, pair_on)
                if here(n - 6, UNITS):
                    dve.wait_ge(msg1T_sb, n - 5)
                    after(dve, msg2_ps, n - 7)
                    dve.tensor_tensor(msg1T_lo[:, k % 2], bank(3 + k % 2, SPLIT),
                                      msg1T_hi[:, k % 2].bitcast(F32), ALU.subtract)\
                       .then_inc(msg1T_lo_sb, 1)
                rstd_step(first_q + 2, slot, pair_on)
                m_ = n - 1
                kk = (k - 1) % TURN
                if here(m_, UNITS):
                    dve.wait_ge(msg1_sb, m_ + 1)
                    st.did(dve.bn_stats(est[:, kk, 0, :], msg1[:, kk, 0, :]))
                rstd_step(first_q + 3, slot, pair_on)
                if here(m_, UNITS):
                    st.did(dve.bn_stats(est[:, kk, 1, :], msg1[:, kk, 1, :]))
                rstd_step(first_q + 4, slot, pair_on)
                if here(n, UNITS):
                    dve.wait_ge(pre_ps, n + 1)
                    dve.wait_ge(row_in[k], turn_rows)
                    v = msg1[:, k].rearrange("p j n -> p (j n)")
                    dve.tensor_tensor(v, bank(1 + k % 2), v, ALU.add).then_inc(pre_sb, 1)
                if here(m_, UNITS):
                    st.join()
                rstd_step(first_q + 5, slot, pair_on)
                if here(m_, UNITS):
                    for j in range(G):
                        st.did(dve.bn_aggr(emv[:, kk, j, :], est[:, kk, j, :]))
                if k % 2 == 0:
                    rstd_step(13, slot, pair_on)
                if k in (1, 5):
                    load_blocks(mybir.EngineType.DVE, blk, n - 6, k + 3, 4 if k == 1 else 2)

            dve.wait_ge(mixG_sb, KD)
            step(dve.tensor_copy(w2_hi[:], w2c[:]))
            step(dve.tensor_tensor(w2_lo[:], w2c[:], w2_hi[:].bitcast(F32), ALU.subtract))
            dve.tensor_copy(ident_r[:], ident[:]).then_inc(w2_split, 1)
            dve.wait_ge(recs_in, 16)
            for n in range(-1, TURN):
                edge_step(n, n % TURN, 32)
            with dve.Fori(1, UNITS // TURN - 1) as i:
                st.enter(i, 1, TURN * 2 * G)
                nw.enter(i, 1, TURN // 2 * 13)
                for k in range(TURN):
                    edge_step(TURN * i + k, k, 32 * i + 32)
            st.leave(UNITS // TURN - 2)
            nw.leave(UNITS // TURN - 2)
            for n in range(UNITS - TURN, LAST):
                edge_step(n, n % TURN, 32 * (n // TURN) + 32)

            def add_hidden(c):
                blocks = CH[c]
                dve.wait_ge(hid_ps, c + 1)
                if c >= 2:
                    dve.wait_ge(upd_ps, 4 * (c - 1))
                for f in range(KD):
                    m = dve.tensor_tensor(hidT[c % 2][:, f, 0:len(blocks), :],
                                          bank(2 + f, len(blocks) * NP).rearrange("p (i n) -> p i n", n=NP),
                                          xnT[:, blocks[0]:blocks[0] + len(blocks), f, 0:NP], ALU.add)
                    if f == 0:
                        st.did(m)
                m.then_inc(hid_pre, 1)

            dve.wait_ge(mixed_ok, NB)
            dve.wait_ge(hpre_sb, len(CH))
            add_hidden(0)
            for c, blocks in enumerate(CH):
                if c + 1 < len(CH):
                    add_hidden(c + 1)
                for t in blocks:
                    dve.wait_ge(upd_ps, t + 1)
                    dve.tensor_tensor(res[R, t, :], res[R, t, :], bank(4 + t % 2, D, rows=NP), ALU.add).then_inc(x2_ok, 1)
                    if t >= 1:
                        dve.wait_ge(x2_ok, t)
                        if t >= 2:
                            st.join()
                        st.did(dve.bn_stats(stats[R, t - 1, :], res[R, t - 1, :]))
                        if t >= 2:
                            st.did(dve.bn_aggr(meanvar[R, t - 2, :], stats[R, t - 2, :]))
            dve.wait_ge(x2_ok, NB)
            step(dve.bn_stats(stats[R, NB - 1, :], res[R, NB - 1, :]))
            for t in (NB - 2, NB - 1):
                st.did(dve.bn_aggr(meanvar[R, t, :], stats[R, t, :]))
            st.join()
            dve.tensor_copy(nw_t[R, 0, 0:1], meanvar[R, 0, 0:1]).then_inc(var2_ok, 1)
            dve.wait_ge(sd2_ok, 1)
            step(dve.reciprocal(rstd[R], rstd[R]))
            dve.scalar_tensor_tensor(nbias[R], meanvar[R, :, 0], -1.0, rstd[R], ALU.mult, ALU.mult).then_inc(rstd2_ok, 1)
            dve.wait_ge(logit_ps, NB)
            step(dve.tensor_tensor(logits[R], bank(7, NB * NE, rows=NP).rearrange("p (t e) -> p t e", e=NE),
                                   rstd[R].unsqueeze(2).broadcast_to([NP, NB, NE]), ALU.mult))
            step(dve.tensor_tensor(logits[R], logits[R], logit0[R].unsqueeze(1).broadcast_to([NP, NB, NE]), ALU.add))
            for t in range(NB):
                st.did(dve.max(top_v[R, t, :], logits[R, t, :]))
            st.join()
            for t in range(NB):
                st.did(dve.max_index(top_e[R, t, :], top_v[R, t, :], logits[R, t, :]))
            st.join()
            dve.tensor_tensor(wtmp[R], top_v[R, :, 1], top_v[R, :, 0], ALU.subtract).then_inc(gap_ok, 1)
            for k in range(TOPK):
                st.did(dve.tensor_copy(top_f[R, k, :], top_e[R, :, k]))
            st.join()
            step(dve.tensor_tensor(hot_k[R], top_f[R].rearrange("p k t -> p (k t)").unsqueeze(1).broadcast_to([NP, NE, KT]),
                                   iota[R, 0:NE].unsqueeze(2).broadcast_to([NP, NE, KT]), ALU.is_equal))
            dve.tensor_copy(nw_t[R, 0, 0:1], hot_k[R, 0, 0:1]).then_inc(hotk_ok, 1)
            dve.wait_ge(route_ps, 1)
            hc = hot_c[R].rearrange("p e m -> p (e m)")
            step(dve.tensor_copy(hc, bank(4, NE * KT, rows=NP)))
            hp = hot_p[R].rearrange("p e m -> p (e m)")
            step(dve.tensor_tensor_scan(hp, hc, hc, 0.0, ALU.add, ALU.bypass))
            step(dve.tensor_copy(e_cum[R], hot_p[R, :, KT - 1]))
            step(dve.tensor_copy(e_cnt[R, 0:1], e_cum[R, 0:1]))
            step(dve.tensor_tensor(e_cnt[R, 1:NE], e_cum[R, 1:NE], e_cum[R, 0:NE - 1], ALU.subtract))
            step(dve.tensor_tensor(e_cum[R], e_cum[R], e_cnt[R], ALU.subtract))
            step(dve.tensor_scalar(e_cnt[R], e_cnt[R], 127.0, None, ALU.add))
            step(dve.tensor_copy(e_int[R], e_cnt[R]))
            step(dve.tensor_scalar(e_int[R], e_int[R], 7, None, ALU.logical_shift_right))
            step(dve.tensor_copy(e_til[R], e_int[R]))
            step(dve.tensor_tensor_scan(e_end[R], e_til[R], e_til[R], 0.0, ALU.add, ALU.bypass))
            step(dve.tensor_tensor(e_til[R], e_end[R], e_til[R], ALU.subtract))
            step(dve.scalar_tensor_tensor(e_cum[R], e_til[R], 128.0, e_cum[R], ALU.mult, ALU.subtract))
            step(dve.tensor_tensor(hp, hp, hc, ALU.subtract))
            step(dve.tensor_tensor(hp, hp, bank(3, NE * KT, rows=NP), ALU.add))
            step(dve.tensor_tensor(hot_p[R], hot_p[R], e_cum[R].unsqueeze(2).broadcast_to([NP, NE, KT]), ALU.add))
            step(dve.tensor_tensor(hot_p[R], hot_p[R], hot_k[R], ALU.mult))
            step(dve.tensor_reduce(slot_f[R].rearrange("p k t -> p (k t)"), hot_p[R].rearrange("p e m -> p m e"),
                                   AX.X, ALU.add))
            dve.tensor_copy(slot_i[R], slot_f[R]).then_inc(slots_ok, 1)
            step(dve.tensor_tensor(e_le[:], e_end[0:1].unsqueeze(1).broadcast_to([1, SLOT_TILES, NE]),
                                   iota[0:1, 0:SLOT_TILES].unsqueeze(2).broadcast_to([1, SLOT_TILES, NE]), ALU.is_le))
            step(dve.tensor_reduce(tile_f[:], e_le[:], AX.X, ALU.add))
            step(dve.tensor_scalar(tile_f[:], tile_f[:], float(NE - 1), None, ALU.min))
            dve.tensor_copy(tile_e[:], tile_f[:]).then_inc(tile_ok, 1)
            dve.wait_ge(tile_ok, 1)

            dve.wait_ge(exp_ok, 1)
            step(dve.tensor_scalar(wgt[R, 0, :], wtmp[R], 1.0, None, ALU.add))
            step(dve.reciprocal(wgt[R, 0, :], wgt[R, 0, :]))
            step(dve.tensor_tensor(wgt[R, 1, :], wgt[R, 0, :], wtmp[R], ALU.mult))
            for e in range(NE):
                dve.wait_ge(w2_lead_ok, e + 1)
                dve.tensor_tensor(w2_rest[:, e], w2_sb[:, e], w2_lead[:, e].bitcast(F32), ALU.subtract).then_inc(w2_rest_ok, 1)
            dve.wait_ge(w1_in, 16 * (NE + 1))
            dve.wait_ge(w2_in, 16 * (NE + 1))
            dve.wait_ge(sent, 16 * KT)

            ex = {}

            def slots_step(n, k):
                load_experts(mybir.EngineType.DVE, ex, n, k)
                m_ = n
                if here(m_, SLOT_TILES):
                    dve.wait_ge(sh_ps, m_ + 1)
                    after(dve, shT_ps, m_ - 1)
                    dve.tensor_tensor(slot_h[k % 2][:], bank(1 + k % 2, HID),
                                      b1_bc[:, bass.ts(ex["wide", k], 1), :].rearrange("p a n -> p (a n)"), ALU.add)\
                       .then_inc(sh_pre, 1)
                m_ = n - 1
                if here(m_, SLOT_TILES):
                    dve.wait_ge(shT_lead, m_ + 1)
                    after(dve, sy_ps, m_ - 1)
                    flat = lambda t: t[(k + 1) % 2][:].rearrange("p c n -> p (c n)")
                    dve.tensor_tensor(flat(slot_hR), bank(3 + (k + 1) % 2), flat(slot_hT).bitcast(F32), ALU.subtract)\
                       .then_inc(shT_sb, 1)
                m_ = n - 2
                if here(m_, SLOT_TILES):
                    dve.wait_ge(sy_ps, m_ + 1)
                    if isinstance(m_, int):
                        after(dve, slot_out[k % 2], 8 * (m_ - k % 2))
                    else:
                        dve.wait_ge(slot_out[k % 2], 8 * (m_ - k % 2))
                    dve.tensor_tensor(slot_y[k % 2][:], bank(5 + k % 2, D),
                                      b2_bc[:, bass.ts(ex["late", k], 1), :].rearrange("p a n -> p (a n)"), ALU.add)\
                       .then_inc(sy_sb, 1)

            steps(dve, slots_step, 0, SLOT_TILES + 2, 1, SLOT_TILES // 4 - 1, 4)
            for t in range(NB):
                dve.wait_ge(pick_in[t % 4], 32 * (t // 4 + 1))
                step(dve.scalar_tensor_tensor(res[R, t, :], pick[t % 4][R, 0, :], wgt[R, 0, t:t + 1], res[R, t, :],
                                              ALU.mult, ALU.add))
                dve.scalar_tensor_tensor(res[R, t, :], pick[t % 4][R, 1, :], wgt[R, 1, t:t + 1], res[R, t, :],
                                         ALU.mult, ALU.add).then_inc(final_ok, 1)
                dve.wait_ge(final_ok, t + 1)
                dve.memset(nw_t[:], 0.0).then_inc(picked, 1)


_INS = ['x', 'src', 'dst', 'edge_weight1', 'L0_gnn_mW1', 'L0_gnn_mb1', 'L0_gnn_ln_g', 'L0_gnn_ln_b', 'L0_gnn_mW2',
        'L0_gnn_mb2', 'L0_gnn_uW1', 'L0_gnn_ub1', 'L0_gnn_uW2', 'L0_gnn_ub2', 'L0_mix_Wqkv', 'L0_mix_Wout',
        'L0_mix_bout', 'L0_ffn_gamma', 'L0_ffn_beta', 'L0_ffn_Wr', 'L0_ffn_br', 'L0_ffn_W1', 'L0_ffn_b1',
        'L0_ffn_W2', 'L0_ffn_b2']


def kernel(**inputs):
    import numpy as _np
    import concourse.bacc as _bacc
    from concourse import mybir as _mybir
    from concourse.bass_utils import run_bass_kernel_spmd as _run

    nc = _bacc.Bacc("TRN2", target_bir_lowering=False, num_devices=1)
    arrays, args = {}, []
    for name in _INS:
        a = _np.ascontiguousarray(inputs[name])
        arrays[f"in_{name}_dram"] = a
        args.append(nc.dram_tensor(f"in_{name}_dram", a.shape, _mybir.dt.from_np(a.dtype), kind="ExternalInput").ap())
    out = nc.dram_tensor("out_0_dram", inputs["x"].shape, _mybir.dt.float32, kind="ExternalOutput").ap()
    gps_layer(nc, *args, out)
    r = _run(nc, [arrays], core_ids=[0])
    return r.results[0]["out_0_dram"]
```
